# Optimizing a Trainium2 kernel written in Bass

```python
import numpy as np
import jax
import jax.numpy as jnp

def _softmax(x, axis=-1):
    return jax.nn.softmax(x, axis=axis)

def _gelu(x):
    return jax.nn.gelu(x, approximate=True)

def _silu(x):
    return jax.nn.silu(x)

def _sigmoid(x):
    return jax.nn.sigmoid(x)

def _layernorm(x, axis=-1, eps=1e-05):
    m = jnp.mean(x, axis=axis, keepdims=True)
    v = jnp.var(x, axis=axis, keepdims=True)
    return (x - m) / jnp.sqrt(v + eps)

def _scatter_add(tgt, idx, src, axis=0):
    return tgt.at[idx].add(src)

def _segment_sum(src, seg, n):
    return jax.ops.segment_sum(src, seg, n)
kernel_name = 'mk_adaln_d1_jaxref_r8_a712e2'

def setup_inputs(seed: int=0):
    np.random.seed(seed)
    _w = jnp.asarray

    def _L0_attn_setup():
        import jax, jax.numpy as jnp
        import numpy as np
        B, L = (2, 128)
        D_MODEL, D_CKV, D_CQ = (128, 32, 64)
        N_HEAD, D_HEAD, D_ROPE = (8, 64, 32)
        N_IDX_HEAD = 4
        K_TS, LW = (96, 64)
        ROPE_BASE = 10000.0

        def _pope(x, angles):
            cos, sin = (jnp.cos(angles), jnp.sin(angles))
            mu1, mu2 = jnp.split(jax.nn.softplus(x), 2, axis=-1)
            return jnp.concatenate([mu1 * cos - mu2 * sin, mu1 * sin + mu2 * cos], axis=-1)

        def _forward(x, W_dkv, W_uk, W_uv, W_dq, W_uq, W_qr, W_kr, W_out, idx_wq, idx_wk, idx_w, raw_delta):
            B_, L_, _ = x.shape
            c_kv = x @ W_dkv
            q_i = (x @ idx_wq).reshape(B_, L_, N_IDX_HEAD, D_HEAD)
            k_i = x @ idx_wk
            s_i = jax.nn.relu(jnp.einsum('bthd,bsd->bths', q_i, k_i))
            I = jnp.einsum('bths,h->bts', s_i, idx_w)
            qpos = jnp.arange(L_)[:, None]
            kpos = jnp.arange(L_)[None, :]
            local = (kpos >= qpos - LW + 1) & (kpos <= qpos)
            causal = kpos > qpos
            I = jnp.where(local[None], jnp.inf, I)
            I = jnp.where(causal[None], -jnp.inf, I)
            kk = min(K_TS, L_)
            _, idx = jax.lax.top_k(I, kk)
            bi = jnp.arange(B_)[:, None, None]
            key_c = (c_kv @ W_uk)[bi, idx].reshape(B_, L_, kk, N_HEAD, D_HEAD)
            value = (c_kv @ W_uv)[bi, idx].reshape(B_, L_, kk, N_HEAD, D_HEAD)
            c_q = x @ W_dq
            query_c = (c_q @ W_uq).reshape(B_, L_, N_HEAD, D_HEAD)
            half = D_ROPE // 2
            theta = 1.0 / ROPE_BASE ** (2.0 * jnp.arange(half, dtype=jnp.float32) / D_ROPE)
            delta = -2.0 * jnp.pi * jax.nn.sigmoid(raw_delta)
            angles_q = jnp.arange(L_, dtype=jnp.float32)[:, None] * theta[None, :] + delta
            query_r = _pope((c_q @ W_qr).reshape(B_, L_, N_HEAD, D_ROPE), angles_q[None, :, None, :])
            kr_sel = (x @ W_kr)[bi, idx]
            angles_k = jnp.arange(kk, dtype=jnp.float32)[:, None] * theta[None, :] + delta
            key_r = _pope(kr_sel, angles_k[None, None, :, :])
            scale = (D_HEAD + D_ROPE) ** (-0.5)
            q_c = query_c.transpose(0, 2, 1, 3)
            q_r = query_r.transpose(0, 2, 1, 3)
            k_c = key_c.transpose(0, 3, 1, 2, 4)
            v = value.transpose(0, 3, 1, 2, 4)
            scores = (jnp.einsum('bhld,bhlkd->bhlk', q_c, k_c) + jnp.einsum('bhld,blkd->bhlk', q_r, key_r)) * scale
            attn = jax.nn.softmax(scores.astype(jnp.float32), axis=-1).astype(v.dtype)
            out = jnp.einsum('bhlk,bhlkd->bhld', attn, v)
            out = out.transpose(0, 2, 1, 3).reshape(B_, L_, N_HEAD * D_HEAD)
            return out @ W_out
        key = jax.random.key(seed)
        ks = jax.random.split(key, 14)

        def w(k, shape, fan_in):
            return jax.random.normal(k, shape, dtype=jnp.float32) * fan_in ** (-0.5)
        return {'x': jax.random.normal(ks[0], (B, L, D_MODEL), dtype=jnp.float32), 'W_dkv': w(ks[1], (D_MODEL, D_CKV), D_MODEL), 'W_uk': w(ks[2], (D_CKV, N_HEAD * D_HEAD), D_CKV), 'W_uv': w(ks[3], (D_CKV, N_HEAD * D_HEAD), D_CKV), 'W_dq': w(ks[4], (D_MODEL, D_CQ), D_MODEL), 'W_uq': w(ks[5], (D_CQ, N_HEAD * D_HEAD), D_CQ), 'W_qr': w(ks[6], (D_CQ, N_HEAD * D_ROPE), D_CQ), 'W_kr': w(ks[7], (D_MODEL, D_ROPE), D_MODEL), 'W_out': w(ks[8], (N_HEAD * D_HEAD, D_MODEL), N_HEAD * D_HEAD), 'idx_wq': w(ks[9], (D_MODEL, N_IDX_HEAD * D_HEAD), D_MODEL), 'idx_wk': w(ks[10], (D_MODEL, D_HEAD), D_MODEL), 'idx_w': jnp.ones((N_IDX_HEAD,), dtype=jnp.float32), 'raw_delta': jax.random.normal(ks[11], (D_ROPE // 2,), dtype=jnp.float32) * 0.1}
    _L0_attn_in = _L0_attn_setup()

    def _L0_ffn_setup():
        import jax, jax.numpy as jnp
        import numpy as np
        DIM = 128
        DEPTH = 2
        HEADS = 8
        DIM_HEAD = 64
        WINDOW = 64
        INNER = HEADS * DIM_HEAD
        HID = int(DIM * 4 * 2 / 3)
        B, N = (2, 1024)
        QK_SCALE = 8.0

        def shift_token(t):
            t1, t2 = jnp.split(t, 2, axis=-1)
            t2 = jnp.pad(t2, ((0, 0), (1, 0), (0, 0)))[:, :-1]
            return jnp.concatenate([t1, t2], axis=-1)

        def l2norm(t):
            return t / jnp.clip(jnp.linalg.norm(t, axis=-1, keepdims=True), 1e-12)

        def rotate_half(x):
            x1, x2 = jnp.split(x, 2, axis=-1)
            return jnp.concatenate([-x2, x1], axis=-1)

        def rotary_xpos(q, k):
            n = q.shape[-2]
            half_idx = jnp.arange(0, DIM_HEAD, 2, dtype=jnp.float32)
            inv_freq = 1.0 / 10000.0 ** (half_idx / DIM_HEAD)
            t = jnp.arange(n, dtype=jnp.float32)
            freqs = t[:, None] * inv_freq[None, :]
            freqs = jnp.concatenate([freqs, freqs], axis=-1)
            base = (half_idx + 0.4 * DIM_HEAD) / (1.4 * DIM_HEAD)
            power = (t - n // 2) / float(WINDOW // 2)
            scale = base[None, :] ** power[:, None]
            scale = jnp.concatenate([scale, scale], axis=-1)
            cos, sin = (jnp.cos(freqs), jnp.sin(freqs))
            q = q * cos * scale + rotate_half(q) * sin * scale
            k = k * cos / scale + rotate_half(k) * sin / scale
            return (q, k)

        def local_attention(q, k, v):
            b, h, n, d = q.shape
            w = n // WINDOW
            bq = q.reshape(b, h, w, WINDOW, d) * QK_SCALE
            bk = k.reshape(b, h, w, WINDOW, d)
            bv = v.reshape(b, h, w, WINDOW, d)

            def look_around(t):
                p = jnp.pad(t, ((0, 0), (0, 0), (1, 0), (0, 0), (0, 0)))
                return jnp.concatenate([p[:, :, :w], p[:, :, 1:]], axis=3)
            bk, bv = (look_around(bk), look_around(bv))
            bt = jnp.arange(n).reshape(w, WINDOW)
            btp = jnp.pad(bt, ((1, 0), (0, 0)), constant_values=-1)
            btk = jnp.concatenate([btp[:w], btp[1:]], axis=1)
            sim = jnp.einsum('bhwid,bhwjd->bhwij', bq, bk)
            i = bt[:, :, None]
            j = btk[:, None, :]
            mask = (i < j) | (i > j + WINDOW) | (j == -1)
            sim = jnp.where(mask, -jnp.finfo(sim.dtype).max, sim)
            attn = jax.nn.softmax(sim, axis=-1)
            out = jnp.einsum('bhwij,bhwjd->bhwid', attn, bv)
            return out.reshape(b, h, n, d)

        def _layer(x, wqkv, qs, ksc, wo, lg, lb, w1, b1, w2, b2):
            b, n, _ = x.shape
            h = shift_token(x)
            qkv = h @ wqkv
            q, k, v = jnp.split(qkv, 3, axis=-1)
            to_heads = lambda t: t.reshape(b, n, HEADS, DIM_HEAD).transpose(0, 2, 1, 3)
            q, k, v = (to_heads(q), to_heads(k), to_heads(v))
            q = l2norm(q) * qs
            k = l2norm(k) * ksc
            q, k = rotary_xpos(q, k)
            o = local_attention(q, k, v)
            o = o.transpose(0, 2, 1, 3).reshape(b, n, INNER)
            x = x + o @ wo
            h = shift_token(x)
            mu = h.mean(-1, keepdims=True)
            var = h.var(-1, keepdims=True)
            h = (h - mu) / jnp.sqrt(var + 1e-05) * lg + lb
            h = h @ w1 + b1
            a, g = jnp.split(h, 2, axis=-1)
            h = a * jax.nn.gelu(g, approximate=False)
            x = x + h @ w2 + b2
            return x
        key = jax.random.key(seed)
        ks = jax.random.split(key, 6)
        return {'x': jax.random.normal(ks[0], (B, N, DIM), jnp.float32), 'wqkv': jax.random.normal(ks[1], (DEPTH, DIM, 3 * INNER), jnp.float32) * 0.02, 'q_scale': jnp.ones((DEPTH, DIM_HEAD), jnp.float32), 'k_scale': jnp.ones((DEPTH, DIM_HEAD), jnp.float32), 'wo': jax.random.normal(ks[2], (DEPTH, INNER, DIM), jnp.float32) * 0.02, 'ln_g': jnp.ones((DEPTH, DIM), jnp.float32), 'ln_b': jnp.zeros((DEPTH, DIM), jnp.float32), 'w1': jax.random.normal(ks[3], (DEPTH, DIM, 2 * HID), jnp.float32) * 0.02, 'b1': jnp.zeros((DEPTH, 2 * HID), jnp.float32), 'w2': jax.random.normal(ks[4], (DEPTH, HID, DIM), jnp.float32) * 0.02, 'b2': jnp.zeros((DEPTH, DIM), jnp.float32)}
    _L0_ffn_in = _L0_ffn_setup()
    _L0_c = _w((lambda *s: np.random.randn(*s).astype(np.float32) * 0.05)(2, 128))
    _L0_wmod = _w((lambda *s: np.random.randn(*s).astype(np.float32) * 0.05)(128, 6 * 128) * 128 ** (-0.5))
    _d = {'L0_attn_x': _L0_attn_in['x'], 'L0_attn_W_dkv': _L0_attn_in['W_dkv'], 'L0_attn_W_uk': _L0_attn_in['W_uk'], 'L0_attn_W_uv': _L0_attn_in['W_uv'], 'L0_attn_W_dq': _L0_attn_in['W_dq'], 'L0_attn_W_uq': _L0_attn_in['W_uq'], 'L0_attn_W_qr': _L0_attn_in['W_qr'], 'L0_attn_W_kr': _L0_attn_in['W_kr'], 'L0_attn_W_out': _L0_attn_in['W_out'], 'L0_attn_idx_wq': _L0_attn_in['idx_wq'], 'L0_attn_idx_wk': _L0_attn_in['idx_wk'], 'L0_attn_idx_w': _L0_attn_in['idx_w'], 'L0_attn_raw_delta': _L0_attn_in['raw_delta'], 'L0_ffn_wqkv': _L0_ffn_in['wqkv'], 'L0_ffn_q_scale': _L0_ffn_in['q_scale'], 'L0_ffn_k_scale': _L0_ffn_in['k_scale'], 'L0_ffn_wo': _L0_ffn_in['wo'], 'L0_ffn_ln_g': _L0_ffn_in['ln_g'], 'L0_ffn_ln_b': _L0_ffn_in['ln_b'], 'L0_ffn_w1': _L0_ffn_in['w1'], 'L0_ffn_b1': _L0_ffn_in['b1'], 'L0_ffn_w2': _L0_ffn_in['w2'], 'L0_ffn_b2': _L0_ffn_in['b2'], 'L0_c': _L0_c, 'L0_wmod': _L0_wmod}
    _x0 = _d['L0_attn_x']
    _d['L0_attn_x'] = jax.random.normal(jax.random.fold_in(jax.random.key(seed), 1), (2, 1024, 128), dtype=_x0.dtype)
    del _x0
    return _d

def reference(L0_attn_x, L0_attn_W_dkv, L0_attn_W_uk, L0_attn_W_uv, L0_attn_W_dq, L0_attn_W_uq, L0_attn_W_qr, L0_attn_W_kr, L0_attn_W_out, L0_attn_idx_wq, L0_attn_idx_wk, L0_attn_idx_w, L0_attn_raw_delta, L0_ffn_wqkv, L0_ffn_q_scale, L0_ffn_k_scale, L0_ffn_wo, L0_ffn_ln_g, L0_ffn_ln_b, L0_ffn_w1, L0_ffn_b1, L0_ffn_w2, L0_ffn_b2, L0_c, L0_wmod):

    def _L0_attn_ref(x, W_dkv, W_uk, W_uv, W_dq, W_uq, W_qr, W_kr, W_out, idx_wq, idx_wk, idx_w, raw_delta):
        import jax, jax.numpy as jnp
        import numpy as np
        B, L = (2, 128)
        D_MODEL, D_CKV, D_CQ = (128, 32, 64)
        N_HEAD, D_HEAD, D_ROPE = (8, 64, 32)
        N_IDX_HEAD = 4
        K_TS, LW = (96, 64)
        ROPE_BASE = 10000.0

        def _pope(x, angles):
            cos, sin = (jnp.cos(angles), jnp.sin(angles))
            mu1, mu2 = jnp.split(jax.nn.softplus(x), 2, axis=-1)
            return jnp.concatenate([mu1 * cos - mu2 * sin, mu1 * sin + mu2 * cos], axis=-1)

        def _forward(x, W_dkv, W_uk, W_uv, W_dq, W_uq, W_qr, W_kr, W_out, idx_wq, idx_wk, idx_w, raw_delta):
            B_, L_, _ = x.shape
            c_kv = x @ W_dkv
            q_i = (x @ idx_wq).reshape(B_, L_, N_IDX_HEAD, D_HEAD)
            k_i = x @ idx_wk
            s_i = jax.nn.relu(jnp.einsum('bthd,bsd->bths', q_i, k_i))
            I = jnp.einsum('bths,h->bts', s_i, idx_w)
            qpos = jnp.arange(L_)[:, None]
            kpos = jnp.arange(L_)[None, :]
            local = (kpos >= qpos - LW + 1) & (kpos <= qpos)
            causal = kpos > qpos
            I = jnp.where(local[None], jnp.inf, I)
            I = jnp.where(causal[None], -jnp.inf, I)
            kk = min(K_TS, L_)
            _, idx = jax.lax.top_k(I, kk)
            bi = jnp.arange(B_)[:, None, None]
            key_c = (c_kv @ W_uk)[bi, idx].reshape(B_, L_, kk, N_HEAD, D_HEAD)
            value = (c_kv @ W_uv)[bi, idx].reshape(B_, L_, kk, N_HEAD, D_HEAD)
            c_q = x @ W_dq
            query_c = (c_q @ W_uq).reshape(B_, L_, N_HEAD, D_HEAD)
            half = D_ROPE // 2
            theta = 1.0 / ROPE_BASE ** (2.0 * jnp.arange(half, dtype=jnp.float32) / D_ROPE)
            delta = -2.0 * jnp.pi * jax.nn.sigmoid(raw_delta)
            angles_q = jnp.arange(L_, dtype=jnp.float32)[:, None] * theta[None, :] + delta
            query_r = _pope((c_q @ W_qr).reshape(B_, L_, N_HEAD, D_ROPE), angles_q[None, :, None, :])
            kr_sel = (x @ W_kr)[bi, idx]
            angles_k = jnp.arange(kk, dtype=jnp.float32)[:, None] * theta[None, :] + delta
            key_r = _pope(kr_sel, angles_k[None, None, :, :])
            scale = (D_HEAD + D_ROPE) ** (-0.5)
            q_c = query_c.transpose(0, 2, 1, 3)
            q_r = query_r.transpose(0, 2, 1, 3)
            k_c = key_c.transpose(0, 3, 1, 2, 4)
            v = value.transpose(0, 3, 1, 2, 4)
            scores = (jnp.einsum('bhld,bhlkd->bhlk', q_c, k_c) + jnp.einsum('bhld,blkd->bhlk', q_r, key_r)) * scale
            attn = jax.nn.softmax(scores.astype(jnp.float32), axis=-1).astype(v.dtype)
            out = jnp.einsum('bhlk,bhlkd->bhld', attn, v)
            out = out.transpose(0, 2, 1, 3).reshape(B_, L_, N_HEAD * D_HEAD)
            return out @ W_out
        return _forward(x, W_dkv, W_uk, W_uv, W_dq, W_uq, W_qr, W_kr, W_out, idx_wq, idx_wk, idx_w, raw_delta)

    def _L0_ffn_ref(x, wqkv, q_scale, k_scale, wo, ln_g, ln_b, w1, b1, w2, b2):
        import jax, jax.numpy as jnp
        import numpy as np
        DIM = 128
        DEPTH = 2
        HEADS = 8
        DIM_HEAD = 64
        WINDOW = 64
        INNER = HEADS * DIM_HEAD
        HID = int(DIM * 4 * 2 / 3)
        B, N = (2, 1024)
        QK_SCALE = 8.0

        def shift_token(t):
            t1, t2 = jnp.split(t, 2, axis=-1)
            t2 = jnp.pad(t2, ((0, 0), (1, 0), (0, 0)))[:, :-1]
            return jnp.concatenate([t1, t2], axis=-1)

        def l2norm(t):
            return t / jnp.clip(jnp.linalg.norm(t, axis=-1, keepdims=True), 1e-12)

        def rotate_half(x):
            x1, x2 = jnp.split(x, 2, axis=-1)
            return jnp.concatenate([-x2, x1], axis=-1)

        def rotary_xpos(q, k):
            n = q.shape[-2]
            half_idx = jnp.arange(0, DIM_HEAD, 2, dtype=jnp.float32)
            inv_freq = 1.0 / 10000.0 ** (half_idx / DIM_HEAD)
            t = jnp.arange(n, dtype=jnp.float32)
            freqs = t[:, None] * inv_freq[None, :]
            freqs = jnp.concatenate([freqs, freqs], axis=-1)
            base = (half_idx + 0.4 * DIM_HEAD) / (1.4 * DIM_HEAD)
            power = (t - n // 2) / float(WINDOW // 2)
            scale = base[None, :] ** power[:, None]
            scale = jnp.concatenate([scale, scale], axis=-1)
            cos, sin = (jnp.cos(freqs), jnp.sin(freqs))
            q = q * cos * scale + rotate_half(q) * sin * scale
            k = k * cos / scale + rotate_half(k) * sin / scale
            return (q, k)

        def local_attention(q, k, v):
            b, h, n, d = q.shape
            w = n // WINDOW
            bq = q.reshape(b, h, w, WINDOW, d) * QK_SCALE
            bk = k.reshape(b, h, w, WINDOW, d)
            bv = v.reshape(b, h, w, WINDOW, d)

            def look_around(t):
                p = jnp.pad(t, ((0, 0), (0, 0), (1, 0), (0, 0), (0, 0)))
                return jnp.concatenate([p[:, :, :w], p[:, :, 1:]], axis=3)
            bk, bv = (look_around(bk), look_around(bv))
            bt = jnp.arange(n).reshape(w, WINDOW)
            btp = jnp.pad(bt, ((1, 0), (0, 0)), constant_values=-1)
            btk = jnp.concatenate([btp[:w], btp[1:]], axis=1)
            sim = jnp.einsum('bhwid,bhwjd->bhwij', bq, bk)
            i = bt[:, :, None]
            j = btk[:, None, :]
            mask = (i < j) | (i > j + WINDOW) | (j == -1)
            sim = jnp.where(mask, -jnp.finfo(sim.dtype).max, sim)
            attn = jax.nn.softmax(sim, axis=-1)
            out = jnp.einsum('bhwij,bhwjd->bhwid', attn, bv)
            return out.reshape(b, h, n, d)

        def _layer(x, wqkv, qs, ksc, wo, lg, lb, w1, b1, w2, b2):
            b, n, _ = x.shape
            h = shift_token(x)
            qkv = h @ wqkv
            q, k, v = jnp.split(qkv, 3, axis=-1)
            to_heads = lambda t: t.reshape(b, n, HEADS, DIM_HEAD).transpose(0, 2, 1, 3)
            q, k, v = (to_heads(q), to_heads(k), to_heads(v))
            q = l2norm(q) * qs
            k = l2norm(k) * ksc
            q, k = rotary_xpos(q, k)
            o = local_attention(q, k, v)
            o = o.transpose(0, 2, 1, 3).reshape(b, n, INNER)
            x = x + o @ wo
            h = shift_token(x)
            mu = h.mean(-1, keepdims=True)
            var = h.var(-1, keepdims=True)
            h = (h - mu) / jnp.sqrt(var + 1e-05) * lg + lb
            h = h @ w1 + b1
            a, g = jnp.split(h, 2, axis=-1)
            h = a * jax.nn.gelu(g, approximate=False)
            x = x + h @ w2 + b2
            return x
        for l in range(DEPTH):
            x = _layer(x, wqkv[l], q_scale[l], k_scale[l], wo[l], ln_g[l], ln_b[l], w1[l], b1[l], w2[l], b2[l])
        return x
    x = L0_attn_x
    mod = (_silu(L0_c) @ L0_wmod).reshape(L0_c.shape[0], 6, 1, -1)
    sa, ca, ga, sb, cb, gb = (mod[:, 0], mod[:, 1], mod[:, 2], mod[:, 3], mod[:, 4], mod[:, 5])
    ga = (2 * (ga >= 0) - 1) * jnp.maximum(jnp.abs(ga), 0.25)
    gb = (2 * (gb >= 0) - 1) * jnp.maximum(jnp.abs(gb), 0.25)
    h = _layernorm(x, axis=-1) * (1 + ca) + sa
    x = x + ga * _L0_attn_ref(h, L0_attn_W_dkv, L0_attn_W_uk, L0_attn_W_uv, L0_attn_W_dq, L0_attn_W_uq, L0_attn_W_qr, L0_attn_W_kr, L0_attn_W_out, L0_attn_idx_wq, L0_attn_idx_wk, L0_attn_idx_w, L0_attn_raw_delta)
    h = _layernorm(x, axis=-1) * (1 + cb) + sb
    x = x + gb * _L0_ffn_ref(h, L0_ffn_wqkv, L0_ffn_q_scale, L0_ffn_k_scale, L0_ffn_wo, L0_ffn_ln_g, L0_ffn_ln_b, L0_ffn_w1, L0_ffn_b1, L0_ffn_w2, L0_ffn_b2)
    return x

_drawn_inputs = setup_inputs


def setup_inputs(seed=0):
    import zlib

    import numpy as np

    out = dict(_drawn_inputs(seed))
    spreads = {'L0_attn_idx_w': (1.0, 0.6),
     'L0_ffn_q_scale': (1.0, 0.6),
     'L0_ffn_k_scale': (1.0, 0.6),
     'L0_ffn_ln_g': (1.0, 0.6),
     'L0_ffn_ln_b': (0.0, 0.8),
     'L0_ffn_b1': (0.0, 0.8),
     'L0_ffn_b2': (0.0, 0.757)}
    factors = {'L0_attn_W_qr': 6.246,
     'L0_attn_W_kr': 4.619,
     'L0_attn_raw_delta': 64.0,
     'L0_ffn_wqkv': 8.0,
     'L0_ffn_wo': 8.0,
     'L0_ffn_w1': 8.0,
     'L0_ffn_w2': 8.0}
    for name, (base, spread) in spreads.items():
        noise = np.random.default_rng([zlib.crc32(name.encode()), seed]).standard_normal(out[name].shape)
        drawn = base * np.exp(spread * noise) if base else spread * noise
        out[name] = jnp.asarray(drawn.astype(out[name].dtype))
    for name, factor in factors.items():
        out[name] = (out[name] * factor).astype(out[name].dtype)
    return out
```

```python
from contextlib import ExitStack

import numpy as np

import concourse.bass as bass
from concourse import mybir

ALU = mybir.AluOpType
ACT = mybir.ActivationFunctionType
AX_X = mybir.AxisListType.X
F32 = mybir.dt.float32
F16 = mybir.dt.float16
BF16 = mybir.dt.bfloat16
U16 = mybir.dt.uint16

P = 128
B, L, D = 2, 1024, 128
TILES = L // P
CKV, CQ, H, DH, ROPE = 32, 64, 8, 64, 32
HALF = ROPE // 2
IDX_HEADS, KTS, LW = 4, 96, 64
NSEL = KTS - LW
TOP_ROUNDS = NSEL // 8
PAIR = 32
UNIT = 16
PAIRS = L // PAIR
PPT = P // PAIR
GROUPS = PAIR // 4
WIN = 80
SCOLS = P + WIN
ATTN_SCALE = float(DH + ROPE) ** -0.5
DEPTH, INNER, WINDOW = 2, 512, 64
HID = int(D * 4 * 2 / 3)
HCH = [(0, 128), (128, 128), (256, HID - 256)]
QK_SCALE = 8.0
LN_EPS = 1e-5
NEG = -1e30
NEGMAX = -3e38
PI = 3.1415925


def constants():
    f = np.float32
    theta = (1.0 / f(10000.0) ** (f(2.0) * np.arange(HALF, dtype=f) / f(ROPE))).astype(f)
    t = np.arange(L, dtype=f)
    out = {}
    out["ident"] = np.eye(P, dtype=f)
    def rope(pos):
        a = (pos.astype(np.float64)[None, :] * theta.astype(np.float64)[:, None])
        c, s = np.cos(a).astype(f), np.sin(a).astype(f)
        p1 = np.concatenate([c, c, -s, s], 0)
        p2 = np.concatenate([-s, -s, -c, c], 0)
        return p1, p2
    rel = t + np.maximum(0.0, t - (LW - 1))
    out["rope"] = np.stack([*rope(t), *rope(rel)], 1).astype(f)
    j = (LW + np.arange(P) % NSEL).astype(np.float64)[:, None] * theta.astype(np.float64)[None, :]
    c, s = np.cos(j), np.sin(j)
    out["rank"] = np.stack([np.concatenate([c, c], 1), np.concatenate([-s, -s], 1),
                            np.concatenate([-s, s], 1), np.concatenate([-c, c], 1)], 1).astype(f)
    selk = np.zeros((P, P), f)
    selq = np.zeros((P, P), f)
    for i in range(32):
        selk[i, i] = 1
        selq[i, i] = selq[i, 64 + i] = 1
        for src in (64 + i, 96 + i):
            selk[src, 64 + i] = selk[src, 96 + i] = 1
            selq[src, 32 + i] = selq[src, 96 + i] = 1
    out["sel"] = np.stack([selk, selq], 1)
    out["keys"] = (np.arange(P)[:, None] + P * np.arange(TILES)[None, :]).astype(f)
    r = np.arange(P)
    tok = r // H
    top = (np.arange(P)[None, :] // NSEL) == (tok % 4)[:, None]
    w = np.arange(WIN)[None, :]
    late = (w >= tok[:, None] + 1) & (w <= tok[:, None] + LW)
    early = np.broadcast_to(w < LW, (P, WIN))
    m = np.stack([np.concatenate([top, early], 1), np.concatenate([top, late], 1)], 1)
    out["umask"] = np.where(m, f(0), f(NEG)).astype(f)
    out["imask"] = np.where(np.arange(P)[None, :] <= r[:, None], f(0), f(NEG)).astype(f)
    key = LW + np.arange(NSEL)[None, :]
    fut = (key > r[:, None])
    out["future"] = np.stack([(~fut).astype(f), fut * key.astype(f)], 1).astype(f)
    half = np.arange(0, DH, 2, dtype=f)
    inv = (f(1.0) / f(10000.0) ** (half / f(DH))).astype(f)
    fr = (t[:, None] * inv[None, :]).astype(f)
    fr = np.concatenate([fr, fr], -1)
    base = ((half + f(0.4 * DH)) / f(1.4 * DH)).astype(f)
    power = ((t - L // 2) / f(WINDOW // 2)).astype(f)
    sc = (base[None, :] ** power[:, None]).astype(f)
    sc = np.concatenate([sc, sc], -1)
    cos, sin = np.cos(fr).astype(f), np.sin(fr).astype(f)
    sgn = np.concatenate([-np.ones(32, f), np.ones(32, f)])[None, :]
    tab = np.stack([cos * sc, cos / sc, sgn * sin * sc, sgn * sin / sc], 1)
    out["xpos"] = np.ascontiguousarray(tab.reshape(TILES, P, 4, DH).transpose(1, 0, 2, 3)).astype(f)
    q = (r % WINDOW)[:, None]
    k = np.arange(P)[None, :]
    ok = (k >= q) & (k <= q + WINDOW)
    first = ok & ((r >= WINDOW)[:, None] | (k >= WINDOW))
    out["wmask"] = np.where(np.stack([first, ok], 1), f(0), f(NEG)).astype(f)
    return out


def kernel_program(nc, ins, consts, out):
    x_d = ins["L0_attn_x"]
    idx_d = nc.dram_tensor("picked_idx", (B * TILES, P, NSEL), F16, kind="Internal").ap()
    c_d = nc.dram_tensor("latent_rows", (B * L, CKV), F32, kind="Internal").ap()

    with ExitStack() as top:
        top.enter_context(nc.allow_non_contiguous_dma(reason="vectors of at most 256 elements, one per partition"))

        def sb(name, shape, dt=F32, ctx=top):
            return ctx.enter_context(nc.sbuf_tensor(name, list(shape), dt))

        ident = sb("ident", [P, P])
        ones = sb("ones", [P, P])
        mod = sb("mod", [P, 6, B])
        x1T = sb("x1T", [P, B, L])
        wqkv = sb("wqkv", [P, DEPTH, 3 * INNER])
        wo = sb("wo", [P, DEPTH, 4, D])
        w1 = sb("w1", [P, DEPTH, 2 * HID])
        w2 = sb("w2", [P, DEPTH, 3, D])
        fvec = sb("fvec", [P, DEPTH, 16])

        with ExitStack() as attn:
            a = Attention(nc, attn, ins, consts, sb, ident, ones, mod, x1T, idx_d, c_d)
            a.ffn = (wqkv, wo, w1, w2, fvec)
            setup_block(nc, a, x_d)
            attention_block(nc, a)
        stack_blocks(nc, top, ins, consts, out, ident, ones, mod, x1T, wqkv, wo, w1, w2, fvec)


class Attention:

    def __init__(self, nc, ctx, ins, consts, sb_, ident, ones, mod, x1T, idx_d, c_d):
        def sb(name, shape, dt=F32):
            return sb_(name, shape, dt, ctx)
        self.ctx, self.ins, self.consts = ctx, ins, consts
        self.ident, self.ones, self.mod, self.x1T, self.idx_d, self.c_d = ident, ones, mod, x1T, idx_d, c_d
        self.hT = sb("hT", [P, B, L])
        self.cqT = sb("cqT", [CQ, B, L])
        self.kiT = sb("kiT", [P, B, L])
        self.khT = sb("khT", [P, B, L])
        self.tabs = sb("tabs", [P, 2, L])
        self.feat = sb("feat", [P, B * TILES, 3, 64], BF16)
        self.WQ = sb("WQ", [CQ, H, P])
        self.wiq = sb("wiq", [P, IDX_HEADS * DH])
        self.Wvo = sb("Wvo", [CKV, H, D])
        self.selm = sb("selm", [P, 2, P])
        self.umask = sb("umask", [P, 2, SCOLS])
        self.imask = sb("imask", [P, P])
        self.future = sb("future", [P, 2, NSEL])
        self.keys = sb("keys", [P, TILES])
        self.wix = sb("wix", [P, IDX_HEADS])
        self.rankCS = sb("rankCS", [P, 2, ROPE])


def setup_block(nc, a, x_d):
    ins, consts = a.ins, a.consts
    wqkv, wo, w1, w2, fvec = a.ffn
    with ExitStack() as ctx:
        def sb(name, shape, dt=F32):
            return ctx.enter_context(nc.sbuf_tensor(name, list(shape), dt))

        def sem(name):
            return ctx.enter_context(nc.semaphore(name))

        x = sb("x", [P, B * TILES, D])
        xn = sb("xn", [P, B * TILES, D])
        st = sb("st", [P, B * TILES, 6])
        mv = sb("mv", [P, B * TILES, 2])
        rstd = sb("rstd", [P, B * TILES])
        mhalf = sb("mhalf", [P, B * TILES])
        wuq = sb("wuq", [CQ, H * DH])
        wuk = sb("wuk", [CKV, H * DH])
        wuv = sb("wuv", [CKV, H * DH])
        wout = sb("wout", [P, 4, D])
        wdq = sb("wdq", [P, CQ])
        WK = sb("WK", [P, P])
        WF = sb("WF", [P, 64])
        wki = sb("wki", [P, 2, DH])
        wT = sb("wT", [P, 4, 128])
        cT = sb("cT", [P, B])
        ce = sb("ce", [P, B])
        cg = sb("cg", [P, B])
        cs = sb("cs", [P, B])
        wmod = sb("wmod", [P, 6, D])
        gsg = sb("gsg", [P, 2, B])
        gab = sb("gab", [P, 2, B])
        dl = sb("dl", [P, 33])
        d1 = sb("d1", [P, 33])
        d2 = sb("d2", [P, 33])
        sg = sb("sg", [P, 33])
        arg = sb("arg", [P, 2, 33])
        sn = sb("sn", [P, 2, 33])
        sind = sb("sind", [P, 33])
        cosd = sb("cosd", [P, 33])
        ropet = sb("ropet", [P, 4, L])
        rankt = sb("rankt", [P, 4, ROPE])
        rtmp = sb("rtmp", [P, 2, ROPE])
        kab = sb("kab", [P, B * L])
        kex = sb("kex", [P, B * L])
        F = sb("F", [P, B * TILES, 64])
        F2 = sb("F2", [P, B * TILES, 64])
        fab = sb("fab", [P, B * TILES, ROPE])
        fex = sb("fex", [P, B * TILES, ROPE])
        banks = [ctx.enter_context(nc.psum_tensor(f"bank{i}", [P, 512], F32)) for i in range(8)]

        x_loaded, w_loaded, c_loaded = sem("x_loaded"), sem("w_loaded"), sem("c_loaded")
        ffn_loaded, rows_stored = sem("ffn_loaded"), sem("rows_stored")
        zeroed, stats, aggr, vareps, rstd_ready, normed = (
            sem("zeroed"), sem("stats"), sem("aggr"), sem("vareps"), sem("rstd_ready"), sem("normed"))
        c_exp, c_den, c_gate, c_silu = sem("c_exp"), sem("c_den"), sem("c_gate"), sem("c_silu")
        mod_mm, mod_copied, mod_gate, mod_ready = sem("mod_mm"), sem("mod_copied"), sem("mod_gate"), sem("mod_ready")
        d_step, d_exp, d_sin, tab_step, tabs_ready = (
            sem("d_step"), sem("d_exp"), sem("d_sin"), sem("tab_step"), sem("tabs_ready"))
        turned, turn_copied = sem("turned"), sem("turn_copied")
        wt_turned, wt_copied, fused, fused_copied = sem("wt_turned"), sem("wt_copied"), sem("fused"), sem("fused_copied")
        proj, proj_copied = sem("proj"), sem("proj_copied")
        kv_mm, kv_abs, kv_exp, kv_ln, kv_soft, kv_rot, kv_sum, kv_done = [
            sem(n) for n in ("kv_mm", "kv_abs", "kv_exp", "kv_ln", "kv_soft", "kv_rot", "kv_sum", "kv_done")]
        ft_mm, ft_abs, ft_exp, ft_ln, ft_soft, ft_c, ft_split = [
            sem(n) for n in ("ft_mm", "ft_abs", "ft_exp", "ft_ln", "ft_soft", "ft_c", "ft_split")]

        N_W, N_C = 23, 18
        block = ctx.enter_context(nc.Block())

        @block.sync
        def _(sp):
            sp.dma_start(x[:], x_d.rearrange("b (n p) d -> p (b n) d", p=P)).then_inc(x_loaded, 16)
            def w(dst, src):
                sp.dma_start(dst, src).then_inc(w_loaded, 16)
            w(cT[:], ins["L0_c"].rearrange("b d -> d b"))
            w(wmod[:], ins["L0_wmod"].rearrange("k (m d) -> k m d", m=6))
            w(wuq[:], ins["L0_attn_W_uq"])
            w(wuk[:], ins["L0_attn_W_uk"])
            w(wuv[:], ins["L0_attn_W_uv"])
            w(wout[:], ins["L0_attn_W_out"].rearrange("(n p) d -> p n d", p=P))
            w(wdq[:], ins["L0_attn_W_dq"])
            w(WK[:, 0:CKV], ins["L0_attn_W_dkv"])
            kr = ins["L0_attn_W_kr"]
            w(WK[:, 64:96], kr)
            w(WK[:, 96:112], kr[:, HALF:ROPE])
            w(WK[:, 112:128], kr[:, 0:HALF])
            w(WF[:, 0:CKV], ins["L0_attn_W_dkv"])
            w(WF[:, CKV:64], kr)
            w(wki[:, 0, :], ins["L0_attn_idx_wk"])
            w(wki[:, 1, :], ins["L0_attn_idx_wk"])
            w(a.wiq[:], ins["L0_attn_idx_wq"])
            qr = ins["L0_attn_W_qr"].rearrange("k (h d) -> k h d", h=H)
            w(a.WQ[:, :, 64:96], qr)
            w(a.WQ[:, :, 96:112], qr[:, :, HALF:ROPE])
            w(a.WQ[:, :, 112:128], qr[:, :, 0:HALF])
            w(a.wix[:], ins["L0_attn_idx_w"].partition_broadcast(P))
            rd = ins["L0_attn_raw_delta"]
            w(dl[:, 0:HALF], rd.partition_broadcast(P))
            w(dl[:, HALF:ROPE], rd.partition_broadcast(P))
            w(dl[0:HALF, 32:33], rd.rearrange("(p o) -> p o", o=1))
            sp.wait_ge(ft_c, 1)
            sp.dma_start(a.c_d.rearrange("(n p) c -> p n c", p=P), F[:, :, 0:CKV]).then_inc(rows_stored, 16)
            sp.wait_ge(rows_stored, 16)

        @block.gpsimd
        def _(pool):
            def c(dst, src):
                pool.dma_start(dst, src).then_inc(c_loaded, 16)
            c(a.ident[:], consts["ident"])
            rd = ins["L0_attn_raw_delta"].rearrange("(p o) -> p o", o=1)
            for r in range(16, P, HALF):
                c(dl[r:r + HALF, 32:33], rd)
            c(ropet[64:128], consts["rope"])
            c(rankt[:], consts["rank"])
            c(a.selm[:], consts["sel"])
            c(a.keys[:], consts["keys"])
            c(a.umask[:], consts["umask"])
            c(a.imask[:], consts["imask"])
            c(a.future[:], consts["future"])
            for l in range(DEPTH):
                pool.dma_start(wqkv[:, l], ins["L0_ffn_wqkv"][l]).then_inc(ffn_loaded, 16)
                pool.dma_start(wo[:, l], ins["L0_ffn_wo"][l].rearrange("(n p) d -> p n d", p=P)).then_inc(ffn_loaded, 16)
                pool.dma_start(w1[:, l], ins["L0_ffn_w1"][l]).then_inc(ffn_loaded, 16)
                pool.dma_start(w2[:, l, 0:2], ins["L0_ffn_w2"][l, 0:256].rearrange("(n p) d -> p n d", p=P)).then_inc(ffn_loaded, 16)
                pool.dma_start(w2[0:HID - 256, l, 2], ins["L0_ffn_w2"][l, 256:HID]).then_inc(ffn_loaded, 16)
                for k, name in enumerate(("L0_ffn_ln_g", "L0_ffn_ln_b", "L0_ffn_b2")):
                    pool.dma_start(fvec[:, l, k:k + 1], ins[name][l].rearrange("(p o) -> p o", o=1)).then_inc(ffn_loaded, 16)
                for half in range(2):
                    for k, (o, n) in enumerate(HCH):
                        pool.dma_start(fvec[0:n, l, 3 + 3 * half + k:4 + 3 * half + k],
                                       ins["L0_ffn_b1"][l, half * HID + o:half * HID + o + n].rearrange("(p o) -> p o", o=1)
                                       ).then_inc(ffn_loaded, 16)
            pool.wait_ge(aggr, B * TILES)
            pool.tensor_scalar(rstd[:], mv[:, :, 1], LN_EPS, None, ALU.add).then_inc(vareps, 1)
            pool.wait_ge(vareps, 1)
            pool.wait_ge(zeroed, 1)
            pool.tensor_tensor(rstd[:], rstd[:], mhalf[:], ALU.pow).then_inc(rstd_ready, 1)
            pool.wait_ge(ffn_loaded, 16 * 14 * DEPTH)

        @block.tensor
        def _(pe):
            pe.wait_ge(w_loaded, 16 * N_W)
            pe.wait_ge(c_silu, 1)
            for k in range(6):
                mm = pe.matmul(banks[7][:, 2 * k:2 * k + 2], wmod[:, k, :], cs[:], start=True, stop=True)
            mm.then_inc(mod_mm, 1)
            pe.wait_ge(c_loaded, 16 * N_C_POOL)
            for n in range(4):
                bk = banks[n]
                pe.transpose(bk[:, 0:64], wuq[:, n * P:(n + 1) * P], a.ident[0:CQ, 0:CQ])
                pe.transpose(bk[:, 64:96], wuk[:, n * P:(n + 1) * P], a.ident[0:CKV, 0:CKV])
                pe.transpose(bk[:, 96:128], wuv[:, n * P:(n + 1) * P], a.ident[0:CKV, 0:CKV]).then_inc(wt_turned, 1)
            pe.wait_ge(wt_copied, 4)
            for h in range(H):
                r = 64 * (h % 2)
                pe.matmul(banks[4 - h % 2][0:CQ, (h // 2) * 32:(h // 2) * 32 + 32], wT[r:r + 64, h // 2, 0:64],
                          wT[r:r + 64, h // 2, 64:96], start=True, stop=True)
            for h in range(H):
                r = 64 * (h % 2)
                mm = pe.matmul(banks[5 + h % 2][0:CKV, (h // 2) * D:(h // 2 + 1) * D], wT[r:r + 64, h // 2, 96:128],
                               wout[r:r + 64, h // 2, :], start=True, stop=True)
            mm.then_inc(fused, 1)
            for q in range(8):
                pe.wait_ge(normed, min(4 * q + 4, 16))
                if q >= 4:
                    pe.wait_ge(turn_copied, q - 3)
                if q == 3:
                    pe.wait_ge(fused_copied, 4)
                src = xn if q < 4 else x
                for n in range(4):
                    mm = pe.transpose(banks[q % 4][:, n * P:(n + 1) * P], src[:, 4 * (q % 4) + n, :], a.ident[:])
                mm.then_inc(turned, 1)
            hT = a.hT[:].rearrange("p b t -> p (b t)")
            pe.wait_ge(turn_copied, 8)
            for q in range(4):
                pe.matmul(banks[q][:], WK[:], hT[:, q * 512:(q + 1) * 512], start=True, stop=True).then_inc(kv_mm, 1)
            for n in range(16):
                mm = pe.matmul(banks[4 + n // 8][:, 64 * (n % 8):64 * (n % 8) + 64], hT[:, n * P:(n + 1) * P],
                               WF[:], start=True, stop=True)
            mm.then_inc(ft_mm, 1)
            for q in range(4):
                if q >= 1:
                    pe.wait_ge(proj_copied, 2 * q)
                pe.matmul(banks[6][0:CQ, :], wdq[:], hT[:, q * 512:(q + 1) * 512], start=True, stop=True).then_inc(proj, 1)
                pe.matmul(banks[7][:], wki[:].rearrange("p a d -> p (a d)"), hT[:, q * 512:(q + 1) * 512],
                          start=True, stop=True).then_inc(proj, 1)
            for q in range(4):
                pe.wait_ge(kv_rot, q + 1)
                pe.matmul(banks[q][:], a.selm[:, 0, :], a.khT[:].rearrange("p b t -> p (b t)")[:, q * 512:(q + 1) * 512],
                          start=True, stop=True).then_inc(kv_sum, 1)

        @block.scalar
        def _(act):
            act.preload_act_table_set("natural_log_exp_and_others")
            act.wait_ge(w_loaded, 16 * N_W)
            act.activation(ce[:], cT[:], ACT.Exp, scale=-1.0).then_inc(c_exp, 1)
            act.wait_ge(c_loaded, 16 * N_C_POOL)
            act.activation(d1[:], dl[:], ACT.Exp, scale=-1.0).then_inc(d_exp, 1)
            act.wait_ge(d_step, 3)
            act.activation(sn[:], arg[:], ACT.Sin).then_inc(d_sin, 1)
            for n in range(4):
                act.wait_ge(wt_turned, n + 1)
                act.copy(wT[:, n, :], banks[n][:, 0:128]).then_inc(wt_copied, 1)
            hT = a.hT[:].rearrange("p b t -> p (b t)")
            xT = a.x1T[:].rearrange("p b t -> p (b t)")
            for q in range(8):
                act.wait_ge(turned, q + 1)
                if q == 0:
                    act.wait_ge(mod_ready, 1)
                b = (q % 4) // 2
                sl = slice((q % 4) * 512, (q % 4 + 1) * 512)
                if q < 4:
                    act.activation(hT[:, sl], banks[q % 4][:], ACT.Identity, scale=a.mod[:, 1, b:b + 1],
                                   bias=a.mod[:, 0, b:b + 1]).then_inc(turn_copied, 1)
                else:
                    act.copy(xT[:, sl], banks[q % 4][:]).then_inc(turn_copied, 1)
            for q in range(4):
                sl = slice(q * 512, (q + 1) * 512)
                act.wait_ge(kv_mm, q + 1)
                act.copy(a.khT[:].rearrange("p b t -> p (b t)")[0:64, sl], banks[q][0:64, :])
                act.activation(kab[64:128, sl], banks[q][64:128, :], ACT.Abs).then_inc(kv_abs, 1)
                act.wait_ge(kv_abs, q + 1)
                act.activation(kex[64:128, sl], kab[64:128, sl], ACT.Exp, scale=-1.0).then_inc(kv_exp, 1)
                act.wait_ge(kv_exp, q + 1)
                act.activation(kab[64:128, sl], kex[64:128, sl], ACT.Ln, bias=1.0).then_inc(kv_ln, 1)
            act.wait_ge(ft_mm, 1)
            for k in range(2):
                fv = banks[4 + k][:].rearrange("p (n f) -> p n f", f=64)
                act.activation(fab[:, 8 * k:8 * k + 8, :], fv[:, :, CKV:64], ACT.Abs)
                act.copy(F[:, 8 * k:8 * k + 8, 0:CKV], fv[:, :, 0:CKV]).then_inc(ft_abs, 1)
            act.wait_ge(ft_abs, 2)
            act.activation(fex[:], fab[:], ACT.Exp, scale=-1.0).then_inc(ft_exp, 1)
            act.wait_ge(ft_exp, 1)
            act.activation(fab[:], fex[:], ACT.Ln, bias=1.0).then_inc(ft_ln, 1)
            cq = a.cqT[:].rearrange("p b t -> p (b t)")
            ki = a.kiT[:].rearrange("p b t -> p (b t)")
            for q in range(4):
                sl = slice(q * 512, (q + 1) * 512)
                act.wait_ge(proj, 2 * q + 1)
                act.copy(cq[:, sl], banks[6][0:CQ, :]).then_inc(proj_copied, 1)
                act.wait_ge(proj, 2 * q + 2)
                act.copy(ki[:, sl], banks[7][:]).then_inc(proj_copied, 1)
            for q in range(4):
                act.wait_ge(kv_sum, q + 1)
                act.copy(a.khT[:].rearrange("p b t -> p (b t)")[:, q * 512:(q + 1) * 512], banks[q][:]).then_inc(kv_done, 1)

        @block.vector
        def _(dve):
            dve.memset(mhalf[:], -0.5)
            dve.memset(WK[:, CKV:64], 0.0)
            dve.memset(a.ones[:], 1.0 / D)
            dve.memset(a.WQ[:, :, CKV:64], 0.0).then_inc(zeroed, 1)
            dve.wait_ge(x_loaded, 16)
            for n in range(B * TILES):
                dve.bn_stats(st[:, n, :], x[:, n, :]).then_inc(stats, 1)
            for n in range(B * TILES):
                dve.wait_ge(stats, n + 1)
                dve.bn_aggr(mv[:, n, :], st[:, n, :]).then_inc(aggr, 1)
            dve.wait_ge(c_exp, 1)
            dve.tensor_scalar(cg[:], ce[:], 1.0, None, ALU.add).then_inc(c_den, 1)
            dve.wait_ge(c_den, 1)
            dve.reciprocal(ce[:], cg[:]).then_inc(c_gate, 1)
            dve.wait_ge(c_gate, 1)
            dve.tensor_tensor(cs[:], cT[:], ce[:], ALU.mult).then_inc(c_silu, 1)
            dve.wait_ge(d_exp, 1)
            dve.tensor_scalar(d2[:], d1[:], 1.0, None, ALU.add).then_inc(d_step, 1)
            dve.wait_ge(d_step, 1)
            dve.reciprocal(sg[:], d2[:]).then_inc(d_step, 1)
            dve.wait_ge(d_step, 2)
            dve.tensor_scalar(arg[:, 0, :], sg[:], PI, None, ALU.mult)
            dve.tensor_scalar(arg[:, 1, :], sg[:], -PI, PI / 2, ALU.mult, ALU.add).then_inc(d_step, 1)
            dve.wait_ge(rstd_ready, 1)
            for n in range(B * TILES):
                dve.tensor_scalar(xn[:, n, :], x[:, n, :], mv[:, n, 0:1], rstd[:, n:n + 1],
                                  ALU.subtract, ALU.mult).then_inc(normed, 1)
            dve.wait_ge(mod_mm, 1)
            mp = banks[7][:, 0:12].rearrange("p (k b) -> p k b", b=B)
            dve.tensor_copy(a.mod[:], mp).then_inc(mod_copied, 1)
            dve.wait_ge(mod_copied, 1)
            for k, o in enumerate((1, 4)):
                dve.tensor_scalar(a.mod[:, o, :], a.mod[:, o, :], 1.0, None, ALU.add)
            for k, o in enumerate((2, 5)):
                dve.tensor_scalar(gsg[:, k, :], a.mod[:, o, :], 0.0, 2.0, ALU.is_ge, ALU.mult)
                dve.scalar_tensor_tensor(out=gab[:, k, :], in0=a.mod[:, o, :], scalar=-1.0, in1=a.mod[:, o, :],
                                         op0=ALU.mult, op1=ALU.max).then_inc(mod_gate, 1)
            dve.wait_ge(mod_gate, 2)
            dve.tensor_scalar(gab[:], gab[:], 0.25, None, ALU.max).then_inc(mod_gate, 1)
            dve.wait_ge(mod_gate, 3)
            for k, o in enumerate((2, 5)):
                last = dve.scalar_tensor_tensor(out=a.mod[:, o, :], in0=gsg[:, k, :], scalar=-1.0, in1=gab[:, k, :],
                                                op0=ALU.add, op1=ALU.mult)
            last.then_inc(mod_ready, 1)
            dve.wait_ge(d_sin, 1)
            dve.scalar_tensor_tensor(out=sind[:], in0=sn[:, 0, :], scalar=-2.0, in1=sn[:, 1, :],
                                     op0=ALU.mult, op1=ALU.mult)
            dve.scalar_tensor_tensor(out=d1[:], in0=sn[:, 0, :], scalar=-2.0, in1=sn[:, 0, :],
                                     op0=ALU.mult, op1=ALU.mult).then_inc(tab_step, 1)
            dve.wait_ge(tab_step, 1)
            dve.tensor_scalar(cosd[:], d1[:], 1.0, None, ALU.add).then_inc(tab_step, 1)
            dve.wait_ge(tab_step, 2)
            for k in range(2):
                dve.tensor_scalar(a.tabs[64:128, k, :], ropet[64:128, 2 * k, :], cosd[64:128, 32:33], None,
                                  ALU.mult).then_inc(tab_step, 1)
            dve.tensor_tensor(rtmp[:], rankt[:, 0:4:2, :], cosd[:, 0:32].unsqueeze(1).broadcast_to([P, 2, ROPE]), ALU.mult)
            dve.tensor_tensor(a.rankCS[:], rankt[:, 1:4:2, :], sind[:, 0:32].unsqueeze(1).broadcast_to([P, 2, ROPE]),
                              ALU.mult).then_inc(tab_step, 1)
            dve.wait_ge(tab_step, 5)
            for k in range(2):
                dve.scalar_tensor_tensor(out=a.tabs[64:128, k, :], in0=ropet[64:128, 2 * k + 1, :],
                                         scalar=sind[64:128, 32:33], in1=a.tabs[64:128, k, :],
                                         op0=ALU.mult, op1=ALU.add)
            dve.tensor_tensor(a.rankCS[:], a.rankCS[:], rtmp[:], ALU.add).then_inc(tabs_ready, 1)
            dve.wait_ge(fused, 1)
            for k in range(2):
                dve.tensor_copy(a.WQ[:, k:H:2, 0:CKV], banks[4 - k][0:CQ, 0:128].rearrange("p (h c) -> p h c", h=4)
                                ).then_inc(fused_copied, 1)
                dve.tensor_copy(a.Wvo[:, k:H:2, :], banks[5 + k][0:CKV, :].rearrange("p (h d) -> p h d", h=4)
                                ).then_inc(fused_copied, 1)
            kh = a.khT[:].rearrange("p b t -> p (b t)")
            dve.wait_ge(tabs_ready, 1)
            for q in range(4):
                sl = slice(q * 512, (q + 1) * 512)
                dve.wait_ge(kv_ln, q + 1)
                dve.scalar_tensor_tensor(out=kex[64:128, sl], in0=banks[q][64:128, :], scalar=0.0, in1=kab[64:128, sl],
                                         op0=ALU.max, op1=ALU.add).then_inc(kv_soft, 1)
                dve.wait_ge(kv_soft, q + 1)
                p0 = (q % 2) * 512
                dve.tensor_tensor(kh[64:128, sl], kex[64:128, sl], a.tabs[64:128, 0, p0:p0 + 512], ALU.mult).then_inc(kv_rot, 1)
            dve.wait_ge(ft_ln, 1)
            for k in range(2):
                fv = banks[4 + k][:].rearrange("p (n f) -> p n f", f=64)
                last = dve.scalar_tensor_tensor(out=F[:, 8 * k:8 * k + 8, CKV:64], in0=fv[:, :, CKV:64], scalar=0.0,
                                                in1=fab[:, 8 * k:8 * k + 8, :], op0=ALU.max, op1=ALU.add)
            last.then_inc(ft_c, 1)
            dve.wait_ge(ft_c, 1)
            dve.tensor_copy(a.feat[:, :, 0, :], F[:]).then_inc(ft_split, 1)
            dve.wait_ge(ft_split, 1)
            dve.tensor_tensor(F2[:], F[:], a.feat[:, :, 0, :], ALU.subtract).then_inc(ft_split, 1)
            dve.wait_ge(ft_split, 2)
            dve.tensor_copy(a.feat[:, :, 1, :], F2[:]).then_inc(ft_split, 1)
            dve.wait_ge(ft_split, 3)
            dve.tensor_tensor(a.feat[:, :, 2, :], F2[:], a.feat[:, :, 1, :], ALU.subtract).then_inc(ft_split, 1)


N_C_POOL = 1 + 7 + 7


class Tally:

    def __init__(self, sem, per, credit=0, before=0):
        self.sem, self.per, self.credit, self.before = sem, per, credit, before

    def wait(self, eng, b, n):
        assert n + self.credit > 0
        eng.wait_ge(self.sem, b * self.per + (n + self.credit + self.before * self.per))


def key_blocks(i):
    n = P * i + P - LW
    return [(o, min(512, n - o)) for o in range(0, n, 512)]


EARLY = 5


def misc_plan():
    plan = []

    def index(i):
        plan.append(("qi", i))
        scores(i)

    def scores(i):
        for kb in range(len(key_blocks(i))):
            for h in range(IDX_HEADS):
                plan.append(("score", i, kb, h))

    def halves(i):
        plan.extend([("half", i, 0), ("half", i, 1)])

    index(0)
    plan.extend([("query", 0, 0), ("query", 0, 1)])
    halves(0)
    index(1)
    for s in range(PAIRS + 2):
        i = s // PPT
        if s % PPT == 3 and i + 2 < TILES:
            scores(i + 2)
        if s % PPT == 3 and i + 1 < TILES:
            halves(i + 1)
        if s % PPT == 2 and i + 2 < TILES:
            plan.append(("qi", i + 2))
        if s % PPT in (1, 2) and i + 1 < TILES:
            plan.append(("query", i + 1, s % PPT - 1))
        if s % PPT == 1 and i >= 1:
            plan.append(("attn", i - 1))
    return {what: n for n, what in enumerate(plan)}


def attention_block(nc, a):
    use = misc_plan()
    assert len(use) % 2 == 0
    pick_ops = {i: 3 * len(key_blocks(i)) + 1 + 3 * TOP_ROUNDS - 1 + (3 if i == 0 else 1) for i in range(TILES)}

    with ExitStack() as ctx:
        def sb(name, shape, dt=F32):
            return ctx.enter_context(nc.sbuf_tensor(name, list(shape), dt))

        def tally(name, per, credit=0):
            return Tally(ctx.enter_context(nc.semaphore(name)), per, credit)

        qi = sb("qi", [P, IDX_HEADS, P])
        relu = sb("relu", [P, 2, 512])
        isum = sb("isum", [P, L])
        vals = sb("vals", [P, 8])
        idx16 = sb("idx16", [P, NSEL], U16)
        idxf = sb("idxf", [P, NSEL])
        idxh = sb("idxh", [P, 2, NSEL], F16)
        idxb = sb("idxb", [P, 2, P * NSEL], F16)
        featb = sb("featb", [P, TILES, 3, 64], BF16)
        oh = sb("oh", [P, 2, TILES, PAIR * NSEL], BF16)
        qsp = sb("qsp", [P, P, H // 2])
        qex = sb("qex", [P, 512])
        QR = sb("QR", [P, 2, P * H])
        QW = sb("QW", [P, P * H])
        QA = sb("QA", [P, 2, P * H])
        G = sb("G", [P, 4, GROUPS, 64])
        gA = sb("gA", [P, GROUPS, ROPE])
        gB = sb("gB", [P, GROUPS, ROPE])
        GT = sb("GT", [P, GROUPS // 2, P])
        Sm = sb("Sm", [P, 2, SCOLS])
        nmx = sb("nmx", [P, 2, 2])
        Z = sb("Z", [P, 2, 2])
        rz = sb("rz", [P, 2, 2])
        Pb = sb("Pb", [P, 2, 2, 256])
        PTb = sb("PTb", [P, 2, 256])
        cw = sb("cw", [WIN, 4, 2, CKV])
        OT = sb("OT", [CKV, 2, P * H])
        psG = [ctx.enter_context(nc.psum_tensor(f"psG{i}", [P, GROUPS, 64], F32)) for i in range(2)]
        psT = ctx.enter_context(nc.psum_tensor("psT", [P, GROUPS // 2, P], F32))
        psS = [ctx.enter_context(nc.psum_tensor(f"psS{i}", [P, 512], F32)) for i in range(2)]
        psPT = ctx.enter_context(nc.psum_tensor("psPT", [P, 2, 256], F32))
        psO = psT[:].rearrange("p n t -> p (n t)")
        psM = [ctx.enter_context(nc.psum_tensor(f"psM{i}", [P, 512], F32)) for i in range(2)]

        n_use = len(use)
        m_ready = tally("m_ready", n_use)
        m_free = [tally("m_free0", n_use // 2, 1), tally("m_free1", n_use // 2, 1)]
        picking = tally("picking", sum(pick_ops.values()))
        idx_stored = tally("idx_stored", 16 * TILES, 32)
        idx_spread = tally("idx_spread", 16 * TILES)
        oh_ready = tally("oh_ready", PAIRS, 8)
        gathered = tally("gathered", PAIRS, 2)
        g_copied = tally("g_copied", PAIRS, 2)
        g_step = tally("g_step", PAIRS)
        g_rot = tally("g_rot", PAIRS, 1)
        t_ready = tally("t_ready", PAIRS)
        gt_copied = tally("gt_copied", PAIRS, 1)
        s_ready = tally("s_ready", PAIRS, 1)
        s_read = tally("s_read", 2 * PAIRS, 16)
        p_exp = tally("p_exp", 2 * PAIRS, 2)
        rz_ready = tally("rz_ready", PAIRS)
        p_ready = tally("p_ready", 2 * PAIRS)
        pt_ready = tally("pt_ready", PAIRS, 2)
        pt_copied = tally("pt_copied", PAIRS, 1)
        cw_loaded = [tally(f"cw_loaded{n}", 32 * PAIRS // 4) for n in range(4)]
        pv_done = tally("pv_done", PAIRS, 4)
        o_copied = tally("o_copied", PAIRS, 2)
        q_abs = tally("q_abs", 2 * TILES)
        q_exp = tally("q_exp", 2 * TILES)
        q_ln = tally("q_ln", 2 * TILES)
        q_pass = tally("q_pass", 2 * TILES)
        q_turn = tally("q_turn", 2 * TILES)
        pe_passed = ctx.enter_context(nc.semaphore("pe_passed"))
        dve_passed = ctx.enter_context(nc.semaphore("dve_passed"))
        cleared = ctx.enter_context(nc.semaphore("cleared"))

        relu_user = [sum(pick_ops[j] for j in range(i)) + 3 * kb + h
                     for i in range(TILES) for kb in range(len(key_blocks(i))) for h in range(1, IDX_HEADS)]
        first_pick = {i: sum(pick_ops[j] for j in range(i)) for i in range(TILES + 1)}

        def hold(eng, passed):
            eng.sem_inc(passed, 1)

        def slot(g):
            return 2 * (g % 4) + g // 4

        def released(eng, b, what, back=0):
            k = use[what]
            m_free[k % 2].wait(eng, b, k // 2 + 1 - back * (n_use // 2))

        block = ctx.enter_context(nc.Block())

        @block.sync
        def _(sp):
            with sp.Fori(0, B) as b:
                def windows(m):
                    pv_done.wait(sp, b, m - 3)
                    for k in range(2):
                        w0 = 0 if m < 2 else PAIR * m + UNIT * k - LW
                        sp.dma_start(cw[:, m % 4, k, :], a.c_d[bass.ds(b * L + w0, WIN), :]).then_inc(cw_loaded[m % 4].sem, 16)

                def spread(i):
                    picking.wait(sp, b, first_pick[i + 1])
                    sp.dma_start(a.idx_d[b * TILES + i], idxh[:, i % 2, :]).then_inc(idx_stored.sem, 16)
                    idx_stored.wait(sp, b, 16 * (i + 1))
                    oh_ready.wait(sp, b, PPT * (i - 1))
                    sp.dma_start(idxb[:, i % 2, :], a.idx_d[b * TILES + i].rearrange("t j -> (t j)").partition_broadcast(P)
                                 ).then_inc(idx_spread.sem, 16)

                spread(0)
                for m in range(PAIRS):
                    windows(m)
                    if m % PPT == 2 and m // PPT + 1 < TILES:
                        spread(m // PPT + 1)

        @block.gpsimd
        def _(pool):
            for t in (m_free[0], m_free[1], idx_stored, oh_ready, gathered, g_copied, g_rot, gt_copied,
                      s_ready, s_read, p_exp, pt_ready, pt_copied, pv_done, o_copied):
                pool.sem_inc(t.sem, t.credit)
            CC = a.rankCS[:, 0:1, :].broadcast_to([P, GROUPS, ROPE])
            SS = a.rankCS[:, 1:2, :].broadcast_to([P, GROUPS, ROPE])
            with pool.Fori(0, B) as b:
                for m in range(PAIRS):
                    g = G[:, m % 4]
                    g_copied.wait(pool, b, m + 1)
                    g_rot.wait(pool, b, m)
                    pool.tensor_tensor(gA[:], g[:, :, CKV:64], CC, ALU.mult)
                    pool.tensor_tensor(gB[:, :, 0:HALF], g[:, :, CKV + HALF:64], SS[:, :, 0:HALF], ALU.mult)
                    pool.tensor_tensor(gB[:, :, HALF:ROPE], g[:, :, CKV:CKV + HALF], SS[:, :, HALF:ROPE],
                                       ALU.mult).then_inc(g_step.sem, 1)
                    g_step.wait(pool, b, m + 1)
                    pool.tensor_tensor(g[:, :, CKV:64], gA[:], gB[:], ALU.add).then_inc(g_rot.sem, 1)

        @block.tensor
        def _(pe):
            pe.wait_ge(cleared, 1)
            with pe.Fori(0, B) as b:
                def bank(what):
                    k = use[what]
                    m_free[k % 2].wait(pe, b, k // 2)
                    return psM[k % 2]

                def index_queries(i):
                    M = bank(("qi", i))
                    for n in range(2):
                        mm = pe.matmul(M[:, n * P:(n + 1) * P], a.wiq[:, n * P:(n + 1) * P],
                                       a.hT[:, b, i * P:(i + 1) * P], start=True, stop=True)
                    mm.then_inc(m_ready.sem, 1)

                def index_scores(i, kb, h):
                    o, n = key_blocks(i)[kb]
                    if kb == 0 and h == 0:
                        released(pe, b, ("qi", i))
                    M = bank(("score", i, kb, h))
                    pe.matmul(M[:, 0:n], qi[:, h, :], a.kiT[:, b, o:o + n],
                              start=True, stop=True).then_inc(m_ready.sem, 1)

                def queries(i, x):
                    M = bank(("query", i, x))
                    for h in range(4):
                        mm = pe.matmul(M[:, h * P:(h + 1) * P], a.WQ[:, 4 * x + h, :],
                                       a.cqT[:, b, i * P:(i + 1) * P], start=True, stop=True)
                    mm.then_inc(m_ready.sem, 1)

                def halves(i):
                    for x in range(2):
                        M = bank(("half", i, x))
                        q_turn.wait(pe, b, 2 * i + 2)
                        pe.matmul(M[:], a.selm[:, 1, :], QW[:, x * 512:(x + 1) * 512],
                                  start=True, stop=True).then_inc(m_ready.sem, 1)

                def attn_out(i):
                    M = bank(("attn", i))
                    o_copied.wait(pe, b, PPT * (i + 1))
                    for h in range(H):
                        mm = pe.matmul(M[:, 0:P], a.Wvo[:, h, :], OT[:, i % 2, h:P * H:H],
                                       start=(h == 0), stop=(h == H - 1))
                    mm.then_inc(m_ready.sem, 1)

                def gather(m, groups, scores):
                    if groups[0] == 0:
                        oh_ready.wait(pe, b, m + 1)
                        g_copied.wait(pe, b, m - 1)
                    nch = m // PPT + 1
                    for g in groups:
                        for c in range(nch):
                            for part in range(3):
                                mm = pe.matmul(psG[m % 2][:, slot(g), :], oh[:, m % 2, c, g * P:(g + 1) * P],
                                               featb[:, c, part, :],
                                               start=(c == 0 and part == 0), stop=(c == nch - 1 and part == 2))
                        if g == GROUPS - 1:
                            mm.then_inc(gathered.sem, 1)
                        for what in scores[2 * g:2 * g + 2]:
                            index_scores(*what)

                def turn_keys(m):
                    g_rot.wait(pe, b, m + 1)
                    gt_copied.wait(pe, b, m)
                    o_copied.wait(pe, b, m - 1)
                    for n in range(GROUPS // 2):
                        mm = pe.transpose(psT[:, n, :], G[:, m % 4, 2 * n:2 * n + 2, :].rearrange("p g f -> p (g f)"), a.ident[:])
                    mm.then_inc(t_ready.sem, 1)

                def local_scores(m):
                    i, p = m // PPT, m % PPT
                    q_pass.wait(pe, b, 2 * i + 2)
                    s_read.wait(pe, b, 2 * m)
                    for k in range(2):
                        w0 = 0 if m < 2 else PAIR * m + UNIT * k - LW
                        c0 = (2 * p + k) * P
                        pe.matmul(psS[k][:, P:SCOLS], QR[:, i % 2, c0:c0 + P], a.khT[:, b, w0:w0 + WIN],
                                  start=True, stop=True)

                def turn_probs(m):
                    p_ready.wait(pe, b, 2 * m + 2)
                    pt_copied.wait(pe, b, m)
                    for k in range(2):
                        for n in range(2):
                            mm = pe.transpose(psPT[:, k, n * P:(n + 1) * P], Pb[:, m % 2, k, n * P:(n + 1) * P], a.ident[:])
                    mm.then_inc(pt_ready.sem, 1)

                def picked_scores(m):
                    i, p = m // PPT, m % PPT
                    for x in range(2):
                        released(pe, b, ("half", i, x))
                    gt_copied.wait(pe, b, m + 1)
                    hold(pe, pe_passed)
                    for g in range(GROUPS):
                        r = 64 * (g // 4)
                        c0 = p * 256 + g * 32
                        mm = pe.matmul(psS[g // 4][32 * (g % 4):32 * (g % 4) + 32, 0:P], QA[r:r + 64, i % 2, c0:c0 + 32],
                                       GT[r:r + 64, g % 4, :], start=True, stop=True)
                    mm.then_inc(s_ready.sem, 1)

                def values(m):
                    pt_copied.wait(pe, b, m + 1)
                    cw_loaded[m % 4].wait(pe, b, 32 * (m // 4 + 1))
                    o_copied.wait(pe, b, m)
                    for k in range(2):
                        pe.matmul(psO[0:CKV, k * P:(k + 1) * P], cw[:, m % 4, k, :], PTb[0:WIN, k, P:256],
                                  start=True, stop=False, skip_group_check=True)
                        for g in range(4):
                            mm = pe.matmul(psO[0:CKV, k * P + 32 * g:k * P + 32 * g + 32], G[:, m % 4, slot(4 * k + g), 0:CKV],
                                           PTb[:, k, 32 * g:32 * g + 32], start=False, stop=(g == 3),
                                           skip_group_check=True)
                    mm.then_inc(pv_done.sem, 1)

                def all_scores(i):
                    return [(i, kb, h) for kb in range(len(key_blocks(i))) for h in range(IDX_HEADS)]

                index_queries(0)
                for what in all_scores(0):
                    index_scores(*what)
                queries(0, 0)
                queries(0, 1)
                halves(0)
                index_queries(1)
                for what in all_scores(1):
                    index_scores(*what)
                for s in range(PAIRS + 2):
                    i = s // PPT
                    scores = all_scores(i + 2) if s % PPT == 3 and i + 2 < TILES else []
                    if s < PAIRS:
                        gather(s, range(0, EARLY), scores)
                    if 1 <= s <= PAIRS:
                        turn_keys(s - 1)
                        local_scores(s - 1)
                    if s >= 2:
                        turn_probs(s - 2)
                    if s < PAIRS:
                        gather(s, range(EARLY, GROUPS), [])
                    if s % PPT == 3 and i + 1 < TILES:
                        halves(i + 1)
                    if 1 <= s <= PAIRS:
                        picked_scores(s - 1)
                    if s >= 2:
                        values(s - 2)
                    if s % PPT == 2 and i + 2 < TILES:
                        index_queries(i + 2)
                    if s % PPT in (1, 2) and i + 1 < TILES:
                        queries(i + 1, s % PPT - 1)
                    if s % PPT == 1 and i >= 1:
                        attn_out(i - 1)

        @block.scalar
        def _(act):
            act.preload_act_table_set("natural_log_exp_and_others")
            act.wait_ge(cleared, 1)
            with act.Fori(0, B) as b:
                def index_queries(i):
                    k = use[("qi", i)]
                    m_ready.wait(act, b, k + 1)
                    q2 = psM[k % 2][:, 0:256].rearrange("p (n t) -> p n t", n=2)
                    act.copy(qi[0:64, 0:IDX_HEADS:2, :], q2[0:64])
                    act.copy(qi[64:128, 1:IDX_HEADS:2, :], q2[64:128]).then_inc(m_free[k % 2].sem, 1)

                def index_scores(i):
                    n_before = 3 * sum(len(key_blocks(j)) for j in range(i))
                    for kb, (o, n) in enumerate(key_blocks(i)):
                        for h in range(1, IDX_HEADS):
                            k = use[("score", i, kb, h)]
                            r = n_before + 3 * kb + h - 1
                            m_ready.wait(act, b, k + 1)
                            if r >= n_before + 2 or i >= 1:
                                picking.wait(act, b, relu_user[r - 2])
                            act.activation(relu[:, r % 2, 0:n], psM[k % 2][:, 0:n], ACT.Relu).then_inc(m_free[k % 2].sem, 1)

                def queries(i, x):
                    k = use[("query", i, x)]
                    n = 2 * i + x
                    m_ready.wait(act, b, k + 1)
                    s_read.wait(act, b, 2 * PPT * (i - 1))
                    q4 = psM[k % 2][0:CKV, :].rearrange("p (h t) -> p h t", h=4)
                    qr = QR[0:CKV, i % 2, :].rearrange("p (t h) -> p h t", h=H)[:, 4 * x:4 * x + 4, :]
                    act.copy(qr, q4)
                    qw = QW[0:CKV, :].rearrange("p (t h) -> p h t", h=H)[:, 4 * x:4 * x + 4, :]
                    act.copy(qw, q4)
                    if n:
                        released(act, b, ("query", (n - 1) // 2, (n - 1) % 2))
                    act.activation(qex[64:128, :], psM[k % 2][64:128, :], ACT.Abs).then_inc(q_abs.sem, 1)
                    q_abs.wait(act, b, n + 1)
                    act.activation(qex[64:128, :], qex[64:128, :], ACT.Exp, scale=-1.0).then_inc(q_exp.sem, 1)
                    q_exp.wait(act, b, n + 1)
                    act.activation(qex[64:128, :], qex[64:128, :], ACT.Ln, bias=1.0).then_inc(q_ln.sem, 1)

                def halves(i):
                    for x in range(2):
                        k = use[("half", i, x)]
                        m_ready.wait(act, b, k + 1)
                        s_read.wait(act, b, 2 * PPT * (i - 1))
                        act.copy(QA[:, i % 2, x * 512:(x + 1) * 512], psM[k % 2][:]).then_inc(m_free[k % 2].sem, 1)

                def copy_rows(m):
                    gathered.wait(act, b, m + 1)
                    pv_done.wait(act, b, m - 3)
                    act.copy(G[:, m % 4], psG[m % 2][:]).then_inc(g_copied.sem, 1)

                def copy_turned(m):
                    t_ready.wait(act, b, m + 1)
                    s_ready.wait(act, b, m)
                    act.copy(GT[:], psT[:]).then_inc(gt_copied.sem, 1)

                def copy_probs(m):
                    pt_ready.wait(act, b, m + 1)
                    pv_done.wait(act, b, m)
                    act.copy(PTb[:], psPT[:]).then_inc(pt_copied.sem, 1)

                def probs(m):
                    for k in range(2):
                        s_read.wait(act, b, 2 * m + k + 1)
                        pt_ready.wait(act, b, m - 1)
                        act.activation(Pb[:, m % 2, k, 0:SCOLS], Sm[:, k, :], ACT.Exp, scale=-1.0,
                                       bias=nmx[:, m % 2, k:k + 1], accum_out=Z[:, m % 2, k:k + 1]).then_inc(p_exp.sem, 1)

                def copy_out(m):
                    i, p = m // PPT, m % PPT
                    pv_done.wait(act, b, m + 1)
                    if i >= 2:
                        released(act, b, ("attn", i - 2))
                    else:
                        released(act, b, ("attn", i + TILES - 2), 1)
                    act.copy(OT[:, i % 2, p * 256:(p + 1) * 256], psO[0:CKV, 0:256]).then_inc(o_copied.sem, 1)

                index_queries(0)
                index_scores(0)
                queries(0, 0)
                queries(0, 1)
                halves(0)
                index_queries(1)
                index_scores(1)
                for s in range(PAIRS + 2):
                    i = s // PPT
                    if s % PPT == 3 and i + 2 < TILES:
                        index_scores(i + 2)
                    if 1 <= s <= PAIRS:
                        copy_turned(s - 1)
                    if s >= 2:
                        copy_probs(s - 2)
                    if s < PAIRS:
                        copy_rows(s)
                    if s % PPT == 3 and i + 1 < TILES:
                        halves(i + 1)
                    if 1 <= s <= PAIRS:
                        probs(s - 1)
                    if s >= 2:
                        copy_out(s - 2)
                    if s % PPT == 2 and i + 2 < TILES:
                        index_queries(i + 2)
                    if s % PPT in (1, 2) and i + 1 < TILES:
                        queries(i + 1, s % PPT - 1)

        @block.vector
        def _(dve):
            dve.memset(QR[32:64], 0.0)
            dve.memset(QW[32:64], 0.0)
            dve.memset(qi[:], 0.0)
            dve.memset(Pb[:, :, :, SCOLS:256], 0.0).then_inc(cleared, 1)
            with dve.Fori(0, B) as b:
                step = [0]

                def pick(ins):
                    ins.then_inc(picking.sem, 1)
                    step[0] += 1
                    picking.wait(dve, b, step[0])
                    hold(dve, dve_passed)

                def index(i):
                    n_before = 3 * sum(len(key_blocks(j)) for j in range(i))
                    for kb, (o, n) in enumerate(key_blocks(i)):
                        k = use[("score", i, kb, 0)]
                        m_ready.wait(dve, b, k + 1)
                        dve.tensor_scalar(isum[:, o:o + n], psM[k % 2][:, 0:n], 0.0, a.wix[:, 0:1], ALU.max,
                                          ALU.mult).then_inc(m_free[k % 2].sem, 1)
                        released(dve, b, ("score", i, kb, 0))
                        for h in range(1, IDX_HEADS):
                            r = n_before + 3 * kb + h - 1
                            released(dve, b, ("score", i, kb, h))
                            pick(dve.scalar_tensor_tensor(out=isum[:, o:o + n], in0=relu[:, r % 2, 0:n],
                                                          scalar=a.wix[:, h:h + 1], in1=isum[:, o:o + n],
                                                          op0=ALU.mult, op1=ALU.add))
                    lo = max(0, P * i - LW)
                    hi = P * i + P - LW
                    pick(dve.tensor_tensor(isum[:, lo:hi], isum[:, lo:hi], a.imask[:, P - (hi - lo):P], ALU.add))

                def top_values(i, r):
                    n = P * i + P - LW
                    pick(dve.max(vals[:], isum[:, 0:n]))

                def top_places(i, r):
                    n = P * i + P - LW
                    pick(dve.max_index(idx16[:, 8 * r:8 * r + 8], vals[:], isum[:, 0:n]))
                    if r < TOP_ROUNDS - 1:
                        pick(dve.match_replace(isum[:, 0:n], vals[:], isum[:, 0:n], NEGMAX))
                        return
                    idx_stored.wait(dve, b, 16 * (i - 1))
                    if i == 0:
                        pick(dve.tensor_copy(idxf[:], idx16[:]))
                        pick(dve.tensor_tensor(idxf[:], idxf[:], a.future[:, 0, :], ALU.mult))
                        pick(dve.tensor_tensor(idxh[:, i % 2, :], idxf[:], a.future[:, 1, :], ALU.add))
                    else:
                        pick(dve.tensor_copy(idxh[:, i % 2, :], idx16[:]))

                def queries(i, x):
                    k = use[("query", i, x)]
                    n = 2 * i + x
                    q_ln.wait(dve, b, n + 1)
                    if n:
                        q_turn.wait(dve, b, n)
                    sp_th = qsp[64:128].rearrange("p t h -> p h t")
                    dve.scalar_tensor_tensor(out=sp_th, in0=psM[k % 2][64:128, :].rearrange("p (h t) -> p h t", h=4),
                                             scalar=0.0, in1=qex[64:128, :].rearrange("p (h t) -> p h t", h=4),
                                             op0=ALU.max, op1=ALU.add).then_inc(m_free[k % 2].sem, 1)
                    released(dve, b, ("query", i, x))
                    t0 = i * P
                    tr = [a.tabs[64:128, j, t0:t0 + P].unsqueeze(2).broadcast_to([64, P, 4]) for j in range(2)]
                    qr = QR[64:128, i % 2, :].rearrange("p (t h) -> p t h", h=H)[:, :, 4 * x:4 * x + 4]
                    qw = QW[64:128, :].rearrange("p (t h) -> p t h", h=H)[:, :, 4 * x:4 * x + 4]
                    dve.tensor_tensor(qr, qsp[64:128], tr[1], ALU.mult).then_inc(q_pass.sem, 1)
                    dve.tensor_tensor(qw, qsp[64:128], tr[0], ALU.mult).then_inc(q_turn.sem, 1)

                def onehot(m):
                    i, p = m // PPT, m % PPT
                    idx_spread.wait(dve, b, 16 * (i + 1))
                    gathered.wait(dve, b, m - 1)
                    for c in range(i + 1):
                        last = dve.tensor_scalar(oh[:, m % 2, c, :], idxb[:, i % 2, p * 1024:(p + 1) * 1024],
                                                 a.keys[:, c:c + 1], None, ALU.is_equal)
                    last.then_inc(oh_ready.sem, 1)

                def masked_max(m):
                    s_ready.wait(dve, b, m + 1)
                    p_exp.wait(dve, b, 2 * m)
                    hold(dve, dve_passed)
                    for k in range(2):
                        dve.tensor_tensor_reduce(out=Sm[:, k, :], in0=psS[k][:, 0:SCOLS], in1=a.umask[:, 0 if m < 2 else 1, :],
                                                 scale=-ATTN_SCALE, scalar=-NEGMAX, op0=ALU.add, op1=ALU.min,
                                                 accum_out=nmx[:, m % 2, k:k + 1]).then_inc(s_read.sem, 1)

                def normalize(m):
                    p_exp.wait(dve, b, 2 * m + 2)
                    dve.reciprocal(rz[:, m % 2, :], Z[:, m % 2, :]).then_inc(rz_ready.sem, 1)
                    rz_ready.wait(dve, b, m + 1)
                    for k in range(2):
                        dve.tensor_scalar(Pb[:, m % 2, k, 0:SCOLS], Pb[:, m % 2, k, 0:SCOLS], rz[:, m % 2, k:k + 1], None,
                                          ALU.mult).then_inc(p_ready.sem, 1)

                def residual(i):
                    k = use[("attn", i)]
                    m_ready.wait(dve, b, k + 1)
                    xs = a.x1T[:, b, i * P:(i + 1) * P]
                    dve.scalar_tensor_tensor(out=xs, in0=psM[k % 2][:, 0:P], scalar=a.mod[:, 2, bass.ds(b, 1)], in1=xs,
                                             op0=ALU.mult, op1=ALU.add).then_inc(m_free[k % 2].sem, 1)

                def top_round(i, r):
                    top_values(i, r)
                    top_places(i, r)

                index(0)
                for r in range(TOP_ROUNDS):
                    top_round(0, r)
                queries(0, 0)
                queries(0, 1)
                index(1)
                gathered.wait(dve, b, 0)
                dve.tensor_copy(featb[:], a.feat[:, bass.ds(b * TILES, TILES), :, :])
                onehot(0)
                top_round(1, 0)
                for s in range(PAIRS + 2):
                    i = s // PPT
                    j, r = (s + 1) // PPT + 1, (s + 1) % PPT
                    if s % PPT == 3 and i + 2 < TILES:
                        index(i + 2)
                    if s + 1 < PAIRS:
                        onehot(s + 1)
                    if s % PPT == 2 and i >= 1:
                        residual(i - 1)
                    if 1 <= s <= PAIRS:
                        masked_max(s - 1)
                    if j < TILES:
                        top_values(j, r)
                    if 1 <= s <= PAIRS:
                        normalize(s - 1)
                    if j < TILES:
                        top_places(j, r)
                    if s % PPT in (1, 2) and i + 1 < TILES:
                        queries(i + 1, s % PPT - 1)
                if (PAIRS + 1) % PPT == 1:
                    residual(TILES - 1)
                assert step[0] == picking.per, (step[0], picking.per)


def stack_blocks(nc, top, ins, consts, out, ident, ones, mod, x1T, wqkv, wo, w1, w2, fvec):
    def sb(name, shape, dt=F32):
        return top.enter_context(nc.sbuf_tensor(name, list(shape), dt))

    X = sb("X", [P, B, L + 1])
    Y = sb("Y", [P, B, L + 1])
    xpos = sb("xpos", [P, TILES, 4, DH])
    xtab = sb("xtab", [P, DEPTH, TILES, 4, DH])
    qks = sb("qks", [P, DEPTH, 2, DH])
    wmask = sb("wmask", [P, 2, P])
    eps = sb("eps", [P, 1])

    norm_block(nc, ins, consts, ones, mod, x1T, X, Y, xpos, xtab, qks, wmask, eps)
    sems = {}

    def sem(name):
        if name not in sems:
            sems[name] = top.enter_context(nc.semaphore(name))
        return sems[name]

    for l in range(DEPTH):
        window_block(nc, l, sem, ident, X, Y, xtab, wmask, wqkv, wo)
        mlp_block(nc, l, sem, ones, X, Y, w1, w2, fvec, eps)
    final_block(nc, ident, mod, x1T, X, out)


def norm_block(nc, ins, consts, ones, mod, x1T, X, Y, xpos, xtab, qks, wmask, eps):
    with ExitStack() as ctx:
        def sb(name, shape, dt=F32):
            return ctx.enter_context(nc.sbuf_tensor(name, list(shape), dt))

        def sem(name):
            return ctx.enter_context(nc.semaphore(name))

        NQ = B * L // 512
        zc = sb("zc", [P, NQ, 512])
        sq = sb("sq", [P, NQ, 512])
        rs = sb("rs", [P, NQ, 512])
        ps = [ctx.enter_context(nc.psum_tensor(f"stat{i}", [P, 512], F32)) for i in range(2 * NQ)]
        loaded, mean_done, centred, squared, var_done = (
            sem("loaded"), sem("mean_done"), sem("centred"), sem("squared"), sem("var_done"))
        logged, rstd_done, scaled, folded, eps_set = (
            sem("logged"), sem("rstd_done"), sem("scaled"), sem("folded"), sem("eps_set"))
        x1 = x1T[:].rearrange("p b t -> p (b t)")
        block = ctx.enter_context(nc.Block())

        @block.sync
        def _(sp):
            sp.dma_start(xpos[:], consts["xpos"]).then_inc(loaded, 16)
            sp.dma_start(wmask[:], consts["wmask"]).then_inc(loaded, 16)
            for l in range(DEPTH):
                for k, name in enumerate(("L0_ffn_q_scale", "L0_ffn_k_scale")):
                    sp.dma_start(qks[:, l, k, :], ins[name][l].partition_broadcast(P)).then_inc(loaded, 16)
            sp.wait_ge(loaded, 16 * (2 + 2 * DEPTH))

        @block.tensor
        def _(pe):
            for q in range(NQ):
                pe.matmul(ps[q][:], ones[:], x1[:, q * 512:(q + 1) * 512], start=True, stop=True).then_inc(mean_done, 1)
            for q in range(NQ):
                pe.wait_ge(squared, q + 1)
                pe.matmul(ps[NQ + q][:], ones[:], sq[:, q, :], start=True, stop=True).then_inc(var_done, 1)

        @block.scalar
        def _(act):
            act.preload_act_table_set("natural_log_exp_and_others")
            for q in range(NQ):
                act.wait_ge(centred, q + 1)
                act.activation(sq[:, q, :], zc[:, q, :], ACT.Square).then_inc(squared, 1)
            act.wait_ge(eps_set, 1)
            for q in range(NQ):
                act.wait_ge(var_done, q + 1)
                act.activation(rs[:, q, :], ps[NQ + q][:], ACT.Ln, bias=eps[:, 0:1]).then_inc(logged, 1)
            for q in range(NQ):
                act.wait_ge(logged, q + 1)
                act.activation(rs[:, q, :], rs[:, q, :], ACT.Exp, scale=-0.5).then_inc(rstd_done, 1)

        @block.vector
        def _(dve):
            dve.memset(eps[:], LN_EPS).then_inc(eps_set, 1)
            dve.memset(X[:, :, 0:1], 0.0)
            dve.memset(Y[:, :, 0:1], 0.0)
            for q in range(NQ):
                dve.wait_ge(mean_done, q + 1)
                dve.tensor_tensor(zc[:, q, :], x1[:, q * 512:(q + 1) * 512], ps[q][:], ALU.subtract).then_inc(centred, 1)
            dve.wait_ge(loaded, 16 * (2 + 2 * DEPTH))
            for l in range(DEPTH):
                for k in range(2):
                    dve.tensor_tensor(xtab[:, l, :, k, :], xpos[:, :, k, :],
                                      qks[:, l, k:k + 1, :].broadcast_to([P, TILES, DH]), ALU.mult)
                    for o in (0, 32):
                        dve.tensor_tensor(xtab[:, l, :, 2 + k, o:o + 32], xpos[:, :, 2 + k, o:o + 32],
                                          qks[:, l, k:k + 1, 32 - o:64 - o].broadcast_to([P, TILES, 32]), ALU.mult)
            for q in range(NQ):
                b, o = q // 2, 1 + 512 * (q % 2)
                dve.wait_ge(rstd_done, q + 1)
                dve.tensor_tensor(zc[:, q, :], zc[:, q, :], rs[:, q, :], ALU.mult).then_inc(scaled, 1)
                dve.wait_ge(scaled, q + 1)
                dve.tensor_scalar(X[:, b, o:o + 512], zc[:, q, :], mod[:, 4, b:b + 1], mod[:, 3, b:b + 1],
                                  ALU.mult, ALU.add)


def window_block(nc, l, sem, ident, X, Y, xtab, wmask, wqkv, wo):
    tag = f"_{l}"
    with ExitStack() as ctx:
        def sb(name, shape, dt=F32):
            return ctx.enter_context(nc.sbuf_tensor(name + tag, list(shape), dt))

        def tally(name, per, credit=0):
            return Tally(sem(name), per, credit, l * B)

        def psum(name, shape):
            return ctx.enter_context(nc.psum_tensor(name + tag, list(shape), F32))

        hs = sb("hs", [P, 2, P])
        sq = sb("sq", [P, 2, INNER])
        rA = sb("rA", [P, 2, INNER])
        rB = sb("rB", [P, 2, INNER])
        ss = sb("ss", [P, 2, 2 * H])
        sg = sb("sg", [P, 2 * H])
        rn = sb("rn", [P, 2, 2 * H])
        mhalf = sb("mhalf", [P, 2 * H])
        qk = sb("qk", [P, 2, 2 * INNER])
        qT = sb("qT", [P, 2, 4, P])
        kT = sb("kT", [P, 2, 4, WINDOW + P])
        vfull = sb("vfull", [P, 4, INNER])
        vhalf = sb("vhalf", [P, 4, INNER])
        Sm = sb("Sm", [P, H, P])
        nmx = sb("nmx", [P, 2, H])
        Z = sb("Z", [P, 2, H])
        rz = sb("rz", [P, 2, H])
        Pm = sb("Pm", [P, 2, H, P])
        PT = sb("PT", [P, H, P])
        OT = sb("OT", [P, 4, P])
        psQ = [psum(f"psQ{k}", [P, INNER]) for k in range(2)]
        psV = psum("psV", [P, INNER])
        psT = [psum(f"psTT{k}", [P, 4, P]) for k in range(2)]
        psS = [psum(f"psSS{k}", [P, 4, P]) for k in range(2)]
        psO = psum("psOO", [P, 4, P])

        n = TILES
        staged = tally("staged", n)
        q_ready = tally("q_ready", n, 2)
        q_squared = tally("q_squared", 2 * n, 2)
        q_rotated = tally("q_rotated", n, 1)
        q_summed = tally("q_summed", n)
        sq_read = tally("sq_read", n, 1)
        ss_safe = tally("ss_safe", n)
        rn_ready = tally("rn_ready", n)
        qk_ready = tally("qk_ready", n, 1)
        v_ready = tally("v_ready", 2 * n)
        v_free = tally("v_free", 2 * n, 1)
        t_ready = tally("t_ready", 2 * n)
        t_free = tally("t_free", 2 * n, 1)
        k_prev = tally("k_prev", n)
        s_ready = tally("s_ready2", n, 2)
        s_read = tally("s_read2", n * H, H)
        p_exp = tally("p_exp2", n * H, H)
        rz_ready = tally("rz_ready2", n)
        p_ready = tally("p_ready2", n)
        o_ready = tally("o_ready", n, 4)
        o_copied = tally("o_copied2", n, 1)
        cleared = sem("cleared2")
        pe_passed = sem("pe_passed2")
        dve_passed = sem("dve_passed2")
        pool_passed = sem("pool_passed2")

        v_use = {w: k for k, w in enumerate([w for s in range(n + 2) for w in
                                             ([("v", s)] if s < n else []) + ([("y", s - 2)] if s >= 2 else [])])}
        t_use = {w: k for k, w in enumerate([w for s in range(n + 2) for w in
                                             ([("qk", s - 1)] if 1 <= s <= n else []) + ([("p", s - 2)] if s >= 2 else [])])}
        block = ctx.enter_context(nc.Block())

        @block.gpsimd
        def _(pool):
            if l == 0:
                for t in (q_ready, q_squared, q_rotated, sq_read, qk_ready, v_free, t_free, s_ready, s_read, p_exp, o_ready,
                          o_copied):
                    pool.sem_inc(t.sem, t.credit)
            pool.wait_ge(cleared, l + 1)
            with pool.Fori(0, B) as b:
                def rotate_sum(i):
                    q_rotated.wait(pool, b, i + 1)
                    pool.tensor_tensor(rA[:], rA[:], rB[:], ALU.add).then_inc(q_summed.sem, 1)
                    sq_read.wait(pool, b, i + 1)
                    pool.sem_inc(pool_passed, 1)
                    pool.tensor_scalar(sg[:], ss[:, i % 2, :], 1e-24, None, ALU.max).then_inc(ss_safe.sem, 1)
                    ss_safe.wait(pool, b, i + 1)
                    qk_ready.wait(pool, b, i - 1 if i else 0)
                    pool.tensor_tensor(rn[:, i % 2, :], sg[:], mhalf[:], ALU.pow).then_inc(rn_ready.sem, 1)

                def probs(i):
                    rz_ready.wait(pool, b, i + 1)
                    pool.tensor_tensor(Pm[:, i % 2], Pm[:, i % 2], rz[:, i % 2, :].unsqueeze(2).broadcast_to([P, H, P]),
                                       ALU.mult).then_inc(p_ready.sem, 1)

                for s in range(n + 2):
                    if s < n:
                        rotate_sum(s)
                    if 1 <= s <= n:
                        probs(s - 1)

        @block.tensor
        def _(pe):
            with pe.Fori(0, B) as b:
                def project(i):
                    staged.wait(pe, b, i + 1)
                    q_squared.wait(pe, b, 2 * i)
                    q_rotated.wait(pe, b, i)
                    for k in range(2):
                        mm = pe.matmul(psQ[k][:], hs[:, i % 2, :], wqkv[:, l, k * INNER:(k + 1) * INNER], start=True, stop=True)
                    mm.then_inc(q_ready.sem, 1)
                    v_free.wait(pe, b, v_use["v", i])
                    pe.matmul(psV[:], hs[:, i % 2, :], wqkv[:, l, 2 * INNER:3 * INNER], start=True, stop=True).then_inc(v_ready.sem, 1)

                def scores(i):
                    qk_ready.wait(pe, b, i + 1)
                    t_free.wait(pe, b, t_use["qk", i])
                    for c in range(8):
                        mm = pe.transpose(psT[c // 4][:, c % 4, :], qk[:, i % 2, c * P:(c + 1) * P], ident[:])
                    mm.then_inc(t_ready.sem, 1)
                    s_read.wait(pe, b, H * i)
                    k_prev.wait(pe, b, i + 1)
                    t_free.wait(pe, b, t_use["qk", i] + 1)
                    pe.sem_inc(pe_passed, 1)
                    for h in range(H):
                        r = 64 * (h % 2)
                        for w in range(2):
                            mm = pe.matmul(psS[h % 2][64 * w:64 * w + 64, h // 2, :], qT[r:r + 64, i % 2, h // 2, 64 * w:64 * w + 64],
                                           kT[r:r + 64, i % 2, h // 2, 64 * w:64 * w + P], start=True, stop=True)
                    mm.then_inc(s_ready.sem, 1)

                def attend(i):
                    p_ready.wait(pe, b, i + 1)
                    t_free.wait(pe, b, t_use["p", i])
                    for h in range(H):
                        mm = pe.transpose(psT[h // 4][:, h % 4, :], Pm[:, i % 2, h, :], ident[:])
                    mm.then_inc(t_ready.sem, 1)
                    o_copied.wait(pe, b, i)
                    t_free.wait(pe, b, t_use["p", i] + 1)
                    for h in range(H):
                        for w in range(2):
                            v = vfull if w else vhalf
                            mm = pe.matmul(psO[64 * (h % 2):64 * (h % 2) + 64, h // 2, 64 * w:64 * w + 64],
                                           v[:, i % 4, h * DH:(h + 1) * DH], PT[:, h, 64 * w:64 * w + 64], start=True, stop=True)
                    mm.then_inc(o_ready.sem, 1)
                    o_copied.wait(pe, b, i + 1)
                    v_free.wait(pe, b, v_use["y", i])
                    for c in range(4):
                        mm = pe.matmul(psV[:, 0:P], wo[:, l, c, :], OT[:, c, :], start=(c == 0), stop=(c == 3))
                    mm.then_inc(v_ready.sem, 1)

                for s in range(n + 2):
                    if s < n:
                        project(s)
                    if 1 <= s <= n:
                        scores(s - 1)
                    if s >= 2:
                        attend(s - 2)

        @block.scalar
        def _(act):
            act.preload_act_table_set("natural_log_exp_and_others")
            act.wait_ge(cleared, l + 1)
            with act.Fori(0, B) as b:
                def stage(i):
                    v_ready.wait(act, b, v_use["v", i - 2] + 1) if i >= 2 else None
                    act.copy(hs[0:64, i % 2, :], X[0:64, b, bass.ds(1 + i * P, P)])
                    act.copy(hs[64:128, i % 2, :], X[64:128, b, bass.ds(i * P, P)]).then_inc(staged.sem, 1)

                def project(i):
                    q_ready.wait(act, b, i + 1)
                    sq_read.wait(act, b, i)
                    act.activation(sq[:, 0, :], psQ[0][:], ACT.Square).then_inc(q_squared.sem, 1)
                    act.activation(sq[:, 1, :], psQ[1][:], ACT.Square).then_inc(q_squared.sem, 1)
                    v_ready.wait(act, b, v_use["v", i] + 1)
                    o_ready.wait(act, b, i - 3)
                    act.copy(vfull[:, i % 4, :], psV[:])
                    act.copy(vhalf[64:128, i % 4, :], psV[0:64, :])
                    act.copy(vhalf[0:64, (i + 1) % 4, :], psV[64:128, :]).then_inc(v_free.sem, 1)

                def turned(i):
                    t_ready.wait(act, b, t_use["qk", i] + 1)
                    s_ready.wait(act, b, i - 1)
                    act.copy(qT[:, i % 2], psT[0][:])
                    act.copy(kT[:, i % 2, :, WINDOW:WINDOW + P], psT[1][:]).then_inc(t_free.sem, 1)

                def probs(i):
                    t_ready.wait(act, b, t_use["p", i - 2] + 1) if i >= 2 else None
                    for h in range(H):
                        s_read.wait(act, b, H * i + h + 1)
                        act.activation(Pm[:, i % 2, h, :], Sm[:, h, :], ACT.Exp, scale=-1.0, bias=nmx[:, i % 2, h:h + 1],
                                       accum_out=Z[:, i % 2, h:h + 1]).then_inc(p_exp.sem, 1)

                def turned_probs(i):
                    t_ready.wait(act, b, t_use["p", i] + 1)
                    o_ready.wait(act, b, i)
                    act.copy(PT[:, 0:4], psT[0][:])
                    act.copy(PT[:, 4:8], psT[1][:]).then_inc(t_free.sem, 1)

                def outputs(i):
                    o_ready.wait(act, b, i + 1)
                    act.copy(OT[:], psO[:]).then_inc(o_copied.sem, 1)

                stage(0)
                for s in range(n + 2):
                    if s + 1 < n:
                        stage(s + 1)
                    if s < n:
                        project(s)
                    if 1 <= s <= n:
                        turned(s - 1)
                    if s >= 2:
                        turned_probs(s - 2)
                    if 1 <= s <= n:
                        probs(s - 1)
                    if s >= 2:
                        outputs(s - 2)

        @block.vector
        def _(dve):
            dve.memset(mhalf[:], -0.5)
            dve.memset(vhalf[0:64, 0, :], 0.0)
            dve.memset(kT[:, 1], 0.0).then_inc(cleared, 1)
            dve.wait_ge(cleared, l + 1)
            with dve.Fori(0, B) as b:
                def project(i):
                    q_ready.wait(dve, b, i + 1)
                    qk_ready.wait(dve, b, i)
                    for k in range(2):
                        q_squared.wait(dve, b, 2 * i + k + 1)
                        v = psQ[k][:].rearrange("p (h d) -> p h d", h=H)
                        dve.tensor_tensor(rA[:, k].rearrange("p (h d) -> p h d", h=H), v,
                                          xtab[:, l, i, k:k + 1, :].broadcast_to([P, H, DH]), ALU.mult)
                        o = rB[:, k].rearrange("p (h d) -> p h d", h=H)
                        for c in (0, 32):
                            last = dve.tensor_tensor(o[:, :, c:c + 32], v[:, :, 32 - c:64 - c],
                                                     xtab[:, l, i, 2 + k:3 + k, c:c + 32].broadcast_to([P, H, 32]), ALU.mult)
                    last.then_inc(q_rotated.sem, 1)
                    dve.tensor_reduce(ss[:, i % 2, :], sq[:].rearrange("p k (h d) -> p (k h) d", d=DH), AX_X,
                                      ALU.add).then_inc(sq_read.sem, 1)

                def normed(i):
                    q_summed.wait(dve, b, i + 1)
                    rn_ready.wait(dve, b, i + 1)
                    if i >= 2:
                        t_ready.wait(dve, b, t_use["qk", i - 2] + 1)
                    dve.tensor_tensor(qk[:, i % 2].rearrange("p (g d) -> p g d", d=DH), rA[:].rearrange("p k (h d) -> p (k h) d", d=DH),
                                      rn[:, i % 2, :].unsqueeze(2).broadcast_to([P, 2 * H, DH]), ALU.mult).then_inc(qk_ready.sem, 1)

                def previous_keys(i):
                    t_free.wait(dve, b, t_use["qk", i] + 1 if i == 0 else t_use["qk", i - 1] + 1)
                    s_ready.wait(dve, b, i - 1)
                    dve.tensor_copy(kT[:, i % 2, :, 0:WINDOW], kT[:, (i + 1) % 2, :, P:P + WINDOW]).then_inc(k_prev.sem, 1)

                def masked_max(i):
                    s_ready.wait(dve, b, i + 1)
                    p_exp.wait(dve, b, H * i)
                    dve.sem_inc(dve_passed, 1)
                    for h in range(H):
                        dve.tensor_tensor_reduce(out=Sm[:, h, :], in0=psS[h % 2][:, h // 2, :], in1=wmask[:, min(i, 1), :],
                                                 scale=-QK_SCALE, scalar=-NEGMAX, op0=ALU.add, op1=ALU.min,
                                                 accum_out=nmx[:, i % 2, h:h + 1]).then_inc(s_read.sem, 1)

                def sums(i):
                    p_exp.wait(dve, b, H * (i + 1))
                    dve.reciprocal(rz[:, i % 2, :], Z[:, i % 2, :]).then_inc(rz_ready.sem, 1)

                def residual(i):
                    v_ready.wait(dve, b, v_use["y", i] + 1)
                    dve.tensor_tensor(Y[:, b, bass.ds(1 + i * P, P)], psV[:, 0:P], X[:, b, bass.ds(1 + i * P, P)],
                                      ALU.add).then_inc(v_free.sem, 1)

                for s in range(n + 2):
                    if 1 <= s <= n:
                        previous_keys(s - 1)
                    if s < n:
                        project(s)
                    if 1 <= s <= n:
                        masked_max(s - 1)
                    if s < n:
                        normed(s)
                    if 1 <= s <= n:
                        sums(s - 1)
                    if s >= 2:
                        residual(s - 2)


def mlp_block(nc, l, sem, ones, X, Y, w1, w2, fvec, eps):
    tag = f"_m{l}"
    with ExitStack() as ctx:
        def sb(name, shape, dt=F32):
            return ctx.enter_context(nc.sbuf_tensor(name + tag, list(shape), dt))

        def tally(name, per, credit=0):
            return Tally(sem(name), per, credit, l * B)

        def psum(name):
            return ctx.enter_context(nc.psum_tensor(name + tag, [P, 512], F32))

        NB = 2
        hs = sb("hs", [P, NB, 512])
        zc = sb("zc", [P, NB, 512])
        sq = sb("sq", [P, NB, 512])
        rs = sb("rs", [P, NB, 512])
        hn = sb("hn", [P, NB, 512])
        gl = sb("gl", [P, 2, 512])
        u = sb("u", [P, NB, 3, 512])
        stat = [psum(f"stat{q}") for q in range(2)]
        psa = [psum(f"psa{q}") for q in range(2)]
        psg = [psum(f"psg{q}") for q in range(2)]
        psy = [psum(f"psy{q}") for q in range(2)]

        staged = tally("mlp_staged", NB)
        mean_done = tally("mlp_mean_done", NB)
        centred = tally("mlp_centred", NB)
        squared = tally("mlp_squared", NB)
        var_done = tally("mlp_var_done", NB)
        logged = tally("mlp_logged", NB)
        rstd = tally("mlp_rstd", NB)
        scaled = tally("mlp_scaled", NB)
        h_ready = tally("mlp_h_ready", NB)
        hid_ready = tally("mlp_hid_ready", 3 * NB)
        gelu = tally("mlp_gelu", 3 * NB, 2)
        gated = tally("mlp_gated", 3 * NB, 2)
        y_ready = tally("mlp_y_ready", NB, 2)
        y_read = tally("mlp_y_read", NB, 2)
        block = ctx.enter_context(nc.Block())

        @block.gpsimd
        def _(pool):
            if l == 0:
                for t in (gelu, gated, y_ready, y_read):
                    pool.sem_inc(t.sem, t.credit)
        @block.tensor
        def _(pe):
            with pe.Fori(0, B) as b:
                for q in range(NB):
                    staged.wait(pe, b, q + 1)
                    pe.matmul(stat[q][:], ones[:], hs[:, q, :], start=True, stop=True).then_inc(mean_done.sem, 1)
                for q in range(NB):
                    squared.wait(pe, b, q + 1)
                    pe.matmul(stat[q][:], ones[:], sq[:, q, :], start=True, stop=True).then_inc(var_done.sem, 1)
                for q in range(NB):
                    h_ready.wait(pe, b, q + 1)
                    for c, (o, w) in enumerate(HCH):
                        k = 3 * q + c
                        gated.wait(pe, b, k - 1)
                        pe.matmul(psg[k % 2][0:w, :], w1[:, l, HID + o:HID + o + w], hn[:, q, :], start=True, stop=True)
                        pe.matmul(psa[k % 2][0:w, :], w1[:, l, o:o + w], hn[:, q, :], start=True, stop=True
                                  ).then_inc(hid_ready.sem, 1)
                for q in range(NB):
                    y_read.wait(pe, b, q - 1)
                    for c, (o, w) in enumerate(HCH):
                        gated.wait(pe, b, 3 * q + c + 1)
                        mm = pe.matmul(psy[q][:], w2[0:w, l, c, :], u[0:w, q, c, :], start=(c == 0), stop=(c == 2))
                    mm.then_inc(y_ready.sem, 1)

        @block.scalar
        def _(act):
            with act.Fori(0, B) as b:
                act.preload_act_table_set("natural_log_exp_and_others")
                for q in range(NB):
                    y_ready.wait(act, b, q - 1)
                    act.copy(hs[0:64, q, :], Y[0:64, b, bass.ds(1 + q * 512, 512)])
                    act.copy(hs[64:128, q, :], Y[64:128, b, bass.ds(q * 512, 512)]).then_inc(staged.sem, 1)
                for q in range(NB):
                    centred.wait(act, b, q + 1)
                    act.activation(sq[:, q, :], zc[:, q, :], ACT.Square).then_inc(squared.sem, 1)
                for q in range(NB):
                    var_done.wait(act, b, q + 1)
                    act.activation(rs[:, q, :], stat[q][:], ACT.Ln, bias=eps[:, 0:1]).then_inc(logged.sem, 1)
                for q in range(NB):
                    logged.wait(act, b, q + 1)
                    act.activation(rs[:, q, :], rs[:, q, :], ACT.Exp, scale=-0.5).then_inc(rstd.sem, 1)
                for k in range(3 * NB):
                    w = HCH[k % 3][1]
                    hid_ready.wait(act, b, k + 1)
                    gated.wait(act, b, k - 1)
                    act.activation(gl[0:w, k % 2, :], psg[k % 2][0:w, :], ACT.Gelu,
                                   bias=fvec[0:w, l, 6 + k % 3:7 + k % 3]).then_inc(gelu.sem, 1)

        @block.vector
        def _(dve):
            with dve.Fori(0, B) as b:
                for q in range(NB):
                    mean_done.wait(dve, b, q + 1)
                    dve.tensor_tensor(zc[:, q, :], hs[:, q, :], stat[q][:], ALU.subtract).then_inc(centred.sem, 1)
                for q in range(NB):
                    rstd.wait(dve, b, q + 1)
                    dve.tensor_tensor(zc[:, q, :], zc[:, q, :], rs[:, q, :], ALU.mult).then_inc(scaled.sem, 1)
                    scaled.wait(dve, b, q + 1)
                    dve.tensor_scalar(hn[:, q, :], zc[:, q, :], fvec[:, l, 0:1], fvec[:, l, 1:2], ALU.mult, ALU.add
                                      ).then_inc(h_ready.sem, 1)
                for k in range(3 * NB):
                    w = HCH[k % 3][1]
                    gelu.wait(dve, b, k + 1)
                    dve.scalar_tensor_tensor(out=u[0:w, k // 3, k % 3, :], in0=psa[k % 2][0:w, :],
                                             scalar=fvec[0:w, l, 3 + k % 3:4 + k % 3], in1=gl[0:w, k % 2, :],
                                             op0=ALU.add, op1=ALU.mult).then_inc(gated.sem, 1)
                for q in range(NB):
                    y_ready.wait(dve, b, q + 1)
                    dve.scalar_tensor_tensor(out=X[:, b, bass.ds(1 + q * 512, 512)], in0=psy[q][:], scalar=fvec[:, l, 2:3],
                                             in1=Y[:, b, bass.ds(1 + q * 512, 512)], op0=ALU.add, op1=ALU.add
                                             ).then_inc(y_read.sem, 1)


def final_block(nc, ident, mod, x1T, X, out):
    with ExitStack() as ctx:
        z = ctx.enter_context(nc.sbuf_tensor("z", [P, B * L], F32))
        o = ctx.enter_context(nc.sbuf_tensor("o", [P, B * TILES, D], F32))
        ps = [ctx.enter_context(nc.psum_tensor(f"psf{q}", [P, 4, D], F32)) for q in range(4)]
        summed, turned, copied, stored = [ctx.enter_context(nc.semaphore(s)) for s in ("summed", "turned_f", "copied_f", "stored")]
        block = ctx.enter_context(nc.Block())
        out_t = out.rearrange("b (n p) d -> p (b n) d", p=P)

        @block.sync
        def _(sp):
            for q in range(4):
                sp.wait_ge(copied, q + 1)
                sp.dma_start(out_t[:, 4 * q:4 * q + 4, :], o[:, 4 * q:4 * q + 4, :]).then_inc(stored, 16)
            sp.wait_ge(stored, 64)

        @block.vector
        def _(dve):
            for q in range(4):
                b, c = q // 2, 512 * (q % 2)
                dve.scalar_tensor_tensor(out=z[:, q * 512:(q + 1) * 512], in0=X[:, b, 1 + c:513 + c], scalar=mod[:, 5, b:b + 1],
                                         in1=x1T[:, b, c:c + 512], op0=ALU.mult, op1=ALU.add).then_inc(summed, 1)

        @block.tensor
        def _(pe):
            for q in range(4):
                pe.wait_ge(summed, q + 1)
                for n in range(4):
                    mm = pe.transpose(ps[q][:, n, :], z[:, (4 * q + n) * P:(4 * q + n + 1) * P], ident[:])
                mm.then_inc(turned, 1)

        @block.scalar
        def _(act):
            for q in range(4):
                act.wait_ge(turned, q + 1)
                act.copy(o[:, 4 * q:4 * q + 4, :], ps[q][:]).then_inc(copied, 1)


_INS = ['L0_attn_x', 'L0_attn_W_dkv', 'L0_attn_W_uk', 'L0_attn_W_uv', 'L0_attn_W_dq', 'L0_attn_W_uq', 'L0_attn_W_qr',
        'L0_attn_W_kr', 'L0_attn_W_out', 'L0_attn_idx_wq', 'L0_attn_idx_wk', 'L0_attn_idx_w', 'L0_attn_raw_delta',
        'L0_ffn_wqkv', 'L0_ffn_q_scale', 'L0_ffn_k_scale', 'L0_ffn_wo', 'L0_ffn_ln_g', 'L0_ffn_ln_b', 'L0_ffn_w1',
        'L0_ffn_b1', 'L0_ffn_w2', 'L0_ffn_b2', 'L0_c', 'L0_wmod']


def kernel(**inputs):
    import concourse.bacc as _bacc
    from concourse import mybir as _mybir
    from concourse.bass_utils import run_bass_kernel_spmd as _run

    nc = _bacc.Bacc("TRN2", target_bir_lowering=False, num_devices=1)
    arrays, ins, consts = {}, {}, {}
    for name in _INS:
        a = np.ascontiguousarray(inputs[name])
        arrays[f"in_{name}"] = a
        ins[name] = nc.dram_tensor(f"in_{name}", a.shape, _mybir.dt.from_np(a.dtype), kind="ExternalInput").ap()
    for name, a in constants().items():
        a = np.ascontiguousarray(a)
        arrays[f"const_{name}"] = a
        consts[name] = nc.dram_tensor(f"const_{name}", a.shape, _mybir.dt.from_np(a.dtype), kind="ExternalInput").ap()
    out = nc.dram_tensor("out_x", (B, L, D), F32, kind="ExternalOutput").ap()
    nc.disable_value_cache = True
    kernel_program(nc, ins, consts, out)
    r = _run(nc, [arrays], core_ids=[0])
    return r.results[0]["out_x"]
```

```python
from contextlib import ExitStack

import numpy as np

import concourse.bass as bass
from concourse import mybir

ALU = mybir.AluOpType
ACT = mybir.ActivationFunctionType
AX_X = mybir.AxisListType.X
F32 = mybir.dt.float32
F16 = mybir.dt.float16
BF16 = mybir.dt.bfloat16
U16 = mybir.dt.uint16

P = 128
B, L, D = 2, 1024, 128
TILES = L // P
CKV, CQ, H, DH, ROPE = 32, 64, 8, 64, 32
HALF = ROPE // 2
IDX_HEADS, KTS, LW = 4, 96, 64
NSEL = KTS - LW
TOP_ROUNDS = NSEL // 8
PAIR = 32
UNIT = 16
PAIRS = L // PAIR
PPT = P // PAIR
GROUPS = PAIR // 4
WIN = 80
SCOLS = P + WIN
ATTN_SCALE = float(DH + ROPE) ** -0.5
DEPTH, INNER, WINDOW = 2, 512, 64
HID = int(D * 4 * 2 / 3)
HCH = [(0, 128), (128, 128), (256, HID - 256)]
QK_SCALE = 8.0
LN_EPS = 1e-5
NEG = -1e30
NEGMAX = -3e38
PI = 3.1415925


def constants():
    f = np.float32
    theta = (1.0 / f(10000.0) ** (f(2.0) * np.arange(HALF, dtype=f) / f(ROPE))).astype(f)
    t = np.arange(L, dtype=f)
    out = {}
    out["ident"] = np.eye(P, dtype=f)
    def rope(pos):
        a = (pos.astype(np.float64)[None, :] * theta.astype(np.float64)[:, None])
        c, s = np.cos(a).astype(f), np.sin(a).astype(f)
        p1 = np.concatenate([c, c, -s, s], 0)
        p2 = np.concatenate([-s, -s, -c, c], 0)
        return p1, p2
    rel = t + np.maximum(0.0, t - (LW - 1))
    out["rope"] = np.stack([*rope(t), *rope(rel)], 1).astype(f)
    j = (LW + np.arange(P) % NSEL).astype(np.float64)[:, None] * theta.astype(np.float64)[None, :]
    c, s = np.cos(j), np.sin(j)
    out["rank"] = np.stack([np.concatenate([c, c], 1), np.concatenate([-s, -s], 1),
                            np.concatenate([-s, s], 1), np.concatenate([-c, c], 1)], 1).astype(f)
    selk = np.zeros((P, P), f)
    selq = np.zeros((P, P), f)
    for i in range(32):
        selk[i, i] = 1
        selq[i, i] = selq[i, 64 + i] = 1
        for src in (64 + i, 96 + i):
            selk[src, 64 + i] = selk[src, 96 + i] = 1
            selq[src, 32 + i] = selq[src, 96 + i] = 1
    out["sel"] = np.stack([selk, selq], 1)
    out["keys"] = (np.arange(P)[:, None] + P * np.arange(TILES)[None, :]).astype(f)
    r = np.arange(P)
    tok = r // H
    top = (np.arange(P)[None, :] // NSEL) == (tok % 4)[:, None]
    w = np.arange(WIN)[None, :]
    late = (w >= tok[:, None] + 1) & (w <= tok[:, None] + LW)
    early = np.broadcast_to(w < LW, (P, WIN))
    m = np.stack([np.concatenate([top, early], 1), np.concatenate([top, late], 1)], 1)
    out["umask"] = np.where(m, f(0), f(NEG)).astype(f)
    out["imask"] = np.where(np.arange(P)[None, :] <= r[:, None], f(0), f(NEG)).astype(f)
    key = LW + np.arange(NSEL)[None, :]
    fut = (key > r[:, None])
    out["future"] = np.stack([(~fut).astype(f), fut * key.astype(f)], 1).astype(f)
    half = np.arange(0, DH, 2, dtype=f)
    inv = (f(1.0) / f(10000.0) ** (half / f(DH))).astype(f)
    fr = (t[:, None] * inv[None, :]).astype(f)
    fr = np.concatenate([fr, fr], -1)
    base = ((half + f(0.4 * DH)) / f(1.4 * DH)).astype(f)
    power = ((t - L // 2) / f(WINDOW // 2)).astype(f)
    sc = (base[None, :] ** power[:, None]).astype(f)
    sc = np.concatenate([sc, sc], -1)
    cos, sin = np.cos(fr).astype(f), np.sin(fr).astype(f)
    sgn = np.concatenate([-np.ones(32, f), np.ones(32, f)])[None, :]
    tab = np.stack([cos * sc, cos / sc, sgn * sin * sc, sgn * sin / sc], 1)
    out["xpos"] = np.ascontiguousarray(tab.reshape(TILES, P, 4, DH).transpose(1, 0, 2, 3)).astype(f)
    q = (r % WINDOW)[:, None]
    k = np.arange(P)[None, :]
    ok = (k >= q) & (k <= q + WINDOW)
    first = ok & ((r >= WINDOW)[:, None] | (k >= WINDOW))
    out["wmask"] = np.where(np.stack([first, ok], 1), f(0), f(NEG)).astype(f)
    return out


def kernel_program(nc, ins, consts, out):
    x_d = ins["L0_attn_x"]
    idx_d = nc.dram_tensor("picked_idx", (B * TILES, P, NSEL), F16, kind="Internal").ap()
    c_d = nc.dram_tensor("latent_rows", (B * L, CKV), F32, kind="Internal").ap()

    with ExitStack() as top:
        top.enter_context(nc.allow_non_contiguous_dma(reason="vectors of at most 256 elements, one per partition"))

        def sb(name, shape, dt=F32, ctx=top):
            return ctx.enter_context(nc.sbuf_tensor(name, list(shape), dt))

        ident = sb("ident", [P, P])
        ones = sb("ones", [P, P])
        mod = sb("mod", [P, 6, B])
        x1T = sb("x1T", [P, B, L])
        wqkv = sb("wqkv", [P, DEPTH, 3 * INNER])
        wo = sb("wo", [P, DEPTH, 4, D])
        w1 = sb("w1", [P, DEPTH, 2 * HID])
        w2 = sb("w2", [P, DEPTH, 3, D])
        fvec = sb("fvec", [P, DEPTH, 16])

        with ExitStack() as attn:
            a = Attention(nc, attn, ins, consts, sb, ident, ones, mod, x1T, idx_d, c_d)
            a.ffn = (wqkv, wo, w1, w2, fvec)
            setup_block(nc, a, x_d)
            attention_block(nc, a)
        stack_blocks(nc, top, ins, consts, out, ident, ones, mod, x1T, wqkv, wo, w1, w2, fvec)


class Attention:

    def __init__(self, nc, ctx, ins, consts, sb_, ident, ones, mod, x1T, idx_d, c_d):
        def sb(name, shape, dt=F32):
            return sb_(name, shape, dt, ctx)
        self.ctx, self.ins, self.consts = ctx, ins, consts
        self.ident, self.ones, self.mod, self.x1T, self.idx_d, self.c_d = ident, ones, mod, x1T, idx_d, c_d
        self.hT = sb("hT", [P, B, L])
        self.cqT = sb("cqT", [CQ, B, L])
        self.kiT = sb("kiT", [P, B, L])
        self.khT = sb("khT", [P, B, L])
        self.tabs = sb("tabs", [P, 2, L])
        self.feat = sb("feat", [P, B * TILES, 3, 64], BF16)
        self.WQ = sb("WQ", [CQ, H, P])
        self.wiq = sb("wiq", [P, IDX_HEADS * DH])
        self.Wvo = sb("Wvo", [CKV, H, D])
        self.selm = sb("selm", [P, 2, P])
        self.umask = sb("umask", [P, 2, SCOLS])
        self.imask = sb("imask", [P, P])
        self.future = sb("future", [P, 2, NSEL])
        self.keys = sb("keys", [P, TILES])
        self.wix = sb("wix", [P, IDX_HEADS])
        self.rankCS = sb("rankCS", [P, 2, ROPE])


def setup_block(nc, a, x_d):
    ins, consts = a.ins, a.consts
    wqkv, wo, w1, w2, fvec = a.ffn
    with ExitStack() as ctx:
        def sb(name, shape, dt=F32):
            return ctx.enter_context(nc.sbuf_tensor(name, list(shape), dt))

        def sem(name):
            return ctx.enter_context(nc.semaphore(name))

        x = sb("x", [P, B * TILES, D])
        xn = sb("xn", [P, B * TILES, D])
        st = sb("st", [P, B * TILES, 6])
        mv = sb("mv", [P, B * TILES, 2])
        rstd = sb("rstd", [P, B * TILES])
        mhalf = sb("mhalf", [P, B * TILES])
        wuq = sb("wuq", [CQ, H * DH])
        wuk = sb("wuk", [CKV, H * DH])
        wuv = sb("wuv", [CKV, H * DH])
        wout = sb("wout", [P, 4, D])
        wdq = sb("wdq", [P, CQ])
        WK = sb("WK", [P, P])
        WF = sb("WF", [P, 64])
        wki = sb("wki", [P, 2, DH])
        wT = sb("wT", [P, 4, 128])
        cT = sb("cT", [P, B])
        ce = sb("ce", [P, B])
        cg = sb("cg", [P, B])
        cs = sb("cs", [P, B])
        wmod = sb("wmod", [P, 6, D])
        gsg = sb("gsg", [P, 2, B])
        gab = sb("gab", [P, 2, B])
        dl = sb("dl", [P, 33])
        d1 = sb("d1", [P, 33])
        d2 = sb("d2", [P, 33])
        sg = sb("sg", [P, 33])
        arg = sb("arg", [P, 2, 33])
        sn = sb("sn", [P, 2, 33])
        sind = sb("sind", [P, 33])
        cosd = sb("cosd", [P, 33])
        ropet = sb("ropet", [P, 4, L])
        rankt = sb("rankt", [P, 4, ROPE])
        rtmp = sb("rtmp", [P, 2, ROPE])
        kab = sb("kab", [P, B * L])
        kex = sb("kex", [P, B * L])
        F = sb("F", [P, B * TILES, 64])
        F2 = sb("F2", [P, B * TILES, 64])
        fab = sb("fab", [P, B * TILES, ROPE])
        fex = sb("fex", [P, B * TILES, ROPE])
        banks = [ctx.enter_context(nc.psum_tensor(f"bank{i}", [P, 512], F32)) for i in range(8)]

        x_loaded, w_loaded, c_loaded = sem("x_loaded"), sem("w_loaded"), sem("c_loaded")
        ffn_loaded, rows_stored = sem("ffn_loaded"), sem("rows_stored")
        zeroed, stats, aggr, vareps, rstd_ready, normed = (
            sem("zeroed"), sem("stats"), sem("aggr"), sem("vareps"), sem("rstd_ready"), sem("normed"))
        c_exp, c_den, c_gate, c_silu = sem("c_exp"), sem("c_den"), sem("c_gate"), sem("c_silu")
        mod_mm, mod_copied, mod_gate, mod_ready = sem("mod_mm"), sem("mod_copied"), sem("mod_gate"), sem("mod_ready")
        d_step, d_exp, d_sin, tab_step, tabs_ready = (
            sem("d_step"), sem("d_exp"), sem("d_sin"), sem("tab_step"), sem("tabs_ready"))
        turned, turn_copied = sem("turned"), sem("turn_copied")
        wt_turned, wt_copied, fused, fused_copied = sem("wt_turned"), sem("wt_copied"), sem("fused"), sem("fused_copied")
        proj, proj_copied = sem("proj"), sem("proj_copied")
        kv_mm, kv_abs, kv_exp, kv_ln, kv_soft, kv_rot, kv_sum, kv_done = [
            sem(n) for n in ("kv_mm", "kv_abs", "kv_exp", "kv_ln", "kv_soft", "kv_rot", "kv_sum", "kv_done")]
        ft_mm, ft_abs, ft_exp, ft_ln, ft_soft, ft_c, ft_split = [
            sem(n) for n in ("ft_mm", "ft_abs", "ft_exp", "ft_ln", "ft_soft", "ft_c", "ft_split")]

        N_W, N_C = 23, 18
        block = ctx.enter_context(nc.Block())

        @block.sync
        def _(sp):
            sp.dma_start(x[:], x_d.rearrange("b (n p) d -> p (b n) d", p=P)).then_inc(x_loaded, 16)
            def w(dst, src):
                sp.dma_start(dst, src).then_inc(w_loaded, 16)
            w(cT[:], ins["L0_c"].rearrange("b d -> d b"))
            w(wmod[:], ins["L0_wmod"].rearrange("k (m d) -> k m d", m=6))
            w(wuq[:], ins["L0_attn_W_uq"])
            w(wuk[:], ins["L0_attn_W_uk"])
            w(wuv[:], ins["L0_attn_W_uv"])
            w(wout[:], ins["L0_attn_W_out"].rearrange("(n p) d -> p n d", p=P))
            w(wdq[:], ins["L0_attn_W_dq"])
            w(WK[:, 0:CKV], ins["L0_attn_W_dkv"])
            kr = ins["L0_attn_W_kr"]
            w(WK[:, 64:96], kr)
            w(WK[:, 96:112], kr[:, HALF:ROPE])
            w(WK[:, 112:128], kr[:, 0:HALF])
            w(WF[:, 0:CKV], ins["L0_attn_W_dkv"])
            w(WF[:, CKV:64], kr)
            w(wki[:, 0, :], ins["L0_attn_idx_wk"])
            w(wki[:, 1, :], ins["L0_attn_idx_wk"])
            w(a.wiq[:], ins["L0_attn_idx_wq"])
            qr = ins["L0_attn_W_qr"].rearrange("k (h d) -> k h d", h=H)
            w(a.WQ[:, :, 64:96], qr)
            w(a.WQ[:, :, 96:112], qr[:, :, HALF:ROPE])
            w(a.WQ[:, :, 112:128], qr[:, :, 0:HALF])
            w(a.wix[:], ins["L0_attn_idx_w"].partition_broadcast(P))
            rd = ins["L0_attn_raw_delta"]
            w(dl[:, 0:HALF], rd.partition_broadcast(P))
            w(dl[:, HALF:ROPE], rd.partition_broadcast(P))
            w(dl[0:HALF, 32:33], rd.rearrange("(p o) -> p o", o=1))
            sp.wait_ge(ft_c, 1)
            sp.dma_start(a.c_d.rearrange("(n p) c -> p n c", p=P), F[:, :, 0:CKV]).then_inc(rows_stored, 16)
            sp.wait_ge(rows_stored, 16)

        @block.gpsimd
        def _(pool):
            def c(dst, src):
                pool.dma_start(dst, src).then_inc(c_loaded, 16)
            c(a.ident[:], consts["ident"])
            rd = ins["L0_attn_raw_delta"].rearrange("(p o) -> p o", o=1)
            for r in range(16, P, HALF):
                c(dl[r:r + HALF, 32:33], rd)
            c(ropet[64:128], consts["rope"])
            c(rankt[:], consts["rank"])
            c(a.selm[:], consts["sel"])
            c(a.keys[:], consts["keys"])
            c(a.umask[:], consts["umask"])
            c(a.imask[:], consts["imask"])
            c(a.future[:], consts["future"])
            pool.wait_ge(aggr, B * TILES)
            pool.tensor_scalar(rstd[:], mv[:, :, 1], LN_EPS, None, ALU.add).then_inc(vareps, 1)
            pool.wait_ge(vareps, 1)
            pool.wait_ge(zeroed, 1)
            pool.tensor_tensor(rstd[:], rstd[:], mhalf[:], ALU.pow).then_inc(rstd_ready, 1)
            for l in range(DEPTH):
                pool.dma_start(wqkv[:, l], ins["L0_ffn_wqkv"][l]).then_inc(ffn_loaded, 16)
                pool.dma_start(wo[:, l], ins["L0_ffn_wo"][l].rearrange("(n p) d -> p n d", p=P)).then_inc(ffn_loaded, 16)
                pool.dma_start(w1[:, l], ins["L0_ffn_w1"][l]).then_inc(ffn_loaded, 16)
                pool.dma_start(w2[:, l, 0:2], ins["L0_ffn_w2"][l, 0:256].rearrange("(n p) d -> p n d", p=P)).then_inc(ffn_loaded, 16)
                pool.dma_start(w2[0:HID - 256, l, 2], ins["L0_ffn_w2"][l, 256:HID]).then_inc(ffn_loaded, 16)
                for k, name in enumerate(("L0_ffn_ln_g", "L0_ffn_ln_b", "L0_ffn_b2")):
                    pool.dma_start(fvec[:, l, k:k + 1], ins[name][l].rearrange("(p o) -> p o", o=1)).then_inc(ffn_loaded, 16)
                for half in range(2):
                    for k, (o, n) in enumerate(HCH):
                        pool.dma_start(fvec[0:n, l, 3 + 3 * half + k:4 + 3 * half + k],
                                       ins["L0_ffn_b1"][l, half * HID + o:half * HID + o + n].rearrange("(p o) -> p o", o=1)
                                       ).then_inc(ffn_loaded, 16)
            pool.wait_ge(ffn_loaded, 16 * 14 * DEPTH)

        @block.tensor
        def _(pe):
            pe.wait_ge(w_loaded, 16 * N_W)
            pe.wait_ge(c_silu, 1)
            for k in range(6):
                mm = pe.matmul(banks[7][:, 2 * k:2 * k + 2], wmod[:, k, :], cs[:], start=True, stop=True)
            mm.then_inc(mod_mm, 1)
            pe.wait_ge(c_loaded, 16 * N_C_POOL)
            for n in range(4):
                bk = banks[n]
                pe.transpose(bk[:, 0:64], wuq[:, n * P:(n + 1) * P], a.ident[0:CQ, 0:CQ])
                pe.transpose(bk[:, 64:96], wuk[:, n * P:(n + 1) * P], a.ident[0:CKV, 0:CKV])
                pe.transpose(bk[:, 96:128], wuv[:, n * P:(n + 1) * P], a.ident[0:CKV, 0:CKV]).then_inc(wt_turned, 1)
            pe.wait_ge(wt_copied, 4)
            for h in range(H):
                r = 64 * (h % 2)
                pe.matmul(banks[4 - h % 2][0:CQ, (h // 2) * 32:(h // 2) * 32 + 32], wT[r:r + 64, h // 2, 0:64],
                          wT[r:r + 64, h // 2, 64:96], start=True, stop=True)
            for h in range(H):
                r = 64 * (h % 2)
                mm = pe.matmul(banks[5 + h % 2][0:CKV, (h // 2) * D:(h // 2 + 1) * D], wT[r:r + 64, h // 2, 96:128],
                               wout[r:r + 64, h // 2, :], start=True, stop=True)
            mm.then_inc(fused, 1)
            for q in range(8):
                pe.wait_ge(normed, min(4 * q + 4, 16))
                if q >= 4:
                    pe.wait_ge(turn_copied, q - 3)
                if q == 3:
                    pe.wait_ge(fused_copied, 4)
                src = xn if q < 4 else x
                for n in range(4):
                    mm = pe.transpose(banks[q % 4][:, n * P:(n + 1) * P], src[:, 4 * (q % 4) + n, :], a.ident[:])
                mm.then_inc(turned, 1)
            hT = a.hT[:].rearrange("p b t -> p (b t)")
            pe.wait_ge(turn_copied, 8)
            for q in range(4):
                pe.matmul(banks[q][:], WK[:], hT[:, q * 512:(q + 1) * 512], start=True, stop=True).then_inc(kv_mm, 1)
            for n in range(16):
                mm = pe.matmul(banks[4 + n // 8][:, 64 * (n % 8):64 * (n % 8) + 64], hT[:, n * P:(n + 1) * P],
                               WF[:], start=True, stop=True)
            mm.then_inc(ft_mm, 1)
            for q in range(4):
                if q >= 1:
                    pe.wait_ge(proj_copied, 2 * q)
                pe.matmul(banks[6][0:CQ, :], wdq[:], hT[:, q * 512:(q + 1) * 512], start=True, stop=True).then_inc(proj, 1)
                pe.matmul(banks[7][:], wki[:].rearrange("p a d -> p (a d)"), hT[:, q * 512:(q + 1) * 512],
                          start=True, stop=True).then_inc(proj, 1)
            for q in range(4):
                pe.wait_ge(kv_rot, q + 1)
                pe.matmul(banks[q][:], a.selm[:, 0, :], a.khT[:].rearrange("p b t -> p (b t)")[:, q * 512:(q + 1) * 512],
                          start=True, stop=True).then_inc(kv_sum, 1)

        @block.scalar
        def _(act):
            act.preload_act_table_set("natural_log_exp_and_others")
            act.wait_ge(w_loaded, 16 * N_W)
            act.activation(ce[:], cT[:], ACT.Exp, scale=-1.0).then_inc(c_exp, 1)
            act.wait_ge(c_loaded, 16 * N_C_POOL)
            act.activation(d1[:], dl[:], ACT.Exp, scale=-1.0).then_inc(d_exp, 1)
            act.wait_ge(d_step, 3)
            act.activation(sn[:], arg[:], ACT.Sin).then_inc(d_sin, 1)
            act.preload_act_table_set("natural_log_exp_and_others")
            for n in range(4):
                act.wait_ge(wt_turned, n + 1)
                act.copy(wT[:, n, :], banks[n][:, 0:128]).then_inc(wt_copied, 1)
            hT = a.hT[:].rearrange("p b t -> p (b t)")
            xT = a.x1T[:].rearrange("p b t -> p (b t)")
            for q in range(8):
                act.wait_ge(turned, q + 1)
                if q == 0:
                    act.wait_ge(mod_ready, 1)
                b = (q % 4) // 2
                sl = slice((q % 4) * 512, (q % 4 + 1) * 512)
                if q < 4:
                    act.activation(hT[:, sl], banks[q % 4][:], ACT.Identity, scale=a.mod[:, 1, b:b + 1],
                                   bias=a.mod[:, 0, b:b + 1]).then_inc(turn_copied, 1)
                else:
                    act.copy(xT[:, sl], banks[q % 4][:]).then_inc(turn_copied, 1)
            for q in range(4):
                sl = slice(q * 512, (q + 1) * 512)
                act.wait_ge(kv_mm, q + 1)
                act.copy(a.khT[:].rearrange("p b t -> p (b t)")[0:64, sl], banks[q][0:64, :])
                act.activation(kab[64:128, sl], banks[q][64:128, :], ACT.Abs).then_inc(kv_abs, 1)
                act.wait_ge(kv_abs, q + 1)
                act.activation(kex[64:128, sl], kab[64:128, sl], ACT.Exp, scale=-1.0).then_inc(kv_exp, 1)
                act.wait_ge(kv_exp, q + 1)
                act.activation(kab[64:128, sl], kex[64:128, sl], ACT.Ln, bias=1.0).then_inc(kv_ln, 1)
            act.wait_ge(ft_mm, 1)
            for k in range(2):
                fv = banks[4 + k][:].rearrange("p (n f) -> p n f", f=64)
                act.activation(fab[:, 8 * k:8 * k + 8, :], fv[:, :, CKV:64], ACT.Abs)
                act.copy(F[:, 8 * k:8 * k + 8, 0:CKV], fv[:, :, 0:CKV]).then_inc(ft_abs, 1)
            act.wait_ge(ft_abs, 2)
            act.activation(fex[:], fab[:], ACT.Exp, scale=-1.0).then_inc(ft_exp, 1)
            act.wait_ge(ft_exp, 1)
            act.activation(fab[:], fex[:], ACT.Ln, bias=1.0).then_inc(ft_ln, 1)
            cq = a.cqT[:].rearrange("p b t -> p (b t)")
            ki = a.kiT[:].rearrange("p b t -> p (b t)")
            for q in range(4):
                sl = slice(q * 512, (q + 1) * 512)
                act.wait_ge(proj, 2 * q + 1)
                act.copy(cq[:, sl], banks[6][0:CQ, :]).then_inc(proj_copied, 1)
                act.wait_ge(proj, 2 * q + 2)
                act.copy(ki[:, sl], banks[7][:]).then_inc(proj_copied, 1)
            for q in range(4):
                act.wait_ge(kv_sum, q + 1)
                act.copy(a.khT[:].rearrange("p b t -> p (b t)")[:, q * 512:(q + 1) * 512], banks[q][:]).then_inc(kv_done, 1)

        @block.vector
        def _(dve):
            dve.memset(mhalf[:], -0.5)
            dve.memset(WK[:, CKV:64], 0.0)
            dve.memset(a.ones[:], 1.0 / D)
            dve.memset(a.WQ[:, :, CKV:64], 0.0).then_inc(zeroed, 1)
            dve.wait_ge(x_loaded, 16)
            for n in range(B * TILES):
                dve.bn_stats(st[:, n, :], x[:, n, :]).then_inc(stats, 1)
            for n in range(B * TILES):
                dve.wait_ge(stats, n + 1)
                dve.bn_aggr(mv[:, n, :], st[:, n, :]).then_inc(aggr, 1)
            dve.wait_ge(c_exp, 1)
            dve.tensor_scalar(cg[:], ce[:], 1.0, None, ALU.add).then_inc(c_den, 1)
            dve.wait_ge(c_den, 1)
            dve.reciprocal(ce[:], cg[:]).then_inc(c_gate, 1)
            dve.wait_ge(c_gate, 1)
            dve.tensor_tensor(cs[:], cT[:], ce[:], ALU.mult).then_inc(c_silu, 1)
            dve.wait_ge(d_exp, 1)
            dve.tensor_scalar(d2[:], d1[:], 1.0, None, ALU.add).then_inc(d_step, 1)
            dve.wait_ge(d_step, 1)
            dve.reciprocal(sg[:], d2[:]).then_inc(d_step, 1)
            dve.wait_ge(d_step, 2)
            dve.tensor_scalar(arg[:, 0, :], sg[:], PI, None, ALU.mult)
            dve.tensor_scalar(arg[:, 1, :], sg[:], -PI, PI / 2, ALU.mult, ALU.add).then_inc(d_step, 1)
            dve.wait_ge(rstd_ready, 1)
            for n in range(B * TILES):
                dve.tensor_scalar(xn[:, n, :], x[:, n, :], mv[:, n, 0:1], rstd[:, n:n + 1],
                                  ALU.subtract, ALU.mult).then_inc(normed, 1)
            dve.wait_ge(mod_mm, 1)
            mp = banks[7][:, 0:12].rearrange("p (k b) -> p k b", b=B)
            dve.tensor_copy(a.mod[:], mp).then_inc(mod_copied, 1)
            dve.wait_ge(mod_copied, 1)
            for k, o in enumerate((1, 4)):
                dve.tensor_scalar(a.mod[:, o, :], a.mod[:, o, :], 1.0, None, ALU.add)
            for k, o in enumerate((2, 5)):
                dve.tensor_scalar(gsg[:, k, :], a.mod[:, o, :], 0.0, 2.0, ALU.is_ge, ALU.mult)
                dve.scalar_tensor_tensor(out=gab[:, k, :], in0=a.mod[:, o, :], scalar=-1.0, in1=a.mod[:, o, :],
                                         op0=ALU.mult, op1=ALU.max).then_inc(mod_gate, 1)
            dve.wait_ge(mod_gate, 2)
            dve.tensor_scalar(gab[:], gab[:], 0.25, None, ALU.max).then_inc(mod_gate, 1)
            dve.wait_ge(mod_gate, 3)
            for k, o in enumerate((2, 5)):
                last = dve.scalar_tensor_tensor(out=a.mod[:, o, :], in0=gsg[:, k, :], scalar=-1.0, in1=gab[:, k, :],
                                                op0=ALU.add, op1=ALU.mult)
            last.then_inc(mod_ready, 1)
            dve.wait_ge(d_sin, 1)
            dve.scalar_tensor_tensor(out=sind[:], in0=sn[:, 0, :], scalar=-2.0, in1=sn[:, 1, :],
                                     op0=ALU.mult, op1=ALU.mult)
            dve.scalar_tensor_tensor(out=d1[:], in0=sn[:, 0, :], scalar=-2.0, in1=sn[:, 0, :],
                                     op0=ALU.mult, op1=ALU.mult).then_inc(tab_step, 1)
            dve.wait_ge(tab_step, 1)
            dve.tensor_scalar(cosd[:], d1[:], 1.0, None, ALU.add).then_inc(tab_step, 1)
            dve.wait_ge(tab_step, 2)
            for k in range(2):
                dve.tensor_scalar(a.tabs[64:128, k, :], ropet[64:128, 2 * k, :], cosd[64:128, 32:33], None,
                                  ALU.mult).then_inc(tab_step, 1)
            dve.tensor_tensor(rtmp[:], rankt[:, 0:4:2, :], cosd[:, 0:32].unsqueeze(1).broadcast_to([P, 2, ROPE]), ALU.mult)
            dve.tensor_tensor(a.rankCS[:], rankt[:, 1:4:2, :], sind[:, 0:32].unsqueeze(1).broadcast_to([P, 2, ROPE]),
                              ALU.mult).then_inc(tab_step, 1)
            dve.wait_ge(tab_step, 5)
            for k in range(2):
                dve.scalar_tensor_tensor(out=a.tabs[64:128, k, :], in0=ropet[64:128, 2 * k + 1, :],
                                         scalar=sind[64:128, 32:33], in1=a.tabs[64:128, k, :],
                                         op0=ALU.mult, op1=ALU.add)
            dve.tensor_tensor(a.rankCS[:], a.rankCS[:], rtmp[:], ALU.add).then_inc(tabs_ready, 1)
            dve.wait_ge(fused, 1)
            for k in range(2):
                dve.tensor_copy(a.WQ[:, k:H:2, 0:CKV], banks[4 - k][0:CQ, 0:128].rearrange("p (h c) -> p h c", h=4)
                                ).then_inc(fused_copied, 1)
                dve.tensor_copy(a.Wvo[:, k:H:2, :], banks[5 + k][0:CKV, :].rearrange("p (h d) -> p h d", h=4)
                                ).then_inc(fused_copied, 1)
            kh = a.khT[:].rearrange("p b t -> p (b t)")
            dve.wait_ge(tabs_ready, 1)
            for q in range(4):
                sl = slice(q * 512, (q + 1) * 512)
                dve.wait_ge(kv_ln, q + 1)
                dve.scalar_tensor_tensor(out=kex[64:128, sl], in0=banks[q][64:128, :], scalar=0.0, in1=kab[64:128, sl],
                                         op0=ALU.max, op1=ALU.add).then_inc(kv_soft, 1)
                dve.wait_ge(kv_soft, q + 1)
                p0 = (q % 2) * 512
                dve.tensor_tensor(kh[64:128, sl], kex[64:128, sl], a.tabs[64:128, 0, p0:p0 + 512], ALU.mult).then_inc(kv_rot, 1)
            dve.wait_ge(ft_ln, 1)
            for k in range(2):
                fv = banks[4 + k][:].rearrange("p (n f) -> p n f", f=64)
                last = dve.scalar_tensor_tensor(out=F[:, 8 * k:8 * k + 8, CKV:64], in0=fv[:, :, CKV:64], scalar=0.0,
                                                in1=fab[:, 8 * k:8 * k + 8, :], op0=ALU.max, op1=ALU.add)
            last.then_inc(ft_c, 1)
            dve.wait_ge(ft_c, 1)
            dve.tensor_copy(a.feat[:, :, 0, :], F[:]).then_inc(ft_split, 1)
            dve.wait_ge(ft_split, 1)
            dve.tensor_tensor(F2[:], F[:], a.feat[:, :, 0, :], ALU.subtract).then_inc(ft_split, 1)
            dve.wait_ge(ft_split, 2)
            dve.tensor_copy(a.feat[:, :, 1, :], F2[:]).then_inc(ft_split, 1)
            dve.wait_ge(ft_split, 3)
            dve.tensor_tensor(a.feat[:, :, 2, :], F2[:], a.feat[:, :, 1, :], ALU.subtract).then_inc(ft_split, 1)


N_C_POOL = 1 + 7 + 7


class Tally:

    def __init__(self, sem, per, credit=0, before=0):
        self.sem, self.per, self.credit, self.before = sem, per, credit, before

    def wait(self, eng, b, n):
        assert n + self.credit > 0
        eng.wait_ge(self.sem, b * self.per + (n + self.credit + self.before * self.per))


def key_blocks(i):
    n = P * i + P - LW
    return [(o, min(512, n - o)) for o in range(0, n, 512)]


EARLY = 5


def scored(s):
    if s == 0:
        return 1
    return s // PPT + 2 if s % PPT == 3 and s // PPT + 2 < TILES else None


def misc_plan():
    plan = []

    def scores(i):
        for kb in range(len(key_blocks(i))):
            for h in range(IDX_HEADS):
                plan.append(("score", i, kb, h))

    def halves(i):
        plan.extend([("half", i, 0), ("half", i, 1)])

    plan.append(("qi", 0))
    scores(0)
    plan.extend([("query", 0, 0), ("query", 0, 1), ("qi", 1)])
    halves(0)
    for s in range(PAIRS + 2):
        i = s // PPT
        if scored(s):
            scores(scored(s))
        if s % PPT == 3 and i + 1 < TILES:
            halves(i + 1)
        if s % PPT == 2 and 1 <= i < TILES:
            plan.append(("attn", i - 1))
        if s % PPT == 2 and i + 2 < TILES:
            plan.append(("qi", i + 2))
        if s % PPT in (0, 1) and i + 1 < TILES:
            plan.append(("query", i + 1, s % PPT))
    plan.append(("attn", TILES - 1))
    return {what: n for n, what in enumerate(plan)}


def attention_block(nc, a):
    use = misc_plan()
    assert len(use) % 2 == 0
    pick_ops = {i: 3 * len(key_blocks(i)) + 1 + 3 * TOP_ROUNDS - 1 + (3 if i == 0 else 1) for i in range(TILES)}

    with ExitStack() as ctx:
        def sb(name, shape, dt=F32):
            return ctx.enter_context(nc.sbuf_tensor(name, list(shape), dt))

        def tally(name, per, credit=0):
            return Tally(ctx.enter_context(nc.semaphore(name)), per, credit)

        qi = sb("qi", [P, IDX_HEADS, P])
        relu = sb("relu", [P, 2, 512])
        isum = sb("isum", [P, L])
        vals = sb("vals", [P, 8])
        idx16 = sb("idx16", [P, NSEL], U16)
        idxf = sb("idxf", [P, NSEL])
        idxh = sb("idxh", [P, 2, NSEL], F16)
        idxb = sb("idxb", [P, 2, P * NSEL], F16)
        featb = sb("featb", [P, TILES, 3, 64], BF16)
        oh = sb("oh", [P, 2, TILES, PAIR * NSEL], BF16)
        qsp = sb("qsp", [P, P, H // 2])
        qex = sb("qex", [P, 512])
        QR = sb("QR", [P, 2, P * H])
        QW = sb("QW", [P, P * H])
        QA = sb("QA", [P, 2, P * H])
        G = sb("G", [P, 4, GROUPS, 64])
        gA = sb("gA", [P, GROUPS, ROPE])
        gB = sb("gB", [P, GROUPS, ROPE])
        GT = sb("GT", [P, GROUPS // 2, P])
        Sm = sb("Sm", [P, 2, SCOLS])
        nmx = sb("nmx", [P, 2, 2])
        Z = sb("Z", [P, 2, 2])
        rz = sb("rz", [P, 2, 2])
        Pb = sb("Pb", [P, 2, 2, 256])
        PTb = sb("PTb", [P, 2, 256])
        cw = sb("cw", [WIN, 4, 2, CKV])
        OT = sb("OT", [CKV, 2, P * H])
        psG = [ctx.enter_context(nc.psum_tensor(f"psG{i}", [P, GROUPS, 64], F32)) for i in range(2)]
        psT = ctx.enter_context(nc.psum_tensor("psT", [P, GROUPS // 2, P], F32))
        psS = [ctx.enter_context(nc.psum_tensor(f"psS{i}", [P, 512], F32)) for i in range(2)]
        psPT = ctx.enter_context(nc.psum_tensor("psPT", [P, 2, 256], F32))
        psO = psT[:].rearrange("p n t -> p (n t)")
        psM = [ctx.enter_context(nc.psum_tensor(f"psM{i}", [P, 512], F32)) for i in range(2)]

        n_use = len(use)
        m_ready = tally("m_ready", n_use)
        m_free = [tally("m_free0", n_use // 2, 1), tally("m_free1", n_use // 2, 1)]
        picking = tally("picking", sum(pick_ops.values()))
        idx_stored = tally("idx_stored", 16 * TILES, 32)
        idx_spread = tally("idx_spread", 16 * TILES)
        oh_ready = tally("oh_ready", PAIRS, 8)
        gathered = tally("gathered", PAIRS, 2)
        g_copied = tally("g_copied", PAIRS, 2)
        g_step = tally("g_step", PAIRS)
        g_rot = tally("g_rot", PAIRS, 1)
        t_ready = tally("t_ready", PAIRS)
        gt_copied = tally("gt_copied", PAIRS, 1)
        s_ready = tally("s_ready", PAIRS, 1)
        s_read = tally("s_read", 2 * PAIRS, 16)
        p_exp = tally("p_exp", 2 * PAIRS, 2)
        rz_ready = tally("rz_ready", PAIRS)
        p_ready = tally("p_ready", 2 * PAIRS)
        pt_ready = tally("pt_ready", PAIRS, 2)
        pt_copied = tally("pt_copied", PAIRS, 1)
        cw_loaded = [tally(f"cw_loaded{n}", 32 * PAIRS // 4) for n in range(4)]
        pv_done = tally("pv_done", PAIRS, 4)
        o_copied = tally("o_copied", PAIRS, 2)
        q_abs = tally("q_abs", 2 * TILES)
        q_exp = tally("q_exp", 2 * TILES)
        q_ln = tally("q_ln", 2 * TILES)
        q_pass = tally("q_pass", 2 * TILES)
        q_turn = tally("q_turn", 2 * TILES)
        pe_passed = ctx.enter_context(nc.semaphore("pe_passed"))
        dve_passed = ctx.enter_context(nc.semaphore("dve_passed"))
        cleared = ctx.enter_context(nc.semaphore("cleared"))

        relu_user = [sum(pick_ops[j] for j in range(i)) + 3 * kb + h
                     for i in range(TILES) for kb in range(len(key_blocks(i))) for h in range(1, IDX_HEADS)]
        first_pick = {i: sum(pick_ops[j] for j in range(i)) for i in range(TILES + 1)}

        def hold(eng, passed):
            eng.sem_inc(passed, 1)

        def slot(g):
            return 2 * (g % 4) + g // 4

        def released(eng, b, what, back=0):
            k = use[what]
            m_free[k % 2].wait(eng, b, k // 2 + 1 - back * (n_use // 2))

        block = ctx.enter_context(nc.Block())

        @block.sync
        def _(sp):
            with sp.Fori(0, B) as b:
                def windows(m):
                    pv_done.wait(sp, b, m - 3)
                    for k in range(2):
                        w0 = 0 if m < 2 else PAIR * m + UNIT * k - LW
                        sp.dma_start(cw[:, m % 4, k, :], a.c_d[bass.ds(b * L + w0, WIN), :]).then_inc(cw_loaded[m % 4].sem, 16)

                def spread(i):
                    picking.wait(sp, b, first_pick[i + 1])
                    sp.dma_start(a.idx_d[b * TILES + i], idxh[:, i % 2, :]).then_inc(idx_stored.sem, 16)
                    idx_stored.wait(sp, b, 16 * (i + 1))
                    oh_ready.wait(sp, b, PPT * (i - 1))
                    sp.dma_start(idxb[:, i % 2, :], a.idx_d[b * TILES + i].rearrange("t j -> (t j)").partition_broadcast(P)
                                 ).then_inc(idx_spread.sem, 16)

                spread(0)
                for m in range(PAIRS):
                    windows(m)
                    if m % PPT == 2 and m // PPT + 1 < TILES:
                        spread(m // PPT + 1)

        @block.gpsimd
        def _(pool):
            for t in (m_free[0], m_free[1], idx_stored, oh_ready, gathered, g_copied, g_rot, gt_copied,
                      s_ready, s_read, p_exp, pt_ready, pt_copied, pv_done, o_copied):
                pool.sem_inc(t.sem, t.credit)
            CC = a.rankCS[:, 0:1, :].broadcast_to([P, GROUPS, ROPE])
            SS = a.rankCS[:, 1:2, :].broadcast_to([P, GROUPS, ROPE])
            with pool.Fori(0, B) as b:
                for m in range(PAIRS):
                    g = G[:, m % 4]
                    g_copied.wait(pool, b, m + 1)
                    g_rot.wait(pool, b, m)
                    pool.tensor_tensor(gA[:], g[:, :, CKV:64], CC, ALU.mult)
                    pool.tensor_tensor(gB[:, :, 0:HALF], g[:, :, CKV + HALF:64], SS[:, :, 0:HALF], ALU.mult)
                    pool.tensor_tensor(gB[:, :, HALF:ROPE], g[:, :, CKV:CKV + HALF], SS[:, :, HALF:ROPE],
                                       ALU.mult).then_inc(g_step.sem, 1)
                    g_step.wait(pool, b, m + 1)
                    pool.tensor_tensor(g[:, :, CKV:64], gA[:], gB[:], ALU.add).then_inc(g_rot.sem, 1)

        @block.tensor
        def _(pe):
            pe.wait_ge(cleared, 1)
            with pe.Fori(0, B) as b:
                def bank(what):
                    k = use[what]
                    m_free[k % 2].wait(pe, b, k // 2)
                    return psM[k % 2]

                def index_queries(i):
                    M = bank(("qi", i))
                    for n in range(2):
                        mm = pe.matmul(M[:, n * P:(n + 1) * P], a.wiq[:, n * P:(n + 1) * P],
                                       a.hT[:, b, i * P:(i + 1) * P], start=True, stop=True)
                    mm.then_inc(m_ready.sem, 1)

                def index_scores(i, kb, h):
                    o, n = key_blocks(i)[kb]
                    if kb == 0 and h == 0:
                        released(pe, b, ("qi", i))
                    M = bank(("score", i, kb, h))
                    pe.matmul(M[:, 0:n], qi[:, h, :], a.kiT[:, b, o:o + n],
                              start=True, stop=True).then_inc(m_ready.sem, 1)

                def queries(i, x):
                    M = bank(("query", i, x))
                    for h in range(4):
                        mm = pe.matmul(M[:, h * P:(h + 1) * P], a.WQ[:, 4 * x + h, :],
                                       a.cqT[:, b, i * P:(i + 1) * P], start=True, stop=True)
                    mm.then_inc(m_ready.sem, 1)

                def halves(i):
                    for x in range(2):
                        M = bank(("half", i, x))
                        q_turn.wait(pe, b, 2 * i + 2)
                        pe.matmul(M[:], a.selm[:, 1, :], QW[:, x * 512:(x + 1) * 512],
                                  start=True, stop=True).then_inc(m_ready.sem, 1)

                def attn_out(i):
                    M = bank(("attn", i))
                    o_copied.wait(pe, b, PPT * (i + 1))
                    for h in range(H):
                        mm = pe.matmul(M[:, 0:P], a.Wvo[:, h, :], OT[:, i % 2, h:P * H:H],
                                       start=(h == 0), stop=(h == H - 1))
                    mm.then_inc(m_ready.sem, 1)

                def gather(m, groups, scores):
                    if groups[0] == 0:
                        oh_ready.wait(pe, b, m + 1)
                        g_copied.wait(pe, b, m - 1)
                    nch = m // PPT + 1
                    for g in groups:
                        for c in range(nch):
                            for part in range(3):
                                mm = pe.matmul(psG[m % 2][:, slot(g), :], oh[:, m % 2, c, g * P:(g + 1) * P],
                                               featb[:, c, part, :],
                                               start=(c == 0 and part == 0), stop=(c == nch - 1 and part == 2))
                        if g == GROUPS - 1:
                            mm.then_inc(gathered.sem, 1)
                        if g:
                            for what in scores[2 * g - 2:2 * g]:
                                index_scores(*what)

                def turn_keys(m):
                    g_rot.wait(pe, b, m + 1)
                    gt_copied.wait(pe, b, m)
                    o_copied.wait(pe, b, m - 1)
                    for n in range(GROUPS // 2):
                        mm = pe.transpose(psT[:, n, :], G[:, m % 4, 2 * n:2 * n + 2, :].rearrange("p g f -> p (g f)"), a.ident[:])
                    mm.then_inc(t_ready.sem, 1)

                def local_scores(m):
                    i, p = m // PPT, m % PPT
                    q_pass.wait(pe, b, 2 * i + 2)
                    s_read.wait(pe, b, 2 * m)
                    for k in range(2):
                        w0 = 0 if m < 2 else PAIR * m + UNIT * k - LW
                        c0 = (2 * p + k) * P
                        pe.matmul(psS[k][:, P:SCOLS], QR[:, i % 2, c0:c0 + P], a.khT[:, b, w0:w0 + WIN],
                                  start=True, stop=True)

                def turn_probs(m):
                    p_ready.wait(pe, b, 2 * m + 2)
                    pt_copied.wait(pe, b, m)
                    for k in range(2):
                        for n in range(2):
                            mm = pe.transpose(psPT[:, k, n * P:(n + 1) * P], Pb[:, m % 2, k, n * P:(n + 1) * P], a.ident[:])
                    mm.then_inc(pt_ready.sem, 1)

                def picked_scores(m):
                    i, p = m // PPT, m % PPT
                    for x in range(2):
                        released(pe, b, ("half", i, x))
                    gt_copied.wait(pe, b, m + 1)
                    hold(pe, pe_passed)
                    for g in range(GROUPS):
                        r = 64 * (g // 4)
                        c0 = p * 256 + g * 32
                        mm = pe.matmul(psS[g // 4][32 * (g % 4):32 * (g % 4) + 32, 0:P], QA[r:r + 64, i % 2, c0:c0 + 32],
                                       GT[r:r + 64, g % 4, :], start=True, stop=True)
                    mm.then_inc(s_ready.sem, 1)

                def values(m):
                    pt_copied.wait(pe, b, m + 1)
                    cw_loaded[m % 4].wait(pe, b, 32 * (m // 4 + 1))
                    o_copied.wait(pe, b, m)
                    for k in range(2):
                        pe.matmul(psO[0:CKV, k * P:(k + 1) * P], cw[:, m % 4, k, :], PTb[0:WIN, k, P:256],
                                  start=True, stop=False, skip_group_check=True)
                        for g in range(4):
                            mm = pe.matmul(psO[0:CKV, k * P + 32 * g:k * P + 32 * g + 32], G[:, m % 4, slot(4 * k + g), 0:CKV],
                                           PTb[:, k, 32 * g:32 * g + 32], start=False, stop=(g == 3),
                                           skip_group_check=True)
                    mm.then_inc(pv_done.sem, 1)

                def all_scores(i):
                    return [(i, kb, h) for kb in range(len(key_blocks(i))) for h in range(IDX_HEADS)]

                index_queries(0)
                for what in all_scores(0):
                    index_scores(*what)
                queries(0, 0)
                queries(0, 1)
                index_queries(1)
                halves(0)
                for s in range(PAIRS + 2):
                    i = s // PPT
                    scores = all_scores(scored(s)) if scored(s) else []
                    if s < PAIRS:
                        gather(s, range(0, EARLY), scores)
                    if s % PPT == 2 and 1 <= i < TILES:
                        attn_out(i - 1)
                    if 1 <= s <= PAIRS:
                        turn_keys(s - 1)
                        local_scores(s - 1)
                    if s >= 2:
                        turn_probs(s - 2)
                    if s < PAIRS:
                        gather(s, range(EARLY, GROUPS), [])
                    if s % PPT == 3 and i + 1 < TILES:
                        halves(i + 1)
                    if 1 <= s <= PAIRS:
                        picked_scores(s - 1)
                    if s >= 2:
                        values(s - 2)
                    if s % PPT == 2 and i + 2 < TILES:
                        index_queries(i + 2)
                    if s % PPT in (0, 1) and i + 1 < TILES:
                        queries(i + 1, s % PPT)
                attn_out(TILES - 1)

        @block.scalar
        def _(act):
            act.preload_act_table_set("natural_log_exp_and_others")
            act.wait_ge(cleared, 1)
            with act.Fori(0, B) as b:
                def index_queries(i):
                    k = use[("qi", i)]
                    m_ready.wait(act, b, k + 1)
                    q2 = psM[k % 2][:, 0:256].rearrange("p (n t) -> p n t", n=2)
                    act.copy(qi[0:64, 0:IDX_HEADS:2, :], q2[0:64])
                    act.copy(qi[64:128, 1:IDX_HEADS:2, :], q2[64:128]).then_inc(m_free[k % 2].sem, 1)

                def index_scores(i):
                    n_before = 3 * sum(len(key_blocks(j)) for j in range(i))
                    for kb, (o, n) in enumerate(key_blocks(i)):
                        for h in range(1, IDX_HEADS):
                            k = use[("score", i, kb, h)]
                            r = n_before + 3 * kb + h - 1
                            m_ready.wait(act, b, k + 1)
                            if r >= n_before + 2 or i >= 1:
                                picking.wait(act, b, relu_user[r - 2])
                            act.activation(relu[:, r % 2, 0:n], psM[k % 2][:, 0:n], ACT.Relu).then_inc(m_free[k % 2].sem, 1)

                def queries(i, x):
                    k = use[("query", i, x)]
                    n = 2 * i + x
                    m_ready.wait(act, b, k + 1)
                    s_read.wait(act, b, 2 * PPT * (i - 1))
                    q4 = psM[k % 2][0:CKV, :].rearrange("p (h t) -> p h t", h=4)
                    qr = QR[0:CKV, i % 2, :].rearrange("p (t h) -> p h t", h=H)[:, 4 * x:4 * x + 4, :]
                    act.copy(qr, q4)
                    qw = QW[0:CKV, :].rearrange("p (t h) -> p h t", h=H)[:, 4 * x:4 * x + 4, :]
                    act.copy(qw, q4)
                    if n:
                        released(act, b, ("query", (n - 1) // 2, (n - 1) % 2))
                    act.activation(qex[64:128, :], psM[k % 2][64:128, :], ACT.Abs).then_inc(q_abs.sem, 1)
                    q_abs.wait(act, b, n + 1)
                    act.activation(qex[64:128, :], qex[64:128, :], ACT.Exp, scale=-1.0).then_inc(q_exp.sem, 1)
                    q_exp.wait(act, b, n + 1)
                    act.activation(qex[64:128, :], qex[64:128, :], ACT.Ln, bias=1.0).then_inc(q_ln.sem, 1)

                def halves(i):
                    for x in range(2):
                        k = use[("half", i, x)]
                        m_ready.wait(act, b, k + 1)
                        s_read.wait(act, b, 2 * PPT * (i - 1))
                        act.copy(QA[:, i % 2, x * 512:(x + 1) * 512], psM[k % 2][:]).then_inc(m_free[k % 2].sem, 1)

                def copy_rows(m):
                    gathered.wait(act, b, m + 1)
                    pv_done.wait(act, b, m - 3)
                    act.copy(G[:, m % 4], psG[m % 2][:]).then_inc(g_copied.sem, 1)

                def copy_turned(m):
                    t_ready.wait(act, b, m + 1)
                    s_ready.wait(act, b, m)
                    act.copy(GT[:], psT[:]).then_inc(gt_copied.sem, 1)

                def copy_probs(m):
                    pt_ready.wait(act, b, m + 1)
                    pv_done.wait(act, b, m)
                    act.copy(PTb[:], psPT[:]).then_inc(pt_copied.sem, 1)

                def probs(m):
                    for k in range(2):
                        s_read.wait(act, b, 2 * m + k + 1)
                        pt_ready.wait(act, b, m - 1)
                        act.activation(Pb[:, m % 2, k, 0:SCOLS], Sm[:, k, :], ACT.Exp, scale=-1.0,
                                       bias=nmx[:, m % 2, k:k + 1], accum_out=Z[:, m % 2, k:k + 1]).then_inc(p_exp.sem, 1)

                def copy_out(m):
                    i, p = m // PPT, m % PPT
                    pv_done.wait(act, b, m + 1)
                    if i >= 2:
                        released(act, b, ("attn", i - 2))
                    else:
                        released(act, b, ("attn", i + TILES - 2), 1)
                    act.copy(OT[:, i % 2, p * 256:(p + 1) * 256], psO[0:CKV, 0:256]).then_inc(o_copied.sem, 1)

                index_queries(0)
                index_scores(0)
                queries(0, 0)
                queries(0, 1)
                index_queries(1)
                halves(0)
                for s in range(PAIRS + 2):
                    i = s // PPT
                    if scored(s):
                        index_scores(scored(s))
                    if 1 <= s <= PAIRS:
                        copy_turned(s - 1)
                    if s >= 2:
                        copy_probs(s - 2)
                    if s < PAIRS:
                        copy_rows(s)
                    if s % PPT == 3 and i + 1 < TILES:
                        halves(i + 1)
                    if 1 <= s <= PAIRS:
                        probs(s - 1)
                    if s >= 2:
                        copy_out(s - 2)
                    if s % PPT == 2 and i + 2 < TILES:
                        index_queries(i + 2)
                    if s % PPT in (0, 1) and i + 1 < TILES:
                        queries(i + 1, s % PPT)

        @block.vector
        def _(dve):
            dve.memset(QR[32:64], 0.0)
            dve.memset(QW[32:64], 0.0)
            dve.memset(qi[:], 0.0)
            dve.memset(Pb[:, :, :, SCOLS:256], 0.0).then_inc(cleared, 1)
            with dve.Fori(0, B) as b:
                step = [0]

                def pick(ins):
                    ins.then_inc(picking.sem, 1)
                    step[0] += 1
                    picking.wait(dve, b, step[0])
                    hold(dve, dve_passed)

                def index(i):
                    n_before = 3 * sum(len(key_blocks(j)) for j in range(i))
                    for kb, (o, n) in enumerate(key_blocks(i)):
                        k = use[("score", i, kb, 0)]
                        m_ready.wait(dve, b, k + 1)
                        dve.tensor_scalar(isum[:, o:o + n], psM[k % 2][:, 0:n], 0.0, a.wix[:, 0:1], ALU.max,
                                          ALU.mult).then_inc(m_free[k % 2].sem, 1)
                        released(dve, b, ("score", i, kb, 0))
                        for h in range(1, IDX_HEADS):
                            r = n_before + 3 * kb + h - 1
                            released(dve, b, ("score", i, kb, h))
                            pick(dve.scalar_tensor_tensor(out=isum[:, o:o + n], in0=relu[:, r % 2, 0:n],
                                                          scalar=a.wix[:, h:h + 1], in1=isum[:, o:o + n],
                                                          op0=ALU.mult, op1=ALU.add))
                    lo = max(0, P * i - LW)
                    hi = P * i + P - LW
                    pick(dve.tensor_tensor(isum[:, lo:hi], isum[:, lo:hi], a.imask[:, P - (hi - lo):P], ALU.add))

                def top_values(i, r):
                    n = P * i + P - LW
                    pick(dve.max(vals[:], isum[:, 0:n]))

                def top_places(i, r):
                    n = P * i + P - LW
                    pick(dve.max_index(idx16[:, 8 * r:8 * r + 8], vals[:], isum[:, 0:n]))
                    if r < TOP_ROUNDS - 1:
                        pick(dve.match_replace(isum[:, 0:n], vals[:], isum[:, 0:n], NEGMAX))
                        return
                    idx_stored.wait(dve, b, 16 * (i - 1))
                    if i == 0:
                        pick(dve.tensor_copy(idxf[:], idx16[:]))
                        pick(dve.tensor_tensor(idxf[:], idxf[:], a.future[:, 0, :], ALU.mult))
                        pick(dve.tensor_tensor(idxh[:, i % 2, :], idxf[:], a.future[:, 1, :], ALU.add))
                    else:
                        pick(dve.tensor_copy(idxh[:, i % 2, :], idx16[:]))

                def queries(i, x):
                    k = use[("query", i, x)]
                    n = 2 * i + x
                    q_ln.wait(dve, b, n + 1)
                    if n:
                        q_turn.wait(dve, b, n)
                    sp_th = qsp[64:128].rearrange("p t h -> p h t")
                    dve.scalar_tensor_tensor(out=sp_th, in0=psM[k % 2][64:128, :].rearrange("p (h t) -> p h t", h=4),
                                             scalar=0.0, in1=qex[64:128, :].rearrange("p (h t) -> p h t", h=4),
                                             op0=ALU.max, op1=ALU.add).then_inc(m_free[k % 2].sem, 1)
                    released(dve, b, ("query", i, x))
                    t0 = i * P
                    tr = [a.tabs[64:128, j, t0:t0 + P].unsqueeze(2).broadcast_to([64, P, 4]) for j in range(2)]
                    qr = QR[64:128, i % 2, :].rearrange("p (t h) -> p t h", h=H)[:, :, 4 * x:4 * x + 4]
                    qw = QW[64:128, :].rearrange("p (t h) -> p t h", h=H)[:, :, 4 * x:4 * x + 4]
                    dve.tensor_tensor(qr, qsp[64:128], tr[1], ALU.mult).then_inc(q_pass.sem, 1)
                    dve.tensor_tensor(qw, qsp[64:128], tr[0], ALU.mult).then_inc(q_turn.sem, 1)

                def onehot(m):
                    i, p = m // PPT, m % PPT
                    idx_spread.wait(dve, b, 16 * (i + 1))
                    gathered.wait(dve, b, m - 1)
                    for c in range(i + 1):
                        last = dve.tensor_scalar(oh[:, m % 2, c, :], idxb[:, i % 2, p * 1024:(p + 1) * 1024],
                                                 a.keys[:, c:c + 1], None, ALU.is_equal)
                    last.then_inc(oh_ready.sem, 1)

                def masked_max(m):
                    s_ready.wait(dve, b, m + 1)
                    p_exp.wait(dve, b, 2 * m)
                    hold(dve, dve_passed)
                    for k in range(2):
                        dve.tensor_tensor_reduce(out=Sm[:, k, :], in0=psS[k][:, 0:SCOLS], in1=a.umask[:, 0 if m < 2 else 1, :],
                                                 scale=-ATTN_SCALE, scalar=-NEGMAX, op0=ALU.add, op1=ALU.min,
                                                 accum_out=nmx[:, m % 2, k:k + 1]).then_inc(s_read.sem, 1)

                def normalize(m):
                    p_exp.wait(dve, b, 2 * m + 2)
                    dve.reciprocal(rz[:, m % 2, :], Z[:, m % 2, :]).then_inc(rz_ready.sem, 1)
                    rz_ready.wait(dve, b, m + 1)
                    for k in range(2):
                        dve.tensor_scalar(Pb[:, m % 2, k, 0:SCOLS], Pb[:, m % 2, k, 0:SCOLS], rz[:, m % 2, k:k + 1], None,
                                          ALU.mult).then_inc(p_ready.sem, 1)

                def residual(i):
                    k = use[("attn", i)]
                    m_ready.wait(dve, b, k + 1)
                    xs = a.x1T[:, b, i * P:(i + 1) * P]
                    dve.scalar_tensor_tensor(out=xs, in0=psM[k % 2][:, 0:P], scalar=a.mod[:, 2, bass.ds(b, 1)], in1=xs,
                                             op0=ALU.mult, op1=ALU.add).then_inc(m_free[k % 2].sem, 1)

                def top_round(i, r):
                    top_values(i, r)
                    top_places(i, r)

                index(0)
                for r in range(TOP_ROUNDS):
                    top_round(0, r)
                queries(0, 0)
                queries(0, 1)
                gathered.wait(dve, b, 0)
                dve.tensor_copy(featb[:], a.feat[:, bass.ds(b * TILES, TILES), :, :])
                onehot(0)
                for s in range(PAIRS + 2):
                    i = s // PPT
                    j, r = (s + 1) // PPT + 1, (s + 1) % PPT
                    if scored(s):
                        index(scored(s))
                    if s + 1 < PAIRS:
                        onehot(s + 1)
                    if s == 0:
                        top_round(1, 0)
                    if s % PPT == 2 and i >= 1:
                        residual(i - 1)
                    if 1 <= s <= PAIRS:
                        masked_max(s - 1)
                    if j < TILES:
                        top_values(j, r)
                    if 1 <= s <= PAIRS:
                        normalize(s - 1)
                    if j < TILES:
                        top_places(j, r)
                    if s % PPT in (0, 1) and i + 1 < TILES:
                        queries(i + 1, s % PPT)
                if (PAIRS + 1) % PPT == 1:
                    residual(TILES - 1)
                assert step[0] == picking.per, (step[0], picking.per)


def stack_blocks(nc, top, ins, consts, out, ident, ones, mod, x1T, wqkv, wo, w1, w2, fvec):
    def sb(name, shape, dt=F32):
        return top.enter_context(nc.sbuf_tensor(name, list(shape), dt))

    X = sb("X", [P, B, L + 1])
    Y = sb("Y", [P, B, L + 1])
    xpos = sb("xpos", [P, TILES, 4, DH])
    xtab = sb("xtab", [P, DEPTH, TILES, 4, DH])
    qks = sb("qks", [P, DEPTH, 2, DH])
    wmask = sb("wmask", [P, 2, P])
    eps = sb("eps", [P, 1])

    norm_block(nc, ins, consts, ones, mod, x1T, X, Y, xpos, xtab, qks, wmask, eps)
    sems = {}

    def sem(name):
        if name not in sems:
            sems[name] = top.enter_context(nc.semaphore(name))
        return sems[name]

    for l in range(DEPTH):
        window_block(nc, l, sem, ident, X, Y, xtab, wmask, wqkv, wo)
        mlp_block(nc, l, sem, ones, X, Y, w1, w2, fvec, eps)
    final_block(nc, ident, mod, x1T, X, out)


def norm_block(nc, ins, consts, ones, mod, x1T, X, Y, xpos, xtab, qks, wmask, eps):
    with ExitStack() as ctx:
        def sb(name, shape, dt=F32):
            return ctx.enter_context(nc.sbuf_tensor(name, list(shape), dt))

        def sem(name):
            return ctx.enter_context(nc.semaphore(name))

        NQ = B * L // 512
        zc = sb("zc", [P, NQ, 512])
        sq = sb("sq", [P, NQ, 512])
        rs = sb("rs", [P, NQ, 512])
        ps = [ctx.enter_context(nc.psum_tensor(f"stat{i}", [P, 512], F32)) for i in range(2 * NQ)]
        loaded, mean_done, centred, squared, var_done = (
            sem("loaded"), sem("mean_done"), sem("centred"), sem("squared"), sem("var_done"))
        logged, rstd_done, scaled, folded, eps_set = (
            sem("logged"), sem("rstd_done"), sem("scaled"), sem("folded"), sem("eps_set"))
        x1 = x1T[:].rearrange("p b t -> p (b t)")
        block = ctx.enter_context(nc.Block())

        @block.sync
        def _(sp):
            sp.dma_start(xpos[:], consts["xpos"]).then_inc(loaded, 16)
            sp.dma_start(wmask[:], consts["wmask"]).then_inc(loaded, 16)
            for l in range(DEPTH):
                for k, name in enumerate(("L0_ffn_q_scale", "L0_ffn_k_scale")):
                    sp.dma_start(qks[:, l, k, :], ins[name][l].partition_broadcast(P)).then_inc(loaded, 16)
            sp.wait_ge(loaded, 16 * (2 + 2 * DEPTH))

        @block.tensor
        def _(pe):
            for q in range(NQ):
                pe.matmul(ps[q][:], ones[:], x1[:, q * 512:(q + 1) * 512], start=True, stop=True).then_inc(mean_done, 1)
            for q in range(NQ):
                pe.wait_ge(squared, q + 1)
                pe.matmul(ps[NQ + q][:], ones[:], sq[:, q, :], start=True, stop=True).then_inc(var_done, 1)

        @block.scalar
        def _(act):
            for q in range(NQ):
                act.wait_ge(centred, q + 1)
                act.activation(sq[:, q, :], zc[:, q, :], ACT.Square).then_inc(squared, 1)
            act.wait_ge(eps_set, 1)
            for q in range(NQ):
                act.wait_ge(var_done, q + 1)
                act.activation(rs[:, q, :], ps[NQ + q][:], ACT.Ln, bias=eps[:, 0:1]).then_inc(logged, 1)
            for q in range(NQ):
                act.wait_ge(logged, q + 1)
                act.activation(rs[:, q, :], rs[:, q, :], ACT.Exp, scale=-0.5).then_inc(rstd_done, 1)

        @block.vector
        def _(dve):
            dve.memset(eps[:], LN_EPS).then_inc(eps_set, 1)
            dve.memset(X[:, :, 0:1], 0.0)
            dve.memset(Y[:, :, 0:1], 0.0)
            for q in range(NQ):
                dve.wait_ge(mean_done, q + 1)
                dve.tensor_tensor(zc[:, q, :], x1[:, q * 512:(q + 1) * 512], ps[q][:], ALU.subtract).then_inc(centred, 1)
            dve.wait_ge(loaded, 16 * (2 + 2 * DEPTH))
            for l in range(DEPTH):
                for k in range(2):
                    dve.tensor_tensor(xtab[:, l, :, k, :], xpos[:, :, k, :],
                                      qks[:, l, k:k + 1, :].broadcast_to([P, TILES, DH]), ALU.mult)
                    for o in (0, 32):
                        dve.tensor_tensor(xtab[:, l, :, 2 + k, o:o + 32], xpos[:, :, 2 + k, o:o + 32],
                                          qks[:, l, k:k + 1, 32 - o:64 - o].broadcast_to([P, TILES, 32]), ALU.mult)
            for q in range(NQ):
                b, o = q // 2, 1 + 512 * (q % 2)
                dve.wait_ge(rstd_done, q + 1)
                dve.tensor_tensor(zc[:, q, :], zc[:, q, :], rs[:, q, :], ALU.mult).then_inc(scaled, 1)
                dve.wait_ge(scaled, q + 1)
                dve.tensor_scalar(X[:, b, o:o + 512], zc[:, q, :], mod[:, 4, b:b + 1], mod[:, 3, b:b + 1],
                                  ALU.mult, ALU.add)


V_RING = 5


def window_block(nc, l, sem, ident, X, Y, xtab, wmask, wqkv, wo):
    tag = f"_{l}"
    with ExitStack() as ctx:
        def sb(name, shape, dt=F32):
            return ctx.enter_context(nc.sbuf_tensor(name + tag, list(shape), dt))

        def tally(name, per, credit=0):
            return Tally(sem(name), per, credit, l)

        def psum(name, shape):
            return ctx.enter_context(nc.psum_tensor(name + tag, list(shape), F32))

        hs = sb("hs", [P, 2, P])
        sq = sb("sq", [P, 2, INNER])
        rA = sb("rA", [P, 2, INNER])
        rB = sb("rB", [P, 2, INNER])
        ss = sb("ss", [P, 2, 2 * H])
        sg = sb("sg", [P, 2 * H])
        rn = sb("rn", [P, 2, 2 * H])
        mhalf = sb("mhalf", [P, 2 * H])
        qk = sb("qk", [P, 2, 2 * INNER])
        qT = sb("qT", [P, 2, 4, P])
        kT = sb("kT", [P, 2, 4, WINDOW + P])
        vfull = sb("vfull", [P, V_RING, INNER])
        vhalf = sb("vhalf", [P, V_RING, INNER])
        Sm = sb("Sm", [P, H, P])
        nmx = sb("nmx", [P, 2, H])
        Z = sb("Z", [P, 2, H])
        rz = sb("rz", [P, 2, H])
        Pm = sb("Pm", [P, 2, H, P])
        PT = sb("PT", [P, H, P])
        OT = sb("OT", [P, 4, P])
        psQ = [psum(f"psQ{k}", [P, INNER]) for k in range(2)]
        psV = psum("psV", [P, INNER])
        psT = [psum(f"psTT{k}", [P, 4, P]) for k in range(2)]
        psS = [psum(f"psSS{k}", [P, 4, P]) for k in range(2)]
        psO = psum("psOO", [P, 4, P])

        n = B * TILES
        staged = tally("staged", n)
        q_ready = tally("q_ready", n, 2)
        q_squared = tally("q_squared", 2 * n, 2)
        q_rotated = tally("q_rotated", n, 1)
        q_summed = tally("q_summed", n)
        sq_read = tally("sq_read", n, 1)
        ss_safe = tally("ss_safe", n)
        rn_ready = tally("rn_ready", n)
        qk_ready = tally("qk_ready", n, 1)
        v_ready = tally("v_ready", 2 * n)
        v_free = tally("v_free", 2 * n, 1)
        t_ready = tally("t_ready", 2 * n)
        t_free = tally("t_free", 2 * n, 1)
        k_prev = tally("k_prev", n)
        s_ready = tally("s_ready2", n, 2)
        s_read = tally("s_read2", n * H, H)
        p_exp = tally("p_exp2", n * H, H)
        rz_ready = tally("rz_ready2", n)
        p_ready = tally("p_ready2", n)
        o_ready = tally("o_ready", n, V_RING)
        o_copied = tally("o_copied2", n, 1)
        cleared = sem("cleared2")

        v_use = {w: k for k, w in enumerate([w for s in range(n + 4) for w in
                                             ([("y", s - 4)] if s >= 4 else []) + ([("v", s)] if s < n else [])])}
        t_use = {w: k for k, w in enumerate([w for s in range(n + 3) for w in
                                             ([("qk", s - 1)] if 1 <= s <= n else []) + ([("p", s - 3)] if s >= 3 else [])])}
        block = ctx.enter_context(nc.Block())

        @block.gpsimd
        def _(pool):
            if l == 0:
                for t in (q_ready, q_squared, q_rotated, sq_read, qk_ready, v_free, t_free, s_ready, s_read, p_exp, o_ready,
                          o_copied):
                    pool.sem_inc(t.sem, t.credit)
            pool.wait_ge(cleared, l + 1)
            def norms(i):
                sq_read.wait(pool, 0, i + 1)
                pool.tensor_scalar(sg[:], ss[:, i % 2, :], 1e-24, None, ALU.max).then_inc(ss_safe.sem, 1)
                ss_safe.wait(pool, 0, i + 1)
                qk_ready.wait(pool, 0, i - 1 if i else 0)
                pool.tensor_tensor(rn[:, i % 2, :], sg[:], mhalf[:], ALU.pow).then_inc(rn_ready.sem, 1)

            def probs(i):
                rz_ready.wait(pool, 0, i + 1)
                pool.tensor_tensor(Pm[:, i % 2], Pm[:, i % 2], rz[:, i % 2, :].unsqueeze(2).broadcast_to([P, H, P]),
                                   ALU.mult).then_inc(p_ready.sem, 1)

            for s in range(n + 3):
                if s >= 3:
                    probs(s - 3)
                if s < n:
                    norms(s)

        @block.tensor
        def _(pe):
            def project_qk(i):
                staged.wait(pe, 0, i + 1)
                q_squared.wait(pe, 0, 2 * i)
                q_rotated.wait(pe, 0, i)
                for k in range(2):
                    mm = pe.matmul(psQ[k][:], hs[:, i % 2, :], wqkv[:, l, k * INNER:(k + 1) * INNER], start=True, stop=True)
                mm.then_inc(q_ready.sem, 1)

            def project_v(i):
                v_free.wait(pe, 0, v_use["v", i])
                pe.matmul(psV[:], hs[:, i % 2, :], wqkv[:, l, 2 * INNER:3 * INNER], start=True, stop=True).then_inc(v_ready.sem, 1)

            def turn_qk(i):
                qk_ready.wait(pe, 0, i + 1)
                t_free.wait(pe, 0, t_use["qk", i])
                for c in range(8):
                    mm = pe.transpose(psT[c // 4][:, c % 4, :], qk[:, i % 2, c * P:(c + 1) * P], ident[:])
                mm.then_inc(t_ready.sem, 1)

            def scores(i):
                s_read.wait(pe, 0, H * i)
                k_prev.wait(pe, 0, i + 1)
                t_free.wait(pe, 0, t_use["qk", i] + 1)
                for h in range(H):
                    r = 64 * (h % 2)
                    for w in range(2):
                        mm = pe.matmul(psS[h % 2][64 * w:64 * w + 64, h // 2, :], qT[r:r + 64, i % 2, h // 2, 64 * w:64 * w + 64],
                                       kT[r:r + 64, i % 2, h // 2, 64 * w:64 * w + P], start=True, stop=True)
                mm.then_inc(s_ready.sem, 1)

            def turn_probs(i):
                p_ready.wait(pe, 0, i + 1)
                t_free.wait(pe, 0, t_use["p", i])
                for h in range(H):
                    mm = pe.transpose(psT[h // 4][:, h % 4, :], Pm[:, i % 2, h, :], ident[:])
                mm.then_inc(t_ready.sem, 1)

            def attend(i):
                o_copied.wait(pe, 0, i)
                t_free.wait(pe, 0, t_use["p", i] + 1)
                for h in range(H):
                    for w in range(2):
                        v = vfull if w else vhalf
                        mm = pe.matmul(psO[64 * (h % 2):64 * (h % 2) + 64, h // 2, 64 * w:64 * w + 64],
                                       v[:, i % V_RING, h * DH:(h + 1) * DH], PT[:, h, 64 * w:64 * w + 64], start=True, stop=True)
                mm.then_inc(o_ready.sem, 1)

            def project_out(i):
                o_copied.wait(pe, 0, i + 1)
                v_free.wait(pe, 0, v_use["y", i])
                for c in range(4):
                    mm = pe.matmul(psV[:, 0:P], wo[:, l, c, :], OT[:, c, :], start=(c == 0), stop=(c == 3))
                mm.then_inc(v_ready.sem, 1)

            for s in range(n + 4):
                if s < n:
                    project_qk(s)
                if 1 <= s <= n:
                    turn_qk(s - 1)
                if s >= 4:
                    project_out(s - 4)
                if 3 <= s <= n + 2:
                    turn_probs(s - 3)
                if 1 <= s <= n:
                    scores(s - 1)
                if s < n:
                    project_v(s)
                if 3 <= s <= n + 2:
                    attend(s - 3)

        @block.scalar
        def _(act):
            act.preload_act_table_set("natural_log_exp_and_others")
            act.wait_ge(cleared, l + 1)
            def stage(i):
                v_ready.wait(act, 0, v_use["v", i - 2] + 1) if i >= 2 else None
                b, o = divmod(i * P, L)
                act.copy(hs[0:64, i % 2, :], X[0:64, b, 1 + o:1 + o + P])
                act.copy(hs[64:128, i % 2, :], X[64:128, b, o:o + P]).then_inc(staged.sem, 1)

            def squares(i):
                q_ready.wait(act, 0, i + 1)
                sq_read.wait(act, 0, i)
                act.activation(sq[:, 0, :], psQ[0][:], ACT.Square).then_inc(q_squared.sem, 1)
                act.activation(sq[:, 1, :], psQ[1][:], ACT.Square).then_inc(q_squared.sem, 1)

            def copy_values(i):
                v_ready.wait(act, 0, v_use["v", i] + 1)
                o_ready.wait(act, 0, i + 1 - V_RING)
                act.copy(vfull[:, i % V_RING, :], psV[:])
                act.copy(vhalf[64:128, i % V_RING, :], psV[0:64, :])
                act.copy(vhalf[0:64, (i + 1) % V_RING, :], psV[64:128, :]).then_inc(v_free.sem, 1)

            def turned(i):
                t_ready.wait(act, 0, t_use["qk", i] + 1)
                s_ready.wait(act, 0, i - 1)
                act.copy(qT[:, i % 2], psT[0][:])
                act.copy(kT[:, i % 2, :, WINDOW:WINDOW + P], psT[1][:]).then_inc(t_free.sem, 1)

            def probs(i):
                if i >= 2:
                    t_ready.wait(act, 0, t_use["p", i - 2] + 1)
                for h in range(H):
                    s_read.wait(act, 0, H * i + h + 1)
                    act.activation(Pm[:, i % 2, h, :], Sm[:, h, :], ACT.Exp, scale=-1.0, bias=nmx[:, i % 2, h:h + 1],
                                   accum_out=Z[:, i % 2, h:h + 1]).then_inc(p_exp.sem, 1)

            def turned_probs(i):
                t_ready.wait(act, 0, t_use["p", i] + 1)
                o_ready.wait(act, 0, i)
                act.copy(PT[:, 0:4], psT[0][:])
                act.copy(PT[:, 4:8], psT[1][:]).then_inc(t_free.sem, 1)

            def outputs(i):
                o_ready.wait(act, 0, i + 1)
                act.copy(OT[:], psO[:]).then_inc(o_copied.sem, 1)

            stage(0)
            for s in range(n + 3):
                if s < n:
                    squares(s)
                if 1 <= s <= n:
                    turned(s - 1)
                if s >= 3:
                    turned_probs(s - 3)
                if s + 1 < n:
                    stage(s + 1)
                if 2 <= s <= n + 1:
                    probs(s - 2)
                if s < n:
                    copy_values(s)
                if s >= 3:
                    outputs(s - 3)

        @block.vector
        def _(dve):
            dve.memset(mhalf[:], -0.5)
            dve.memset(vhalf[0:64, 0, :], 0.0)
            dve.memset(kT[:, 1], 0.0).then_inc(cleared, 1)
            dve.wait_ge(cleared, l + 1)
            def squares_summed(i):
                q_squared.wait(dve, 0, 2 * i + 2)
                dve.tensor_reduce(ss[:, i % 2, :], sq[:].rearrange("p k (h d) -> p (k h) d", d=DH), AX_X,
                                  ALU.add).then_inc(sq_read.sem, 1)

            def rotate(i):
                qk_ready.wait(dve, 0, i)
                for k in range(2):
                    v = psQ[k][:].rearrange("p (h d) -> p h d", h=H)
                    dve.tensor_tensor(rA[:, k].rearrange("p (h d) -> p h d", h=H), v,
                                      xtab[:, l, i % TILES, k:k + 1, :].broadcast_to([P, H, DH]), ALU.mult)
                    o = rB[:, k].rearrange("p (h d) -> p h d", h=H)
                    for c in (0, 32):
                        last = dve.tensor_tensor(o[:, :, c:c + 32], v[:, :, 32 - c:64 - c],
                                                 xtab[:, l, i % TILES, 2 + k:3 + k, c:c + 32].broadcast_to([P, H, 32]), ALU.mult)
                last.then_inc(q_rotated.sem, 1)
                q_rotated.wait(dve, 0, i + 1)
                dve.tensor_tensor(rA[:], rA[:], rB[:], ALU.add).then_inc(q_summed.sem, 1)

            def normed(i):
                q_summed.wait(dve, 0, i + 1)
                rn_ready.wait(dve, 0, i + 1)
                if i >= 2:
                    t_ready.wait(dve, 0, t_use["qk", i - 2] + 1)
                dve.tensor_tensor(qk[:, i % 2].rearrange("p (g d) -> p g d", d=DH), rA[:].rearrange("p k (h d) -> p (k h) d", d=DH),
                                  rn[:, i % 2, :].unsqueeze(2).broadcast_to([P, 2 * H, DH]), ALU.mult).then_inc(qk_ready.sem, 1)

            def previous_keys(i):
                t_free.wait(dve, 0, t_use["qk", i] + 1 if i == 0 else t_use["qk", i - 1] + 1)
                s_ready.wait(dve, 0, i - 1)
                dve.tensor_copy(kT[:, i % 2, :, 0:WINDOW], kT[:, (i + 1) % 2, :, P:P + WINDOW]).then_inc(k_prev.sem, 1)

            def masked_max(i):
                s_ready.wait(dve, 0, i + 1)
                p_exp.wait(dve, 0, H * i)
                for h in range(H):
                    dve.tensor_tensor_reduce(out=Sm[:, h, :], in0=psS[h % 2][:, h // 2, :], in1=wmask[:, min(i % TILES, 1), :],
                                             scale=-QK_SCALE, scalar=-NEGMAX, op0=ALU.add, op1=ALU.min,
                                             accum_out=nmx[:, i % 2, h:h + 1]).then_inc(s_read.sem, 1)

            def sums(i):
                p_exp.wait(dve, 0, H * (i + 1))
                dve.reciprocal(rz[:, i % 2, :], Z[:, i % 2, :]).then_inc(rz_ready.sem, 1)

            def residual(i):
                v_ready.wait(dve, 0, v_use["y", i] + 1)
                b, o = divmod(i * P, L)
                dve.tensor_tensor(Y[:, b, 1 + o:1 + o + P], psV[:, 0:P], X[:, b, 1 + o:1 + o + P], ALU.add).then_inc(v_free.sem, 1)

            for s in range(n + 4):
                if 3 <= s <= n + 2:
                    sums(s - 3)
                if 2 <= s <= n + 1:
                    masked_max(s - 2)
                if 1 <= s <= n:
                    previous_keys(s - 1)
                if s < n:
                    squares_summed(s)
                if s >= 4:
                    residual(s - 4)
                if s < n:
                    rotate(s)
                    normed(s)


def mlp_block(nc, l, sem, ones, X, Y, w1, w2, fvec, eps):
    tag = f"_m{l}"
    with ExitStack() as ctx:
        def sb(name, shape, dt=F32):
            return ctx.enter_context(nc.sbuf_tensor(name + tag, list(shape), dt))

        def tally(name, per, credit=0):
            return Tally(sem(name), per, credit, l)

        def psum(name):
            return ctx.enter_context(nc.psum_tensor(name + tag, [P, 512], F32))

        blocks = [(b, o) for b in range(B) for o in range(0, L, 512)]
        NB = len(blocks)
        hs = sb("hs", [P, NB, 512])
        zc = sb("zc", [P, NB, 512])
        sq = sb("sq", [P, NB, 512])
        rs = sb("rs", [P, NB, 512])
        hn = sb("hn", [P, NB, 512])
        gl = sb("gl", [P, 2, 512])
        u = sb("u", [P, NB, 3, 512])
        psa = [psum(f"psa{q}") for q in range(2)]
        psg = [psum(f"psg{q}") for q in range(2)]
        psy = [psum(f"psy{q}") for q in range(2)]
        stat = [psum(f"stat{q}") for q in range(2)] + psy

        staged = tally("mlp_staged", NB)
        mean_done = tally("mlp_mean_done", NB)
        centred = tally("mlp_centred", NB)
        squared = tally("mlp_squared", NB)
        var_done = tally("mlp_var_done", NB)
        logged = tally("mlp_logged", NB)
        rstd = tally("mlp_rstd", NB)
        scaled = tally("mlp_scaled", NB)
        h_ready = tally("mlp_h_ready", NB)
        hid_ready = tally("mlp_hid_ready", 3 * NB)
        gelu = tally("mlp_gelu", 3 * NB)
        gated = tally("mlp_gated", 3 * NB, 2)
        y_ready = tally("mlp_y_ready", NB)
        y_read = tally("mlp_y_read", NB, 2)
        block = ctx.enter_context(nc.Block())

        @block.gpsimd
        def _(pool):
            if l == 0:
                for t in (gated, y_read):
                    pool.sem_inc(t.sem, t.credit)

        @block.tensor
        def _(pe):
            def hidden(q):
                h_ready.wait(pe, 0, q + 1)
                for c, (o, w) in enumerate(HCH):
                    k = 3 * q + c
                    gated.wait(pe, 0, k - 1)
                    pe.matmul(psg[k % 2][0:w, :], w1[:, l, HID + o:HID + o + w], hn[:, q, :], start=True, stop=True)
                    pe.matmul(psa[k % 2][0:w, :], w1[:, l, o:o + w], hn[:, q, :], start=True, stop=True
                              ).then_inc(hid_ready.sem, 1)

            def output(q):
                logged.wait(pe, 0, NB)
                y_read.wait(pe, 0, q - 1)
                gated.wait(pe, 0, 3 * q + 3)
                for c, (o, w) in enumerate(HCH):
                    mm = pe.matmul(psy[q % 2][:], w2[0:w, l, c, :], u[0:w, q, c, :], start=(c == 0), stop=(c == 2))
                mm.then_inc(y_ready.sem, 1)

            for q in range(NB):
                staged.wait(pe, 0, q + 1)
                pe.matmul(stat[q][:], ones[:], hs[:, q, :], start=True, stop=True).then_inc(mean_done.sem, 1)
            for q in range(NB):
                squared.wait(pe, 0, q + 1)
                pe.matmul(stat[q][:], ones[:], sq[:, q, :], start=True, stop=True).then_inc(var_done.sem, 1)
            for q in range(NB):
                hidden(q)
                if q:
                    output(q - 1)
            output(NB - 1)

        @block.scalar
        def _(act):
            for q, (b, o) in enumerate(blocks):
                act.copy(hs[0:64, q, :], Y[0:64, b, 1 + o:1 + o + 512])
                act.copy(hs[64:128, q, :], Y[64:128, b, o:o + 512]).then_inc(staged.sem, 1)
            for q in range(NB):
                centred.wait(act, 0, q + 1)
                act.activation(sq[:, q, :], zc[:, q, :], ACT.Square).then_inc(squared.sem, 1)
            for q in range(NB):
                var_done.wait(act, 0, q + 1)
                act.activation(rs[:, q, :], stat[q][:], ACT.Ln, bias=eps[:, 0:1]).then_inc(logged.sem, 1)
                logged.wait(act, 0, q + 1)
                act.activation(rs[:, q, :], rs[:, q, :], ACT.Exp, scale=-0.5).then_inc(rstd.sem, 1)
            for k in range(3 * NB):
                w = HCH[k % 3][1]
                hid_ready.wait(act, 0, k + 1)
                gated.wait(act, 0, k - 1)
                act.activation(gl[0:w, k % 2, :], psg[k % 2][0:w, :], ACT.Gelu,
                               bias=fvec[0:w, l, 6 + k % 3:7 + k % 3]).then_inc(gelu.sem, 1)

        @block.vector
        def _(dve):
            def residual(q):
                b, o = blocks[q]
                y_ready.wait(dve, 0, q + 1)
                dve.scalar_tensor_tensor(out=X[:, b, 1 + o:1 + o + 512], in0=psy[q % 2][:], scalar=fvec[:, l, 2:3],
                                         in1=Y[:, b, 1 + o:1 + o + 512], op0=ALU.add, op1=ALU.add).then_inc(y_read.sem, 1)

            for q in range(NB):
                mean_done.wait(dve, 0, q + 1)
                dve.tensor_tensor(zc[:, q, :], hs[:, q, :], stat[q][:], ALU.subtract).then_inc(centred.sem, 1)
            for q in range(NB):
                rstd.wait(dve, 0, q + 1)
                dve.tensor_tensor(zc[:, q, :], zc[:, q, :], rs[:, q, :], ALU.mult).then_inc(scaled.sem, 1)
                scaled.wait(dve, 0, q + 1)
                dve.tensor_scalar(hn[:, q, :], zc[:, q, :], fvec[:, l, 0:1], fvec[:, l, 1:2], ALU.mult, ALU.add
                                  ).then_inc(h_ready.sem, 1)
            for k in range(3 * NB):
                q, w = k // 3, HCH[k % 3][1]
                gelu.wait(dve, 0, k + 1)
                dve.scalar_tensor_tensor(out=u[0:w, q, k % 3, :], in0=psa[k % 2][0:w, :],
                                         scalar=fvec[0:w, l, 3 + k % 3:4 + k % 3], in1=gl[0:w, k % 2, :],
                                         op0=ALU.add, op1=ALU.mult).then_inc(gated.sem, 1)
                if k % 3 == 0 and q >= 2:
                    residual(q - 2)
            residual(NB - 2)
            residual(NB - 1)


def final_block(nc, ident, mod, x1T, X, out):
    with ExitStack() as ctx:
        z = ctx.enter_context(nc.sbuf_tensor("z", [P, B * L], F32))
        o = ctx.enter_context(nc.sbuf_tensor("o", [P, B * TILES, D], F32))
        ps = [ctx.enter_context(nc.psum_tensor(f"psf{q}", [P, 4, D], F32)) for q in range(4)]
        summed, turned, copied, stored = [ctx.enter_context(nc.semaphore(s)) for s in ("summed", "turned_f", "copied_f", "stored")]
        block = ctx.enter_context(nc.Block())
        out_t = out.rearrange("b (n p) d -> p (b n) d", p=P)

        @block.sync
        def _(sp):
            for q in range(4):
                sp.wait_ge(copied, q + 1)
                sp.dma_start(out_t[:, 4 * q:4 * q + 4, :], o[:, 4 * q:4 * q + 4, :]).then_inc(stored, 16)
            sp.wait_ge(stored, 64)

        @block.vector
        def _(dve):
            for q in range(4):
                b, c = q // 2, 512 * (q % 2)
                dve.scalar_tensor_tensor(out=z[:, q * 512:(q + 1) * 512], in0=X[:, b, 1 + c:513 + c], scalar=mod[:, 5, b:b + 1],
                                         in1=x1T[:, b, c:c + 512], op0=ALU.mult, op1=ALU.add).then_inc(summed, 1)

        @block.tensor
        def _(pe):
            for q in range(4):
                pe.wait_ge(summed, q + 1)
                for n in range(4):
                    mm = pe.transpose(ps[q][:, n, :], z[:, (4 * q + n) * P:(4 * q + n + 1) * P], ident[:])
                mm.then_inc(turned, 1)

        @block.scalar
        def _(act):
            for q in range(4):
                act.wait_ge(turned, q + 1)
                act.copy(o[:, 4 * q:4 * q + 4, :], ps[q][:]).then_inc(copied, 1)


_INS = ['L0_attn_x', 'L0_attn_W_dkv', 'L0_attn_W_uk', 'L0_attn_W_uv', 'L0_attn_W_dq', 'L0_attn_W_uq', 'L0_attn_W_qr',
        'L0_attn_W_kr', 'L0_attn_W_out', 'L0_attn_idx_wq', 'L0_attn_idx_wk', 'L0_attn_idx_w', 'L0_attn_raw_delta',
        'L0_ffn_wqkv', 'L0_ffn_q_scale', 'L0_ffn_k_scale', 'L0_ffn_wo', 'L0_ffn_ln_g', 'L0_ffn_ln_b', 'L0_ffn_w1',
        'L0_ffn_b1', 'L0_ffn_w2', 'L0_ffn_b2', 'L0_c', 'L0_wmod']


def kernel(**inputs):
    import concourse.bacc as _bacc
    from concourse import mybir as _mybir
    from concourse.bass_utils import run_bass_kernel_spmd as _run

    nc = _bacc.Bacc("TRN2", target_bir_lowering=False, num_devices=1)
    arrays, ins, consts = {}, {}, {}
    for name in _INS:
        a = np.ascontiguousarray(inputs[name])
        arrays[f"in_{name}"] = a
        ins[name] = nc.dram_tensor(f"in_{name}", a.shape, _mybir.dt.from_np(a.dtype), kind="ExternalInput").ap()
    for name, a in constants().items():
        a = np.ascontiguousarray(a)
        arrays[f"const_{name}"] = a
        consts[name] = nc.dram_tensor(f"const_{name}", a.shape, _mybir.dt.from_np(a.dtype), kind="ExternalInput").ap()
    out = nc.dram_tensor("out_x", (B, L, D), F32, kind="ExternalOutput").ap()
    nc.disable_value_cache = True
    kernel_program(nc, ins, consts, out)
    r = _run(nc, [arrays], core_ids=[0])
    return r.results[0]["out_x"]
```
